# Optimizing a Trainium2 kernel written in Bass

```python
import numpy as np
import jax
import jax.numpy as jnp

def _softmax(x, axis=-1):
    return jax.nn.softmax(x, axis=axis)

def _gelu(x):
    return jax.nn.gelu(x, approximate=True)

def _silu(x):
    return jax.nn.silu(x)

def _sigmoid(x):
    return jax.nn.sigmoid(x)

def _layernorm(x, axis=-1, eps=1e-05):
    m = jnp.mean(x, axis=axis, keepdims=True)
    v = jnp.var(x, axis=axis, keepdims=True)
    return (x - m) / jnp.sqrt(v + eps)

def _scatter_add(tgt, idx, src, axis=0):
    return tgt.at[idx].add(src)

def _segment_sum(src, seg, n):
    return jax.ops.segment_sum(src, seg, n)
kernel_name = 'mk_prb_d2_jaxref_r4_fbcd01'

def setup_inputs(seed: int=0):
    np.random.seed(seed)
    _w = jnp.asarray

    def _L0_attn_setup():
        import jax, jax.numpy as jnp
        import numpy as np
        HID = 512
        HEADS = 16
        HD = HID // HEADS
        EPS = 1e-06

        def _heads(x, b, s):
            return x.reshape(b, s, HEADS, HD).transpose(0, 2, 1, 3)
        key = jax.random.key(seed)
        ks = jax.random.split(key, 9)
        s = 1.0 / np.sqrt(HID)
        return {'hidden_states': jax.random.normal(ks[0], (4, 1024, HID), jnp.float32), 'q_w': jax.random.normal(ks[1], (HID, HID), jnp.float32) * s, 'q_b': jnp.zeros((HID,), jnp.float32), 'k_w': jax.random.normal(ks[2], (HID, HID), jnp.float32) * s, 'k_b': jnp.zeros((HID,), jnp.float32), 'v_w': jax.random.normal(ks[3], (HID, HID), jnp.float32) * s, 'v_b': jnp.zeros((HID,), jnp.float32), 'o_w': jax.random.normal(ks[4], (HID, HID), jnp.float32) * s, 'o_b': jnp.zeros((HID,), jnp.float32)}
    _L0_attn_in = _L0_attn_setup()

    def _L0_ffn_setup():
        import jax, jax.numpy as jnp
        import numpy as np
        B, S, EMB = (4, 512, 512)
        LAT, HID = (128, 256)
        E, K = (16, 8)
        SCALE = 2.5

        def _w(key, shape, fan_in):
            return jax.random.normal(key, shape, jnp.float32) * fan_in ** (-0.5)

        def _sqrelu(x):
            return jnp.square(jax.nn.relu(x))
        key = jax.random.key(seed)
        ks = jax.random.split(key, 11)
        return {'x': jax.random.normal(ks[0], (B, S, EMB), jnp.float32), 'sw1': _w(ks[1], (HID, EMB), EMB), 'swg': _w(ks[2], (HID, EMB), EMB), 'sw2': _w(ks[3], (EMB, HID), HID), 'rw1': _w(ks[4], (E, HID, LAT), LAT), 'rwg': _w(ks[5], (E, HID, LAT), LAT), 'rw2': _w(ks[6], (E, LAT, HID), HID), 'Wg': _w(ks[7], (E, EMB), EMB), 'Wdown': _w(ks[8], (LAT, EMB), EMB), 'Wup': _w(ks[9], (EMB, LAT), LAT), 'biases': jnp.zeros((E,), jnp.float32)}
    _L0_ffn_in = _L0_ffn_setup()

    def _L1_attn_setup():
        import jax, jax.numpy as jnp
        import numpy as np
        B, N, H = (1, 1024, 512)
        NH, HD = (16, H // 16)
        WINDOW = 1024
        EPS = 1e-06
        THETA = 10000.0
        NEG = -1e+30

        def rmsnorm(x, w):
            var = jnp.mean(jnp.square(x.astype(jnp.float32)), axis=-1, keepdims=True)
            return (x * jax.lax.rsqrt(var + EPS)).astype(w.dtype) * w

        def rotate_half(x):
            x1, x2 = (x[..., :x.shape[-1] // 2], x[..., x.shape[-1] // 2:])
            return jnp.concatenate((-x2, x1), axis=-1)
        key = jax.random.key(seed)
        k1, k2, k3 = jax.random.split(key, 3)
        x = jax.random.normal(k1, (B, N, H), dtype=jnp.float32)
        w_qkv = jax.random.normal(k2, (H, 3 * H), dtype=jnp.float32) * (1.0 / np.sqrt(H))
        w_out = jax.random.normal(k3, (H, H), dtype=jnp.float32) * (1.0 / np.sqrt(H))
        q_gamma = jnp.ones((HD,), dtype=jnp.float32)
        k_gamma = jnp.ones((HD,), dtype=jnp.float32)
        return {'x': x, 'w_qkv': w_qkv, 'w_out': w_out, 'q_gamma': q_gamma, 'k_gamma': k_gamma}
    _L1_attn_in = _L1_attn_setup()

    def _L1_ffn_setup():
        import jax, jax.numpy as jnp
        import numpy as np
        CAPACITY = 0.125
        HEAD_DIM = 128
        N_HEADS = 16
        N_KV_HEADS = 8
        ROPE_THETA = 10000.0
        EPS = 1e-06

        def _rms_norm(x, w):
            return x * jax.lax.rsqrt(jnp.mean(x * x, axis=-1, keepdims=True) + EPS) * w

        def _rotate_half(t):
            h = t.shape[-1] // 2
            return jnp.concatenate([-t[..., h:], t[..., :h]], axis=-1)
        key = jax.random.key(seed)
        ks = jax.random.split(key, 12)
        B, T, D = (4, 1024, 512)
        I = 2048
        s = 0.02
        return {'hidden_states': jax.random.normal(ks[0], (B, T, D), jnp.float32), 'w_router': jax.random.normal(ks[1], (D,), jnp.float32) * s, 'wq': jax.random.normal(ks[2], (D, N_HEADS * HEAD_DIM), jnp.float32) * s, 'bq': jnp.zeros((N_HEADS * HEAD_DIM,), jnp.float32), 'wk': jax.random.normal(ks[3], (D, N_KV_HEADS * HEAD_DIM), jnp.float32) * s, 'bk': jnp.zeros((N_KV_HEADS * HEAD_DIM,), jnp.float32), 'wv': jax.random.normal(ks[4], (D, N_KV_HEADS * HEAD_DIM), jnp.float32) * s, 'bv': jnp.zeros((N_KV_HEADS * HEAD_DIM,), jnp.float32), 'wo': jax.random.normal(ks[5], (N_HEADS * HEAD_DIM, D), jnp.float32) * s, 'w_gate': jax.random.normal(ks[6], (D, I), jnp.float32) * s, 'w_up': jax.random.normal(ks[7], (D, I), jnp.float32) * s, 'w_down': jax.random.normal(ks[8], (I, D), jnp.float32) * s, 'ln1_w': jnp.ones((D,), jnp.float32), 'ln2_w': jnp.ones((D,), jnp.float32)}
    _L1_ffn_in = _L1_ffn_setup()
    _d = {'L0_attn_hidden_states': _L0_attn_in['hidden_states'], 'L0_attn_q_w': _L0_attn_in['q_w'], 'L0_attn_q_b': _L0_attn_in['q_b'], 'L0_attn_k_w': _L0_attn_in['k_w'], 'L0_attn_k_b': _L0_attn_in['k_b'], 'L0_attn_v_w': _L0_attn_in['v_w'], 'L0_attn_v_b': _L0_attn_in['v_b'], 'L0_attn_o_w': _L0_attn_in['o_w'], 'L0_attn_o_b': _L0_attn_in['o_b'], 'L0_ffn_sw1': _L0_ffn_in['sw1'], 'L0_ffn_swg': _L0_ffn_in['swg'], 'L0_ffn_sw2': _L0_ffn_in['sw2'], 'L0_ffn_rw1': _L0_ffn_in['rw1'], 'L0_ffn_rwg': _L0_ffn_in['rwg'], 'L0_ffn_rw2': _L0_ffn_in['rw2'], 'L0_ffn_Wg': _L0_ffn_in['Wg'], 'L0_ffn_Wdown': _L0_ffn_in['Wdown'], 'L0_ffn_Wup': _L0_ffn_in['Wup'], 'L0_ffn_biases': _L0_ffn_in['biases'], 'L1_attn_w_qkv': _L1_attn_in['w_qkv'], 'L1_attn_w_out': _L1_attn_in['w_out'], 'L1_attn_q_gamma': _L1_attn_in['q_gamma'], 'L1_attn_k_gamma': _L1_attn_in['k_gamma'], 'L1_ffn_w_router': _L1_ffn_in['w_router'], 'L1_ffn_wq': _L1_ffn_in['wq'], 'L1_ffn_bq': _L1_ffn_in['bq'], 'L1_ffn_wk': _L1_ffn_in['wk'], 'L1_ffn_bk': _L1_ffn_in['bk'], 'L1_ffn_wv': _L1_ffn_in['wv'], 'L1_ffn_bv': _L1_ffn_in['bv'], 'L1_ffn_wo': _L1_ffn_in['wo'], 'L1_ffn_w_gate': _L1_ffn_in['w_gate'], 'L1_ffn_w_up': _L1_ffn_in['w_up'], 'L1_ffn_w_down': _L1_ffn_in['w_down'], 'L1_ffn_ln1_w': _L1_ffn_in['ln1_w'], 'L1_ffn_ln2_w': _L1_ffn_in['ln2_w']}
    _x0 = _d['L0_attn_hidden_states']
    _d['L0_attn_hidden_states'] = jax.random.normal(jax.random.fold_in(jax.random.key(seed), 1), (1, 2048, 512), dtype=_x0.dtype)
    del _x0
    return _d

def reference(L0_attn_hidden_states, L0_attn_q_w, L0_attn_q_b, L0_attn_k_w, L0_attn_k_b, L0_attn_v_w, L0_attn_v_b, L0_attn_o_w, L0_attn_o_b, L0_ffn_sw1, L0_ffn_swg, L0_ffn_sw2, L0_ffn_rw1, L0_ffn_rwg, L0_ffn_rw2, L0_ffn_Wg, L0_ffn_Wdown, L0_ffn_Wup, L0_ffn_biases, L1_attn_w_qkv, L1_attn_w_out, L1_attn_q_gamma, L1_attn_k_gamma, L1_ffn_w_router, L1_ffn_wq, L1_ffn_bq, L1_ffn_wk, L1_ffn_bk, L1_ffn_wv, L1_ffn_bv, L1_ffn_wo, L1_ffn_w_gate, L1_ffn_w_up, L1_ffn_w_down, L1_ffn_ln1_w, L1_ffn_ln2_w):

    def _L0_attn_ref(hidden_states, q_w, q_b, k_w, k_b, v_w, v_b, o_w, o_b):
        import jax, jax.numpy as jnp
        import numpy as np
        HID = 512
        HEADS = 16
        HD = HID // HEADS
        EPS = 1e-06

        def _heads(x, b, s):
            return x.reshape(b, s, HEADS, HD).transpose(0, 2, 1, 3)
        b, s, _ = hidden_states.shape
        q = _heads(hidden_states @ q_w.T + q_b, b, s)
        k = _heads(hidden_states @ k_w.T + k_b, b, s)
        v = _heads(hidden_states @ v_w.T + v_b, b, s)
        qp = jax.nn.elu(q) + 1.0
        kp = jax.nn.elu(k) + 1.0
        kv = jnp.einsum('bhsd,bhse->bhde', kp, v)
        z = jnp.einsum('bhsd,bhd->bhs', qp, kp.sum(axis=2))[..., None]
        attn = jnp.einsum('bhsd,bhde->bhse', qp, kv) / (z + EPS)
        out = attn.transpose(0, 2, 1, 3).reshape(b, s, HID)
        return out @ o_w.T + o_b

    def _L0_ffn_ref(x, sw1, swg, sw2, rw1, rwg, rw2, Wg, Wdown, Wup, biases):
        import jax, jax.numpy as jnp
        import numpy as np
        B, S, EMB = (4, 512, 512)
        LAT, HID = (128, 256)
        E, K = (16, 8)
        SCALE = 2.5

        def _w(key, shape, fan_in):
            return jax.random.normal(key, shape, jnp.float32) * fan_in ** (-0.5)

        def _sqrelu(x):
            return jnp.square(jax.nn.relu(x))
        b, s, d = x.shape
        x2 = x.reshape(-1, d)
        shared = x2 @ sw1.T * _sqrelu(x2 @ swg.T) @ sw2.T
        xl = x2 @ Wdown.T
        probas = jax.nn.sigmoid(x2 @ Wg.T)
        _, idx = jax.lax.top_k(probas + biases, K)
        p = jnp.take_along_axis(probas, idx, axis=-1)
        p = p / p.sum(-1, keepdims=True) * SCALE
        T = x2.shape[0]
        w_dense = jnp.zeros((T, E), x2.dtype).at[jnp.arange(T)[:, None], idx].add(p)
        acc = jnp.zeros_like(xl)
        for e in range(E):
            ye = xl @ rw1[e].T * _sqrelu(xl @ rwg[e].T) @ rw2[e].T
            acc = acc + w_dense[:, e:e + 1] * ye
        out = shared + acc @ Wup.T
        return out.reshape(b, s, d)

    def _L1_attn_ref(x, w_qkv, w_out, q_gamma, k_gamma):
        import jax, jax.numpy as jnp
        import numpy as np
        B, N, H = (1, 1024, 512)
        NH, HD = (16, H // 16)
        WINDOW = 1024
        EPS = 1e-06
        THETA = 10000.0
        NEG = -1e+30

        def rmsnorm(x, w):
            var = jnp.mean(jnp.square(x.astype(jnp.float32)), axis=-1, keepdims=True)
            return (x * jax.lax.rsqrt(var + EPS)).astype(w.dtype) * w

        def rotate_half(x):
            x1, x2 = (x[..., :x.shape[-1] // 2], x[..., x.shape[-1] // 2:])
            return jnp.concatenate((-x2, x1), axis=-1)
        b, n, _ = x.shape
        qkv = jnp.einsum('bnh,hm->bnm', x, w_qkv)
        q, k, v = jnp.split(qkv, 3, axis=-1)
        q = q.reshape(b, n, NH, HD).transpose(0, 2, 1, 3)
        k = k.reshape(b, n, NH, HD).transpose(0, 2, 1, 3)
        v = v.reshape(b, n, NH, HD).transpose(0, 2, 1, 3)
        q = rmsnorm(q, q_gamma)
        k = rmsnorm(k, k_gamma)
        inv_freq = 1.0 / THETA ** (jnp.arange(0, HD, 2, dtype=jnp.float32) / HD)
        t = jnp.arange(n, dtype=jnp.float32)
        freqs = t[:, None] * inv_freq[None, :]
        emb = jnp.concatenate((freqs, freqs), axis=-1)
        cos = jnp.cos(emb)[None, None, :, :]
        sin = jnp.sin(emb)[None, None, :, :]
        q = q * cos + rotate_half(q) * sin
        k = k * cos + rotate_half(k) * sin
        kv_len = k.shape[-2]
        q_idx = jnp.arange(n)[:, None] + (kv_len - n)
        k_idx = jnp.arange(kv_len)[None, :]
        mask = (q_idx >= k_idx) & (q_idx - k_idx <= WINDOW)
        scores = jnp.einsum('bhqd,bhkd->bhqk', q, k) / np.sqrt(HD)
        scores = jnp.where(mask[None, None, :, :], scores, NEG)
        attn = jax.nn.softmax(scores, axis=-1)
        out = jnp.einsum('bhqk,bhkd->bhqd', attn, v)
        out = out.transpose(0, 2, 1, 3).reshape(b, n, H)
        return jnp.einsum('bnh,hm->bnm', out, w_out)

    def _L1_ffn_ref(hidden_states, w_router, wq, bq, wk, bk, wv, bv, wo, w_gate, w_up, w_down, ln1_w, ln2_w):
        import jax, jax.numpy as jnp
        import numpy as np
        CAPACITY = 0.125
        HEAD_DIM = 128
        N_HEADS = 16
        N_KV_HEADS = 8
        ROPE_THETA = 10000.0
        EPS = 1e-06

        def _rms_norm(x, w):
            return x * jax.lax.rsqrt(jnp.mean(x * x, axis=-1, keepdims=True) + EPS) * w

        def _rotate_half(t):
            h = t.shape[-1] // 2
            return jnp.concatenate([-t[..., h:], t[..., :h]], axis=-1)
        B, T, D = hidden_states.shape
        k = max(1, int(T * CAPACITY))
        scores = jnp.einsum('btd,d->bt', hidden_states, w_router)
        _, idx = jax.lax.top_k(scores, k)
        idx = jnp.sort(idx, axis=-1)
        b = jnp.arange(B)[:, None]
        sel = hidden_states[b, idx]
        sel_scores = scores[b, idx]
        S = B * k
        x = sel.reshape(S, D)
        pos = idx.reshape(S)
        inv_freq = 1.0 / ROPE_THETA ** (jnp.arange(0, HEAD_DIM, 2, dtype=jnp.float32) / HEAD_DIM)
        ang = pos.astype(jnp.float32)[:, None] * inv_freq
        cos = jnp.concatenate([jnp.cos(ang), jnp.cos(ang)], axis=-1)[:, None, :]
        sin = jnp.concatenate([jnp.sin(ang), jnp.sin(ang)], axis=-1)[:, None, :]
        h = _rms_norm(x, ln1_w)
        q = (h @ wq + bq).reshape(S, N_HEADS, HEAD_DIM)
        kk = (h @ wk + bk).reshape(S, N_KV_HEADS, HEAD_DIM)
        v = (h @ wv + bv).reshape(S, N_KV_HEADS, HEAD_DIM)
        q = q * cos + _rotate_half(q) * sin
        kk = kk * cos + _rotate_half(kk) * sin
        rep = N_HEADS // N_KV_HEADS
        kk = jnp.repeat(kk, rep, axis=1)
        v = jnp.repeat(v, rep, axis=1)
        att = jnp.einsum('shd,thd->hst', q, kk) / np.sqrt(HEAD_DIM)
        causal = jnp.tril(jnp.ones((S, S), bool))
        att = jnp.where(causal[None], att, jnp.finfo(att.dtype).min)
        att = jax.nn.softmax(att, axis=-1)
        attn_out = jnp.einsum('hst,thd->shd', att, v).reshape(S, N_HEADS * HEAD_DIM) @ wo
        x1 = x + attn_out
        h2 = _rms_norm(x1, ln2_w)
        mlp = jax.nn.silu(h2 @ w_gate) * (h2 @ w_up) @ w_down
        processed = x1 + mlp
        gate = jax.nn.sigmoid(sel_scores).reshape(S, 1)
        gated = gate * processed + (1.0 - gate) * x
        output = hidden_states.at[b, idx].set(gated.reshape(B, k, D))
        return output
    x = L0_attn_hidden_states
    xn = _layernorm(x, axis=-1)
    x = x + _L0_attn_ref(xn, L0_attn_q_w, L0_attn_q_b, L0_attn_k_w, L0_attn_k_b, L0_attn_v_w, L0_attn_v_b, L0_attn_o_w, L0_attn_o_b) + _L0_ffn_ref(xn, L0_ffn_sw1, L0_ffn_swg, L0_ffn_sw2, L0_ffn_rw1, L0_ffn_rwg, L0_ffn_rw2, L0_ffn_Wg, L0_ffn_Wdown, L0_ffn_Wup, L0_ffn_biases)
    xn = _layernorm(x, axis=-1)
    x = x + _L1_attn_ref(xn, L1_attn_w_qkv, L1_attn_w_out, L1_attn_q_gamma, L1_attn_k_gamma) + _L1_ffn_ref(xn, L1_ffn_w_router, L1_ffn_wq, L1_ffn_bq, L1_ffn_wk, L1_ffn_bk, L1_ffn_wv, L1_ffn_bv, L1_ffn_wo, L1_ffn_w_gate, L1_ffn_w_up, L1_ffn_w_down, L1_ffn_ln1_w, L1_ffn_ln2_w)
    return x

_drawn_inputs = setup_inputs


def setup_inputs(seed=0):
    import zlib

    import numpy as np

    out = dict(_drawn_inputs(seed))
    spreads = {'L0_attn_q_b': (0.0, 0.8),
     'L0_attn_k_b': (0.0, 0.8),
     'L0_attn_v_b': (0.0, 0.1),
     'L0_attn_o_b': (0.0, 0.1),
     'L0_ffn_biases': (0.0, 0.1),
     'L1_attn_q_gamma': (1.0, 0.6),
     'L1_attn_k_gamma': (1.0, 0.6),
     'L1_ffn_bq': (0.0, 0.8),
     'L1_ffn_bk': (0.0, 0.8),
     'L1_ffn_bv': (0.0, 0.8),
     'L1_ffn_ln1_w': (1.0, 0.6),
     'L1_ffn_ln2_w': (1.0, 0.6)}
    factors = {'L0_attn_q_w': 8.0,
     'L0_attn_k_w': 8.0,
     'L0_attn_v_w': 4.934,
     'L1_ffn_w_router': 4.399,
     'L1_ffn_wq': 8.0,
     'L1_ffn_wk': 8.0,
     'L1_ffn_wv': 7.438,
     'L1_ffn_wo': 5.324,
     'L1_ffn_w_gate': 6.52,
     'L1_ffn_w_up': 6.378,
     'L1_ffn_w_down': 6.425,
     'L1_attn_w_qkv': 7.789,
     'L1_attn_w_out': 7.681}
    for name, (base, spread) in spreads.items():
        noise = np.random.default_rng([zlib.crc32(name.encode()), seed]).standard_normal(out[name].shape)
        drawn = base * np.exp(spread * noise) if base else spread * noise
        out[name] = jnp.asarray(drawn.astype(out[name].dtype))
    for name, factor in factors.items():
        out[name] = (out[name] * factor).astype(out[name].dtype)
    return out
```

```python
from contextlib import ExitStack

import numpy as np

import concourse.bass as bass
from concourse import mybir

P = 128
F32 = mybir.dt.float32
F32R = mybir.dt.float32r
BF16 = mybir.dt.bfloat16
U32 = mybir.dt.uint32
I32 = mybir.dt.int32
ALU = mybir.AluOpType
ACT = mybir.ActivationFunctionType
AX = mybir.AxisListType.X

T = 2048
D = 512
NT = T // P
NC = D // P
TB = 512
NB = T // TB
BT = TB // P
BANK = 512
LN_EPS = 1e-5
RMS_EPS = 1e-6
NEG = -1e30

H0, HD = 16, 32
EXPERTS, TOPK, LAT, HID = 16, 8, 128, 256
ROUTE_SCALE = 2.5
WINDOW = 1024

SEL = T // 8
NS = SEL // P
NHQ, NHK, HDF = 16, 8, 128
INTER = 2048


def raw(ap):
    return ap.bitcast(F32)


class Chain:

    def __init__(self, eng, sem):
        self.eng, self.sem, self.n = eng, sem, 0

    def done(self, ins):
        self.n += 1
        ins.then_inc(self.sem, 1)
        self.eng.wait_ge(self.sem, self.n)


def mm3(pe, out, parts, start=True, stop=True, **kw):
    last = None
    for n, ((ah, al), (bh, bl)) in enumerate(parts):
        end = n == len(parts) - 1
        pe.matmul(out, ah, bh, start=start and n == 0, stop=False, **kw)
        pe.matmul(out, ah, bl, start=False, stop=False, **kw)
        last = pe.matmul(out, al, bh, start=False, stop=stop and end, **kw)
    return last


def mm32(pe, out, parts, start=True, stop=True, **kw):
    last = None
    for n, (a, b) in enumerate(parts):
        last = pe.matmul(out, a, b, start=start and n == 0, stop=stop and n == len(parts) - 1, **kw)
    return last


class Memory:

    def __init__(self, nc, stack, tag=""):
        self.nc, self.stack, self.tag = nc, stack, tag

    def sb(self, name, shape, dt=F32):
        return self.stack.enter_context(self.nc.sbuf_tensor(self.tag + name, shape, dt))


class Shared:
    pass


def stage_constants(nc, G):
    zeroed, made, blocks = G.sem("const_zeroed"), G.sem("const_made"), G.sem("const_blocks")
    with nc.sbuf_tensor("headsel32", [P, NC, P], F32) as headsel, nc.Block() as block:

        @block.gpsimd
        def _(pool):
            pool.memset(G.ident[:, :], 0.0)
            pool.memset(headsel[:, :, :], 0.0)
            pool.memset(G.upper[:, :], 0.0)
            pool.memset(G.strict[:, :], 1.0)
            pool.memset(G.lower[:, :], 0.0).then_inc(zeroed, 1)
            pool.wait_ge(zeroed, 1)
            pool.affine_select(out=G.ident[:, :], in_=G.ident[:, :], compare_op=ALU.not_equal, fill=1.0,
                               base=0, pattern=[[-1, P]], channel_multiplier=1).then_inc(made, 1)
            pool.affine_select(out=G.upper[:, :], in_=G.upper[:, :], compare_op=ALU.is_ge, fill=NEG,
                               base=0, pattern=[[1, P]], channel_multiplier=-1).then_inc(made, 1)
            pool.affine_select(out=G.lower[:, :], in_=G.lower[:, :], compare_op=ALU.is_ge, fill=NEG,
                               base=0, pattern=[[-1, P]], channel_multiplier=1).then_inc(made, 1)
            hs = headsel[:, :, :].rearrange("p g (j d) -> p g j d", d=HD)
            pool.affine_select(out=hs, in_=hs, compare_op=ALU.not_equal, fill=1.0, base=0,
                               pattern=[[P // HD, NC], [1, P // HD], [0, HD]], channel_multiplier=-1).then_inc(made, 1)
            pool.affine_select(out=G.strict[:, :], in_=G.strict[:, :], compare_op=ALU.is_gt, fill=0.0,
                               base=0, pattern=[[1, P]], channel_multiplier=-1).then_inc(made, 1)

        @block.vector
        def _(dve):
            dve.memset(G.headmask[:, :], 0.0).then_inc(blocks, 1)
            dve.memset(G.ones[:, :], 1.0)
            dve.memset(G.ksb[:, :, :], 0.0)
            dve.wait_ge(blocks, 1)
            for j in range(P // HD):
                dve.memset(G.headmask[j * HD:(j + 1) * HD, j * HD:(j + 1) * HD], 1.0)
            dve.wait_ge(made, 5)
            dve.tensor_copy(G.headsel[:, :, :], headsel[:, :, :])
            dve.tensor_copy(G.identb[:, :], G.ident[:, :])
            dve.tensor_copy(G.identr[:, :], G.ident[:, :]).then_inc(blocks, 1)
            dve.wait_ge(blocks, 2)


def stage_normalize(nc, G, tag, x_dram, xn_dram, r_dram, router=None, score_dram=None):
    wr_in, wrh_done, wr_done, sc_mm, sc_sb, st_mm, st_sb = (G.sem(tag + n) for n in (
        "wr_in", "wrh", "wr", "sc_mm", "sc_sb", "st_mm", "st_sb"))
    x_in = [G.sem(f"{tag}x_in{g}") for g in range(NB)]
    var_ready, sd_ready = G.sem(tag + "var_ready"), G.sem(tag + "sd_ready")
    xn_ready, xt_ready = G.sem(tag + "xn_ready"), G.sem(tag + "xt_ready")
    hi_ready, lo_ready, link = G.sem(tag + "hi_ready"), G.sem(tag + "lo_ready"), G.sem(tag + "ln_link")
    RING = 4
    res_ready, r_stored = G.sem(tag + "res_ready"), G.sem(tag + "r_stored")
    xn_stored = [G.sem(f"{tag}xn_stored{n}") for n in range(RING)]
    X, xTh, xTl = G.X, G.xTh, G.xTl
    with ExitStack() as stack:
        M = Memory(nc, stack, tag)
        stats, mv = M.sb("stats", [P, NT, 6]), M.sb("mv", [P, NT, 2])
        ve, sd, rstd = M.sb("ve", [P, NT]), M.sb("sd", [P, NT]), M.sb("rstd", [P, NT])
        xn = M.sb("xn", [P, RING, D])
        wr, wrh, wrl = M.sb("wr", [P, NC]), M.sb("wrh", [P, NC, 2], F32R), M.sb("wrl", [P, NC, 2], F32R)
        sT = M.sb("sT", [NT, P])
        block = stack.enter_context(nc.Block())

        @block.sync
        def _(sp):
            if x_dram is not None:
                for g in range(NB):
                    sp.dma_start(X[:, g * BT:(g + 1) * BT, :],
                                 x_dram.rearrange("(t p) d -> p t d", p=P)[:, g * BT:(g + 1) * BT, :]
                                 ).then_inc(x_in[g], 16)
            if xn_dram is not None:
                sp.dma_start(wr[:, :], router).then_inc(wr_in, 16)
                for t in range(NT):
                    sp.wait_ge(xn_ready, t + 1)
                    sp.dma_start(xn_dram[t * P:(t + 1) * P, :], xn[:, t % RING, :]).then_inc(xn_stored[t % RING], 16)
                    sp.wait_ge(res_ready, t + 1)
                    sp.dma_start(r_dram[t * P:(t + 1) * P, :], X[:, t, :]).then_inc(r_stored, 16)
                sp.wait_ge(st_sb, 1)
                sp.dma_start(score_dram.rearrange("(t p) -> t p", p=P), sT[:, :]).then_inc(r_stored, 16)
                sp.wait_ge(r_stored, (NT + 1) * 16)
                for n in range(RING):
                    sp.wait_ge(xn_stored[n], 16 * NT // RING)

        @block.vector
        def _(dve):
            chain = Chain(dve, link)
            if xn_dram is not None:
                dve.wait_ge(wr_in, 16)
                for n in range(2):
                    last = dve.tensor_copy(wrh[:, :, n:n + 1], wr[:, :].unsqueeze(2))
                last.then_inc(wrh_done, 1)
                dve.wait_ge(wrh_done, 1)
                for n in range(2):
                    last = dve.tensor_tensor(wrl[:, :, n:n + 1], wr[:, :].unsqueeze(2), raw(wrh[:, :, n:n + 1]),
                                             ALU.subtract)
                last.then_inc(wr_done, 1)
            for g in range(NB):
                tiles = range(g * BT, (g + 1) * BT)
                if x_dram is not None:
                    dve.wait_ge(x_in[g], 16)
                for t in tiles:
                    last = dve.bn_stats(stats[:, t, :], X[:, t, :])
                chain.done(last)
                for t in tiles:
                    last = dve.bn_aggr(mv[:, t, :], stats[:, t, :])
                chain.done(last)
                dve.tensor_scalar_add(ve[:, g * BT:(g + 1) * BT], mv[:, g * BT:(g + 1) * BT, 1],
                                      LN_EPS).then_inc(var_ready, 1)
                dve.wait_ge(sd_ready, g + 1)
                chain.done(dve.reciprocal(rstd[:, g * BT:(g + 1) * BT], sd[:, g * BT:(g + 1) * BT]))
                for t in tiles:
                    if t >= RING:
                        dve.wait_ge(xt_ready, t - RING + 1)
                        if xn_dram is not None:
                            dve.wait_ge(xn_stored[t % RING], 16 * (t // RING))
                            dve.wait_ge(res_ready, t - RING + 1)
                    dve.tensor_scalar(xn[:, t % RING, :], X[:, t, :], mv[:, t, 0:1], rstd[:, t:t + 1],
                                      ALU.subtract, ALU.mult).then_inc(xn_ready, 1)
                for t in tiles:
                    dve.wait_ge(hi_ready, t + 1)
                    cols = slice(t * P, (t + 1) * P)
                    dve.tensor_tensor(xTl[:, :, cols], G.ps[t % RING][:, :].rearrange("p (c n) -> p c n", c=NC),
                                      raw(xTh[:, :, cols]), ALU.subtract).then_inc(lo_ready, 1)
            if xn_dram is not None:
                dve.wait_ge(sc_mm, 1)
                dve.tensor_copy(G.pair[:, :, 1], G.ps[RING][:, 0:2 * NT].rearrange("p (t n) -> p t n", n=2)[:, :, 0]
                                ).then_inc(sc_sb, 1)

        if xn_dram is not None:
            @block.gpsimd
            def _(pool):
                for t in range(NT):
                    pool.wait_ge(xn_ready, t + 1)
                    pool.tensor_tensor(X[:, t, :], X[:, t, :], xn[:, t % RING, :], ALU.add).then_inc(res_ready, 1)

        @block.tensor
        def _(pe):
            for t in range(NT):
                pe.wait_ge(xn_ready, t + 1)
                if t >= RING:
                    pe.wait_ge(lo_ready, t - RING + 1)
                for c in range(NC):
                    last = pe.transpose(G.ps[t % RING][:, c * P:(c + 1) * P],
                                        xn[:, t % RING, c * P:(c + 1) * P], G.ident[:, :])
                last.then_inc(xt_ready, 1)
            if xn_dram is not None:
                pe.wait_ge(wr_done, 1)
                for t in range(NT):
                    pe.wait_ge(lo_ready, t + 1)
                    cols = slice(t * P, (t + 1) * P)
                    last = mm3(pe, G.ps[RING][:, 2 * t:2 * t + 2], [((xTh[:, c, cols], xTl[:, c, cols]),
                                                                    (wrh[:, c, :], wrl[:, c, :])) for c in range(NC)])
                last.then_inc(sc_mm, 1)
                pe.wait_ge(sc_sb, 1)
                pe.transpose(G.ps[RING + 1][0:NT, 0:P], G.pair[:, :, 1], G.ident[:, :]).then_inc(st_mm, 1)

        @block.scalar
        def _(act):
            for g in range(NB):
                act.wait_ge(var_ready, g + 1)
                act.activation(sd[:, g * BT:(g + 1) * BT], ve[:, g * BT:(g + 1) * BT], ACT.Sqrt).then_inc(sd_ready, 1)
                for t in range(g * BT, (g + 1) * BT):
                    act.wait_ge(xt_ready, t + 1)
                    act.activation(xTh[:, :, t * P:(t + 1) * P],
                                   G.ps[t % RING][:, :].rearrange("p (c n) -> p c n", c=NC),
                                   ACT.Copy).then_inc(hi_ready, 1)
            if xn_dram is not None:
                act.wait_ge(st_mm, 1)
                act.activation(sT[:, :], G.ps[RING + 1][0:NT, 0:P], ACT.Copy).then_inc(st_sb, 1)


def split_weights(nc, G, tag, jobs, stage_cols):
    w_in = [G.sem(f"{tag}w_in{n}") for n in range(2)]
    w_hi, w_lo = G.sem(tag + "w_hi"), G.sem(tag + "w_lo")
    with ExitStack() as stack:
        stage = Memory(nc, stack, tag).sb("stage", [P, 2, stage_cols])
        block = stack.enter_context(nc.Block())

        def at(n):
            return stage[:, n % 2, 0:jobs[n][0].shape[1]]

        @block.sync
        def _(sp):
            for n, (hi, lo, src) in enumerate(jobs):
                if n >= 2:
                    sp.wait_ge(w_lo, n - 1)
                dst = at(n)
                if len(src.shape) == 3:
                    dst = dst.rearrange("p (c n) -> p c n", c=src.shape[1])
                sp.dma_start(dst, src).then_inc(w_in[n % 2], 16)

        @block.scalar
        def _(act):
            for n, (hi, lo, src) in enumerate(jobs):
                act.wait_ge(w_in[n % 2], 16 * (n // 2 + 1))
                act.activation(hi, at(n), ACT.Copy).then_inc(w_hi, 1)

        @block.vector
        def _(dve):
            for n, (hi, lo, src) in enumerate(jobs):
                dve.wait_ge(w_hi, n + 1)
                dve.tensor_tensor(lo, at(n), raw(hi), ALU.subtract).then_inc(w_lo, 1)


def stage_kv(nc, G, I, S):
    logit_ready, p1 = G.sem("kv_logit"), G.sem("kv_exp")
    k_mm, v_mm, kx_ready, e_ready, r_ready = (G.sem("kv_" + n) for n in ("k_mm", "v_mm", "kx", "e", "r"))
    kp_ready, v_ready, kv_done, link = (G.sem("kv_" + n) for n in ("kp", "v", "done", "link"))
    bias_in, gate_done, wt_mm, wt_sb, wt_out, sums = (G.sem("kv_" + n) for n in
                                                   ("bias", "gate", "wtmm", "wtsb", "wtout", "sums"))
    n_ready = G.sem("kv_n")
    pss, xTh, xTl = G.ps, G.xTh, G.xTl
    with ExitStack() as stack:
        M = Memory(nc, stack, "kv_")
        kbb, vbb, gb = M.sb("kbb", [P, D]), M.sb("vbb", [P, D]), M.sb("gb", [P, EXPERTS])
        kx, ke, kr = M.sb("kx", [P, 2, D]), M.sb("ke", [P, 2, D]), M.sb("kr", [P, 2, D])
        kp, vv = M.sb("kp", [P, 2, D]), M.sb("vv", [P, 2, D])
        gz, gp = M.sb("gz", [P, NT, EXPERTS]), M.sb("gp", [P, NT, EXPERTS])
        gbias, grep = M.sb("gbias", [P, NT, EXPERTS]), M.sb("grep", [P, NT, EXPERTS])
        top = M.sb("top", [P, NT, 8])
        gw, gsum, ginv = M.sb("gw", [P, NT, EXPERTS]), M.sb("gsum", [P, NT]), M.sb("ginv", [P, NT])
        wT = M.sb("wT", [EXPERTS, T])
        wts = {}
        for n, cols in (("k", NC * D), ("v", NC * D), ("g", NC * EXPERTS)):
            wts[n] = (M.sb(n + "h", [P, cols], F32R), M.sb(n + "l", [P, cols], F32R))
        split_weights(nc, G, "kvw_", [
            (wts["g"][0][:, :], wts["g"][1][:, :], I["wgT"].rearrange("(c p) n -> p c n", p=P)),
            (wts["k"][0][:, :], wts["k"][1][:, :], I["kT"].rearrange("(c p) n -> p c n", p=P)),
            (wts["v"][0][:, :], wts["v"][1][:, :], I["vT"].rearrange("(c p) n -> p c n", p=P)),
        ], NC * D)

        def w(n, c):
            h, l = wts[n]
            k = h.shape[1] // NC
            return h[:, c * k:(c + 1) * k], l[:, c * k:(c + 1) * k]

        def x(t, c):
            cols = slice(t * P, (t + 1) * P)
            return xTh[:, c, cols], xTl[:, c, cols]

        block = stack.enter_context(nc.Block())

        @block.sync
        def _(sp):
            sp.dma_start(kbb[:, :], I["k_b"].partition_broadcast(P)).then_inc(bias_in, 16)
            sp.dma_start(vbb[:, :], I["v_b"].partition_broadcast(P)).then_inc(bias_in, 16)
            sp.dma_start(gb[:, :], I["biases"].partition_broadcast(P)).then_inc(bias_in, 16)
            sp.wait_ge(wt_sb, 4)
            sp.dma_start(S.wscr, wT[:, :]).then_inc(wt_out, 16)
            sp.wait_ge(wt_out, 16)

        @block.tensor
        def _(pe):
            for t in range(NT):
                last = mm3(pe, pss[6][:, t * EXPERTS:(t + 1) * EXPERTS],
                           [(x(t, c), w("g", c)) for c in range(NC)])
            last.then_inc(logit_ready, 1)

            def sums_of(t):
                pe.wait_ge(kp_ready, t + 1)
                pe.wait_ge(v_ready, t + 1)
                for g in range(NC):
                    first = t == 0 and g == 0
                    pe.matmul(pss[4][:, g * P:(g + 1) * P], kp[:, t % 2, g * P:(g + 1) * P],
                              vv[:, t % 2, g * P:(g + 1) * P], start=first, stop=t == NT - 1,
                              skip_group_check=True)
                    last = pe.matmul(pss[5][:, 2 * g:2 * g + 2], kp[:, t % 2, g * P:(g + 1) * P],
                                     G.ones[:, 0:2], start=first, stop=t == NT - 1, skip_group_check=True)
                last.then_inc(kv_done, 1)

            for t in range(NT):
                if t >= 2:
                    pe.wait_ge(kx_ready, t - 1)
                mm3(pe, pss[t % 2][:, :], [(x(t, c), w("k", c)) for c in range(NC)]).then_inc(k_mm, 1)
                if t >= 2:
                    pe.wait_ge(v_ready, t - 1)
                mm3(pe, pss[2 + t % 2][:, :], [(x(t, c), w("v", c)) for c in range(NC)]).then_inc(v_mm, 1)
                if t >= 1:
                    sums_of(t - 1)
            sums_of(NT - 1)
            pe.wait_ge(gate_done, 1)
            pe.wait_ge(kx_ready, NT)
            pe.wait_ge(v_ready, NT)
            for t in range(NT):
                last = pe.transpose(pss[t // BT][0:EXPERTS, (t % BT) * P:(t % BT + 1) * P], gw[:, t, :],
                                    G.ident[:, :])
                if t % BT == BT - 1:
                    last.then_inc(wt_mm, 1)

        @block.scalar
        def _(act):
            act.wait_ge(logit_ready, 1)
            act.activation(gz[:, :, :], pss[6][:, 0:NT * EXPERTS].rearrange("p (t e) -> p t e", t=NT), ACT.Exp,
                           scale=-1.0).then_inc(p1, 1)
            for t in range(NT):
                act.wait_ge(kx_ready, t + 1)
                if t >= 2:
                    act.wait_ge(kp_ready, t - 1)
                act.activation(ke[:, t % 2, :], kx[:, t % 2, :], ACT.Relu, scale=-1.0).then_inc(n_ready, 1)
                act.wait_ge(n_ready, t + 1)
                act.activation(ke[:, t % 2, :], ke[:, t % 2, :], ACT.Exp, scale=-1.0).then_inc(e_ready, 1)
                act.activation(kr[:, t % 2, :], kx[:, t % 2, :], ACT.Relu).then_inc(r_ready, 1)
            for g in range(NB):
                act.wait_ge(wt_mm, g + 1)
                act.activation(wT[:, g * TB:(g + 1) * TB], pss[g][0:EXPERTS, :], ACT.Copy).then_inc(wt_sb, 1)

        @block.vector
        def _(dve):
            chain = Chain(dve, link)
            dve.wait_ge(bias_in, 48)

            def gates():
                dve.wait_ge(p1, 1)
                chain.done(dve.tensor_scalar_add(gz[:, :, :], gz[:, :, :], 1.0))
                chain.done(dve.reciprocal(gp[:, :, :], gz[:, :, :]))
                chain.done(dve.tensor_tensor(gbias[:, :, :], gp[:, :, :],
                                             gb[:, :].unsqueeze(1).to_broadcast([P, NT, EXPERTS]), ALU.add))
                for t in range(NT):
                    last = dve.max(top[:, t, :], gbias[:, t, :])
                chain.done(last)
                for t in range(NT):
                    last = dve.match_replace(grep[:, t, :], top[:, t, :], gbias[:, t, :], NEG)
                chain.done(last)
                chain.done(dve.tensor_tensor(grep[:, :, :], grep[:, :, :], gbias[:, :, :], ALU.not_equal))
                chain.done(dve.tensor_tensor(gw[:, :, :], gp[:, :, :], grep[:, :, :], ALU.mult))
                chain.done(dve.reduce_sum(gsum[:, :], gw[:, :, :], axis=AX))
                chain.done(dve.reciprocal(ginv[:, :], gsum[:, :]))
                chain.done(dve.tensor_scalar(ginv[:, :], ginv[:, :], ROUTE_SCALE, None, ALU.mult))
                dve.tensor_tensor(gw[:, :, :], gw[:, :, :], ginv[:, :].unsqueeze(2).to_broadcast([P, NT, EXPERTS]),
                                  ALU.mult).then_inc(gate_done, 1)

            for t in range(NT):
                dve.wait_ge(k_mm, t + 1)
                if t >= 2:
                    dve.wait_ge(r_ready, t - 1)
                dve.tensor_tensor(kx[:, t % 2, :], pss[t % 2][:, :], kbb[:, :], ALU.add).then_inc(kx_ready, 1)
                dve.wait_ge(v_mm, t + 1)
                if t >= 2:
                    dve.wait_ge(kv_done, t - 1)
                dve.tensor_tensor(vv[:, t % 2, :], pss[2 + t % 2][:, :], vbb[:, :], ALU.add).then_inc(v_ready, 1)
                dve.wait_ge(e_ready, t + 1)
                dve.wait_ge(r_ready, t + 1)
                dve.tensor_tensor(kp[:, t % 2, :], ke[:, t % 2, :], kr[:, t % 2, :], ALU.add).then_inc(kp_ready, 1)
                if t == 2:
                    gates()
            dve.wait_ge(kv_done, NT)
            for g in range(NC):
                dve.tensor_tensor(G.kvb[:, g, :], pss[4][:, g * P:(g + 1) * P], G.headmask[:, :], ALU.mult)
            for g in range(NC):
                for j in range(P // HD):
                    rows = slice(j * HD, (j + 1) * HD)
                    h = g * (P // HD) + j
                    last = dve.tensor_copy(G.ksb[rows, g, h:h + 1], pss[5][rows, 2 * g:2 * g + 1])
            last.then_inc(sums, 1)
            dve.wait_ge(sums, 1)


def wait(eng, sem, value):
    if not isinstance(value, int) or value > 0:
        eng.wait_ge(sem, value)


def looped(eng, iterations, body):
    body(0, True, False)
    with eng.Fori(1, iterations - 1) as i:
        body(i, False, False)
    body(iterations - 1, False, True)


def stage_experts(nc, G, I, S):
    xl_mm, xl_hi, xl_lo = (G.sem("ex_" + n) for n in ("xl_mm", "xl_hi", "xl_lo"))
    w_in, wb_in = ([G.sem(f"ex_{n}{k}") for k in range(2)] for n in ("w_in", "wb_in"))
    w_hi, w_lo, g_mm, u_mm, r_done, rw_done = (G.sem("ex_" + n) for n in
                                              ("w_hi", "w_lo", "g_mm", "u_mm", "relu", "rw"))
    t_done, h_done, hh_done, hl_done, down_done = (G.sem("ex_" + n) for n in ("t", "h", "hh", "hl", "down"))
    acc_hi, acc_lo = G.sem("ex_acc_hi"), G.sem("ex_acc_lo")
    U = 2 * NB
    W = 2 * HID + 2 * LAT
    RING = 2
    with ExitStack() as stack:
        M = Memory(nc, stack, "ex_")
        xlh, xll = M.sb("xlh", [P, T], F32R), M.sb("xll", [P, T], F32R)
        wdh, wdl = M.sb("wdh", [P, NC * LAT], F32R), M.sb("wdl", [P, NC * LAT], F32R)
        split_weights(nc, G, "exw_", [(wdh[:, :], wdl[:, :], I["wdT"].rearrange("(c p) n -> p c n", p=P))], NC * LAT)
        ws = M.sb("ws", [P, 2, W])
        wh, wl = M.sb("wh", [P, 2, W], F32R), M.sb("wl", [P, 2, W], F32R)
        wb = M.sb("wb", [P, 2, T])
        r, rw, tt, hh, hl = (M.sb(n, [P, RING, TB], dt) for n, dt in
                             (("r", F32), ("rw", F32), ("t", F32), ("hh", F32R), ("hl", F32R)))
        h = M.sb("h", [P, RING, TB])
        block = stack.enter_context(nc.Block())
        acc = [G.ps[b] for b in range(NB)]
        gate = [G.ps[NB + k] for k in range(2)]
        up = [G.ps[NB + 2 + k] for k in range(2)]

        def where(k):
            return k // U, (k % U) // 2, k % 2

        @block.sync
        def _(sp):
            def load(e, par, early):
                if not early:
                    sp.wait_ge(w_lo, e - 1)
                sp.dma_start(ws[:, par, :], I["ew"][bass.ds(e, 1), :, :].rearrange("a p n -> (a p) n")
                             ).then_inc(w_in[par], 16)
                if not early:
                    sp.wait_ge(rw_done, (e - 1) * U)
                sp.dma_start(wb[:, par, :], S.wscr[bass.ds(e, 1), :].rearrange("a n -> (a n)").partition_broadcast(P)
                             ).then_inc(wb_in[par], 16)

            load(0, 0, True)
            load(1, 1, True)
            with sp.Fori(1, EXPERTS // 2) as i:
                for par in range(2):
                    load(i * 2 + par, par, False)

        @block.tensor
        def _(pe):
            for b in range(NB):
                cols = slice(b * TB, (b + 1) * TB)
                mm3(pe, acc[b][:, :], [((wdh[:, c * LAT:(c + 1) * LAT], wdl[:, c * LAT:(c + 1) * LAT]),
                                        (G.xTh[:, c, cols], G.xTl[:, c, cols])) for c in range(NC)]
                    ).then_inc(xl_mm, 1)
            pe.wait_ge(xl_lo, NB)

            def w(par, col):
                return wh[:, par, col:col + P], wl[:, par, col:col + P]

            def xl(b):
                return xlh[:, b * TB:(b + 1) * TB], xll[:, b * TB:(b + 1) * TB]

            def gates(i, k):
                n = i * 2 * U + k
                par, b, half = where(k % (2 * U))
                if k % U == 0:
                    wait(pe, w_lo, i * 2 + k // U + 1)
                wait(pe, r_done, n - 1)
                mm3(pe, gate[k % 2][:, :], [(w(par, HID + half * P), xl(b))]).then_inc(g_mm, 1)

            def ups(i, k):
                n = i * 2 * U + k
                par, b, half = where(k)
                wait(pe, h_done, n - 1)
                mm3(pe, up[k % 2][:, :], [(w(par, half * P), xl(b))]).then_inc(u_mm, 1)

            def downs(i, k, first, last):
                n = i * 2 * U + k
                par, b, half = where(k % (2 * U))
                wait(pe, hl_done, n + 1)
                s = k % 2
                mm3(pe, acc[b][:, :], [(w(par, 2 * HID + half * P), (hh[:, s, :], hl[:, s, :]))],
                    start=first and 0 <= k < U and half == 0, stop=last and k >= U and half == 1,
                    skip_group_check=True).then_inc(down_done, 1)

            gates(0, 0)

            def body(i, first, last):
                for k in range(2 * U):
                    if not (last and k == 2 * U - 1):
                        gates(i, k + 1)
                    ups(i, k)
                    if not (first and k < 2):
                        downs(i, k - 2, first, last)

            looped(pe, EXPERTS // 2, body)
            for k in range(2 * U - 2, 2 * U):
                downs(EXPERTS // 2 - 1, k, False, True)

        @block.scalar
        def _(act):
            for b in range(NB):
                act.wait_ge(xl_mm, b + 1)
                act.activation(xlh[:, b * TB:(b + 1) * TB], acc[b][:, :], ACT.Copy).then_inc(xl_hi, 1)

            def split(i, e):
                n = i * 2 + e
                act.wait_ge(w_in[e % 2], i * 16 + 16 * (e // 2) + 16)
                wait(act, down_done, (n - 1) * U)
                act.activation(wh[:, e % 2, :], ws[:, e % 2, :], ACT.Copy).then_inc(w_hi, 1)

            def relu(i, k):
                n = i * 2 * U + k
                act.wait_ge(g_mm, n + 1)
                wait(act, t_done, n - 1)
                act.activation(r[:, k % 2, :], gate[k % 2][:, :], ACT.Relu).then_inc(r_done, 1)

            def high(i, k):
                n = i * 2 * U + k
                act.wait_ge(h_done, n + 1)
                wait(act, down_done, n - 1)
                act.activation(hh[:, k % 2, :], h[:, k % 2, :], ACT.Copy).then_inc(hh_done, 1)

            split(0, 0)
            relu(0, 0)

            def body(i, first, last):
                for k in range(2 * U):
                    if not (last and k == 2 * U - 1):
                        relu(i, k + 1)
                    high(i, k)
                    if k % U == 3 and not (last and k > U):
                        split(i, k // U + 1)

            looped(act, EXPERTS // 2, body)
            for b in range(NB):
                act.wait_ge(down_done, EXPERTS * U)
                act.activation(G.acch[:, b * TB:(b + 1) * TB], acc[b][:, :], ACT.Copy).then_inc(acc_hi, 1)

        @block.gpsimd
        def _(pool):
            def split(i, e):
                n = i * 2 + e
                pool.wait_ge(w_hi, n + 1)
                pool.tensor_tensor(wl[:, e % 2, :], ws[:, e % 2, :], raw(wh[:, e % 2, :]), ALU.subtract).then_inc(w_lo, 1)

            def weigh(i, k):
                n = i * 2 * U + k
                par, b, half = where(k)
                if k % U == 0:
                    pool.wait_ge(wb_in[par], i * 16 + 16)
                pool.wait_ge(r_done, n + 1)
                wait(pool, t_done, n - 1)
                pool.tensor_tensor(rw[:, k % 2, :], r[:, k % 2, :], wb[:, par, b * TB:(b + 1) * TB],
                                   ALU.mult).then_inc(rw_done, 1)

            split(0, 0)

            def body(i, first, last):
                for k in range(2 * U):
                    weigh(i, k)
                    if k % U == 4 and not (last and k > U):
                        split(i, k // U + 1)

            looped(pool, EXPERTS // 2, body)

        @block.vector
        def _(dve):
            for b in range(NB):
                cols = slice(b * TB, (b + 1) * TB)
                dve.wait_ge(xl_hi, b + 1)
                dve.tensor_tensor(xll[:, cols], acc[b][:, :], raw(xlh[:, cols]), ALU.subtract).then_inc(xl_lo, 1)

            def square(i, k):
                n = i * 2 * U + k
                dve.wait_ge(rw_done, n + 1)
                wait(dve, h_done, n - 1)
                dve.tensor_tensor(tt[:, k % 2, :], r[:, k % 2, :], rw[:, k % 2, :], ALU.mult).then_inc(t_done, 1)

            def hidden(i, k):
                n = i * 2 * U + k
                dve.wait_ge(u_mm, n + 1)
                dve.wait_ge(t_done, n + 1)
                wait(dve, hl_done, n - 1)
                dve.tensor_tensor(h[:, k % 2, :], up[k % 2][:, :], tt[:, k % 2, :], ALU.mult).then_inc(h_done, 1)

            def low(i, k):
                n = i * 2 * U + k
                dve.wait_ge(hh_done, n + 1)
                wait(dve, down_done, n - 1)
                dve.tensor_tensor(hl[:, k % 2, :], h[:, k % 2, :], raw(hh[:, k % 2, :]), ALU.subtract).then_inc(hl_done, 1)

            square(0, 0)

            def body(i, first, last):
                for k in range(2 * U):
                    hidden(i, k)
                    if not (last and k == 2 * U - 1):
                        square(i, k + 1)
                    low(i, k)

            looped(dve, EXPERTS // 2, body)
            for b in range(NB):
                cols = slice(b * TB, (b + 1) * TB)
                dve.wait_ge(acc_hi, b + 1)
                dve.tensor_tensor(G.accl[:, cols], acc[b][:, :], raw(G.acch[:, cols]), ALU.subtract).then_inc(acc_lo, 1)


def stage_attend0(nc, G, I):
    q_mm, e_done, r_done, qp_done, z_mm, zi_done, zs_mm, zs_sb, a_mm, at_done, link, b_in = (
        G.sem("at_" + n) for n in ("q_mm", "e", "r", "qp", "z_mm", "zi", "zs_mm", "zs_sb", "a_mm", "at", "link", "b_in"))
    n_done, nqb_done = G.sem("at_n"), G.sem("at_nqb")
    with ExitStack() as stack:
        M = Memory(nc, stack, "at_")
        qh, ql = M.sb("qh", [P, NC * D], F32R), M.sb("ql", [P, NC * D], F32R)
        split_weights(nc, G, "atw_", [(qh[:, :], ql[:, :], I["qT"].rearrange("(c p) n -> p c n", p=P))], NC * D)
        qb, nqb = M.sb("qb", [P, NC]), M.sb("nqb", [P, NC])
        e, r, qp = M.sb("e", [P, 2, TB]), M.sb("r", [P, 2, TB]), M.sb("qp", [P, 2 * NC, TB])
        zi, zs = M.sb("zi", [H0, TB]), M.sb("zs", [P, 2, TB])
        zh, zl = M.sb("zh", [P, 2, TB], F32R), M.sb("zl", [P, 2, TB], F32R)
        zz = M.sb("zz", [P, TB])
        block = stack.enter_context(nc.Block())
        UN = NB * NC

        @block.sync
        def _(sp):
            sp.dma_start(qb[:, :], I["q_b"]).then_inc(b_in, 16)

        @block.tensor
        def _(pe):
            def queries(b):
                cols = slice(b * TB, (b + 1) * TB)
                for g in range(NC):
                    n = b * NC + g
                    wait(pe, e_done, n - 1)
                    wait(pe, r_done, n - 1)
                    mm3(pe, G.ps[n % 2][:, :], [((qh[:, c * D + g * P:c * D + (g + 1) * P], ql[:, c * D + g * P:c * D + (g + 1) * P]),
                                                 (G.xTh[:, c, cols], G.xTl[:, c, cols])) for c in range(NC)]).then_inc(q_mm, 1)

            def attend(b):
                wait(pe, zi_done, b - 1)
                for g in range(NC):
                    n = b * NC + g
                    pe.wait_ge(qp_done, n + 1)
                    last = pe.matmul(G.ps[6 + b % 2][0:H0, :], G.ksb[:, g, :], qp[:, n % (2 * NC), :],
                                     start=g == 0, stop=g == NC - 1)
                last.then_inc(z_mm, 1)
                for g in range(NC):
                    n = b * NC + g
                    wait(pe, at_done, n - 1)
                    pe.matmul(G.ps[2 + n % 2][:, :], G.kvb[:, g, :], qp[:, n % (2 * NC), :],
                              start=True, stop=True).then_inc(a_mm, 1)
                    if g == 0:
                        pe.wait_ge(zi_done, b + 1)
                    wait(pe, zs_sb, n - 1)
                    for m, z in enumerate((zh, zl)):
                        last = pe.matmul(G.ps[4 + n % 2][:, :], G.headsel[:, g, :], z[:, b % 2, :],
                                         start=m == 0, stop=m == 1)
                    last.then_inc(zs_mm, 1)

            queries(0)
            for b in range(NB):
                if b + 1 < NB:
                    queries(b + 1)
                attend(b)

        @block.scalar
        def _(act):
            act.wait_ge(b_in, 16)
            act.mul(nqb[:, :], qb[:, :], -1.0).then_inc(nqb_done, 1)
            act.wait_ge(nqb_done, 1)
            def features(b):
                for g in range(NC):
                    n = b * NC + g
                    act.wait_ge(q_mm, n + 1)
                    wait(act, qp_done, n - 1)
                    act.activation(e[:, n % 2, :], G.ps[n % 2][:, :], ACT.Relu, bias=nqb[:, g:g + 1],
                                   scale=-1.0).then_inc(n_done, 1)
                    act.wait_ge(n_done, n + 1)
                    act.activation(e[:, n % 2, :], e[:, n % 2, :], ACT.Exp, scale=-1.0).then_inc(e_done, 1)
                    act.activation(r[:, n % 2, :], G.ps[n % 2][:, :], ACT.Relu, bias=qb[:, g:g + 1]).then_inc(r_done, 1)

            features(0)
            for b in range(NB):
                if b + 1 < NB:
                    features(b + 1)
                for g in range(NC):
                    n = b * NC + g
                    act.wait_ge(zs_mm, n + 1)
                    wait(act, at_done, n - 1)
                    act.activation(zs[:, n % 2, :], G.ps[4 + n % 2][:, :], ACT.Copy).then_inc(zs_sb, 1)

        @block.vector
        def _(dve):
            chain = Chain(dve, link)
            chain.done(dve.memset(zz[:, :], 0.0))
            for s in range(2):
                dve.tensor_copy(zh[:, s, :], zz[:, :])
                last = dve.tensor_copy(zl[:, s, :], zz[:, :])
            chain.done(last)
            def features(b):
                for g in range(NC):
                    n = b * NC + g
                    dve.wait_ge(e_done, n + 1)
                    dve.wait_ge(r_done, n + 1)
                    wait(dve, a_mm, n - 2 * NC + 1)
                    dve.tensor_tensor(qp[:, n % (2 * NC), :], e[:, n % 2, :], r[:, n % 2, :], ALU.add).then_inc(qp_done, 1)

            features(0)
            for b in range(NB):
                if b + 1 < NB:
                    features(b + 1)
                dve.wait_ge(z_mm, b + 1)
                wait(dve, zs_mm, (b - 1) * NC)
                chain.done(dve.tensor_scalar_add(zi[:, :], G.ps[6 + b % 2][0:H0, :], RMS_EPS))
                chain.done(dve.reciprocal(zi[:, :], zi[:, :]))
                chain.done(dve.tensor_copy(zh[0:H0, b % 2, :], zi[:, :]))
                dve.tensor_tensor(zl[0:H0, b % 2, :], zi[:, :], raw(zh[0:H0, b % 2, :]),
                                  ALU.subtract).then_inc(zi_done, 1)
                for g in range(NC):
                    n = b * NC + g
                    dve.wait_ge(a_mm, n + 1)
                    dve.wait_ge(zs_sb, n + 1)
                    dve.tensor_tensor(G.X[:, n, :], G.ps[2 + n % 2][:, :], zs[:, n % 2, :], ALU.mult).then_inc(at_done, 1)


def stage_output0(nc, G, I):
    names = ("u_mm", "r", "t", "h", "hh", "hl", "ath", "atl", "o_mm", "x1")
    u_mm, r_done, t_done, h_done, hh_done, hl_done, ath_done, atl_done, o_mm, x1_done = (G.sem("o0_" + n) for n in names)
    x_in = [G.sem(f"o0_x_in{n}") for n in range(2)]
    xb_done, b_in = G.sem("o0_xb"), G.sem("o0_b_in")
    with ExitStack() as stack:
        M = Memory(nc, stack, "o0_")
        w = {}
        jobs = []
        for name, src, cols in (("sw1", "sw1T", NC * HID), ("swg", "swgT", NC * HID), ("o", "oT", NC * D),
                                ("sw2", "sw2T", 2 * D), ("up", "wupT", D)):
            w[name] = (M.sb(name + "h", [P, cols], F32R), M.sb(name + "l", [P, cols], F32R))
            jobs.append((w[name][0][:, :], w[name][1][:, :], I[src].rearrange("(c p) n -> p c n", p=P)))
        split_weights(nc, G, "o0w_", jobs, NC * D)
        ob = M.sb("ob", [P, D])
        ath, atl = M.sb("ath", [P, NC, TB], F32R), M.sb("atl", [P, NC, TB], F32R)
        hsh, hsl = M.sb("hsh", [P, 2, TB], F32R), M.sb("hsl", [P, 2, TB], F32R)
        r, h = M.sb("r", [P, TB]), M.sb("h", [P, TB])
        xr = M.sb("xr", [P, 2, D])
        block = stack.enter_context(nc.Block())

        def cut(name, width, c, col, n):
            a = c * width + col
            return w[name][0][:, a:a + n], w[name][1][:, a:a + n]

        @block.sync
        def _(sp):
            sp.dma_start(ob[:, :], I["o_b"].partition_broadcast(P)).then_inc(b_in, 16)
            for t in range(NT):
                wait(sp, x1_done, t - 1)
                sp.dma_start(xr[:, t % 2, :], I["x"][t * P:(t + 1) * P, :]).then_inc(x_in[t % 2], 16)

        @block.gpsimd
        def _(pool):
            pool.wait_ge(b_in, 16)
            for t in range(NT):
                pool.wait_ge(x_in[t % 2], 16 * (t // 2 + 1))
                pool.tensor_tensor(xr[:, t % 2, :], xr[:, t % 2, :], ob[:, :], ALU.add).then_inc(xb_done, 1)

        @block.tensor
        def _(pe):
            def shared(b):
                cols = slice(b * TB, (b + 1) * TB)
                for half in range(2):
                    n = 2 * b + half
                    wait(pe, h_done, n - 1)
                    for k, name in enumerate(("swg", "sw1")):
                        mm3(pe, G.ps[2 * (n % 2) + k][:, :], [(cut(name, HID, c, half * P, P), (G.xTh[:, c, cols], G.xTl[:, c, cols]))
                                                              for c in range(NC)]).then_inc(u_mm, 1)

            def outputs(b):
                pe.wait_ge(atl_done, (b + 1) * NC)
                pe.wait_ge(hl_done, 2 * (b + 1))
                for k in range(BT):
                    t = b * BT + k
                    wait(pe, x1_done, t - 1)
                    rows = slice(k * P, (k + 1) * P)
                    parts = [((ath[:, g, rows], atl[:, g, rows]), cut("o", D, g, 0, D)) for g in range(NC)]
                    parts += [((hsh[:, c, rows], hsl[:, c, rows]), cut("sw2", D, c, 0, D)) for c in range(2)]
                    parts += [((G.acch[:, t * P:(t + 1) * P], G.accl[:, t * P:(t + 1) * P]), cut("up", D, 0, 0, D))]
                    mm3(pe, G.ps[4 + t % 2][:, :], parts).then_inc(o_mm, 1)

            shared(0)
            for b in range(NB):
                if b + 1 < NB:
                    shared(b + 1)
                outputs(b)

        @block.scalar
        def _(act):
            for b in range(NB):
                for half in range(2):
                    n = 2 * b + half
                    act.wait_ge(u_mm, 2 * n + 1)
                    wait(act, h_done, n)
                    act.activation(r[:, :], G.ps[2 * (n % 2)][:, :], ACT.Relu).then_inc(r_done, 1)
                    act.wait_ge(h_done, n + 1)
                    wait(act, o_mm, b * BT)
                    act.activation(hsh[:, half, :], h[:, :], ACT.Copy).then_inc(hh_done, 1)
                wait(act, o_mm, b * BT)
                for g in range(NC):
                    act.activation(ath[:, g, :], G.X[:, b * NC + g, :], ACT.Copy).then_inc(ath_done, 1)

        @block.vector
        def _(dve):
            for step in range(NB + 1):
                b = step
                if step < NB:
                    for half in range(2):
                        n = 2 * b + half
                        dve.wait_ge(r_done, n + 1)
                        wait(dve, hl_done, n)
                        dve.tensor_tensor(r[:, :], r[:, :], r[:, :], ALU.mult).then_inc(t_done, 1)
                        dve.wait_ge(t_done, n + 1)
                        dve.wait_ge(u_mm, 2 * n + 2)
                        dve.tensor_tensor(h[:, :], G.ps[2 * (n % 2) + 1][:, :], r[:, :], ALU.mult).then_inc(h_done, 1)
                        dve.wait_ge(hh_done, n + 1)
                        wait(dve, o_mm, b * BT)
                        dve.tensor_tensor(hsl[:, half, :], h[:, :], raw(hsh[:, half, :]), ALU.subtract).then_inc(hl_done, 1)
                    for g in range(NC):
                        dve.wait_ge(ath_done, b * NC + g + 1)
                        dve.tensor_tensor(atl[:, g, :], G.X[:, b * NC + g, :], raw(ath[:, g, :]), ALU.subtract).then_inc(atl_done, 1)
                    dve.wait_ge(atl_done, (b + 1) * NC)
                    for k in range(BT):
                        t = b * BT + k
                        dve.wait_ge(o_mm, t + 1)
                        dve.wait_ge(xb_done, t + 1)
                        dve.tensor_tensor(G.X[:, t, :], G.ps[4 + t % 2][:, :], xr[:, t % 2, :], ALU.add).then_inc(x1_done, 1)


def stage_qkv(nc, G, I, S):
    names = ("qk_mm", "v_mm", "sq", "ms", "sd", "qn", "t1", "t2", "y", "yt_mm", "hh", "hl", "v_sb", "link", "tables", "ones")
    qk_mm, v_mm, sq_done, ms_done, sd_done, qn_done, t1_done, t2_done, y_done, yt_mm, hh_done, hl_done, v_sb, link, tables, ones_done = (
        G.sem("qkv_" + n) for n in names)
    tab_in = G.sem("qkv_tab_in")
    qk_out, v_out = ([G.sem(f"qkv_{n}{k}") for k in range(2)] for n in ("qk_out", "v_out"))
    with ExitStack() as stack:
        M = Memory(nc, stack, "qkv_")
        w = {n: (M.sb(n + "h", [P, NC * D], F32R), M.sb(n + "l", [P, NC * D], F32R)) for n in "qkv"}
        split_weights(nc, G, "qkvw_", [
            (w[n][0][:, :], w[n][1][:, :], I["w_qkv"][:, k * D:(k + 1) * D].rearrange("(c p) n -> p c n", p=P))
            for k, n in enumerate("qkv")], NC * D)
        cs = [M.sb("cos", [P, NT, HD]), M.sb("sin", [P, NT, HD])]
        gam = M.sb("gam", [P, 2, 2, HD])
        tab = M.sb("tab", [P, 2, 2, NT, HD])
        sq = M.sb("sq", [P, 2, D])
        ms, sd, rs = (M.sb(n, [P, 2, H0]) for n in ("ms", "sd", "rs"))
        qn, t1, t2 = (M.sb(n, [P, 2, D]) for n in ("qn", "t1", "t2"))
        yh, yl = M.sb("yh", [P, 2, 2, NC, P], F32R), M.sb("yl", [P, 2, 2, NC, P], F32R)
        vs = M.sb("vs", [P, 2, H0, 2 * HD])
        block = stack.enter_context(nc.Block())

        @block.sync
        def _(sp):
            for k, n in enumerate(("cos32", "sin32")):
                sp.dma_start(cs[k][:, :, :], I[n].rearrange("(t p) d -> p t d", p=P)).then_inc(tab_in, 16)
            for k, n in enumerate(("q_gamma", "k_gamma")):
                for m in range(2):
                    sp.dma_start(gam[:, k, m, :], I[n][m, :].partition_broadcast(P)).then_inc(tab_in, 16)
            for t in range(NT):
                rows = slice(t * P, (t + 1) * P)
                sp.wait_ge(v_sb, t + 1)
                sp.dma_start(S.v[:, :, t, :].rearrange("r p n -> p r n"),
                             vs[:, t % 2, :, :].rearrange("p (r h) n -> p r (h n)", h=2)).then_inc(v_out[t % 2], 16)
                sp.wait_ge(hl_done, 2 * (t + 1))
                for k in range(2):
                    for part, y in enumerate((yh, yl)):
                        sp.dma_start(S.qk[k, part, :, rows].rearrange("(g p) t -> p g t", p=P),
                                     raw(y[:, t % 2, k, :, :])).then_inc(qk_out[t % 2], 16)
            for k in range(2):
                sp.wait_ge(v_out[k], 16 * NT // 2)
                sp.wait_ge(qk_out[k], 64 * NT // 2)

        @block.tensor
        def _(pe):
            def x(t, c):
                cols = slice(t * P, (t + 1) * P)
                return G.xTh[:, c, cols], G.xTl[:, c, cols]

            def product(t, n, bank):
                return mm3(pe, G.ps[bank], [(x(t, c), (w[n][0][:, c * D:(c + 1) * D], w[n][1][:, c * D:(c + 1) * D]))
                                            for c in range(NC)])

            def transposes(t):
                for k in range(2):
                    pe.wait_ge(y_done, 2 * t + k + 1)
                    wait(pe, hl_done, 2 * (t - 1) + k + 1)
                    for g in range(NC):
                        last = pe.transpose(G.ps[6 + k][:, g * P:(g + 1) * P], t2[:, k, g * P:(g + 1) * P], G.ident[:, :])
                    last.then_inc(yt_mm, 1)

            for t in range(NT):
                for k in range(2):
                    wait(pe, qn_done, 2 * (t - 2) + k + 1)
                    product(t, "qk"[k], 2 * (t % 2) + k).then_inc(qk_mm, 1)
                if t >= 1:
                    transposes(t - 1)
                wait(pe, v_sb, t - 1)
                product(t, "v", 4 + t % 2).then_inc(v_mm, 1)
            transposes(NT - 1)

        @block.scalar
        def _(act):
            def high(t):
                for k in range(2):
                    act.wait_ge(yt_mm, 2 * t + k + 1)
                    if t >= 2:
                        act.wait_ge(qk_out[t % 2], 64 * (t // 2))
                    act.activation(yh[:, t % 2, k, :, :], G.ps[6 + k].rearrange("p (g n) -> p g n", g=NC),
                                   ACT.Copy).then_inc(hh_done, 1)

            act.wait_ge(ones_done, 1)
            for t in range(NT):
                for k in range(2):
                    act.wait_ge(qk_mm, 2 * t + k + 1)
                    wait(act, ms_done, t)
                    act.activation(sq[:, k, :], G.ps[2 * (t % 2) + k], ACT.Square).then_inc(sq_done, 1)
                act.wait_ge(ms_done, t + 1)
                act.activation(sd[:, :, :], ms[:, :, :], ACT.Sqrt).then_inc(sd_done, 1)
                if t >= 1:
                    high(t - 1)
                act.wait_ge(v_mm, t + 1)
                if t >= 2:
                    act.wait_ge(v_out[t % 2], 16 * (t // 2))
                act.activation(vs[:, t % 2, :, 0:HD], G.ps[4 + t % 2].rearrange("p (h d) -> p h d", h=H0),
                               ACT.Copy).then_inc(v_sb, 1)
            high(NT - 1)

        @block.gpsimd
        def _(pool):
            pool.memset(vs[:, :, :, HD:2 * HD], 1.0).then_inc(ones_done, 1)
            pool.wait_ge(tables, 1)
            for t in range(NT):
                for k in range(2):
                    pool.wait_ge(qn_done, 2 * t + k + 1)
                    wait(pool, y_done, 2 * (t - 1) + k + 1)
                    pool.tensor_tensor(t1[:, k, :].rearrange("p (h d) -> p h d", h=H0),
                                       qn[:, k, :].rearrange("p (h d) -> p h d", h=H0),
                                       tab[:, k, 0, t, :].unsqueeze(1).to_broadcast([P, H0, HD]), ALU.mult).then_inc(t1_done, 1)

        @block.vector
        def _(dve):
            chain = Chain(dve, link)
            dve.wait_ge(tab_in, 96)
            for k in range(2):
                for m in range(2):
                    last = dve.tensor_tensor(tab[:, k, m, :, :], cs[m][:, :, :],
                                             gam[:, k, m, :].unsqueeze(1).to_broadcast([P, NT, HD]), ALU.mult)
            last.then_inc(tables, 1)
            dve.wait_ge(tables, 1)

            def low(t):
                for k in range(2):
                    dve.wait_ge(hh_done, 2 * t + k + 1)
                    dve.tensor_tensor(yl[:, t % 2, k, :, :], G.ps[6 + k].rearrange("p (g n) -> p g n", g=NC),
                                      raw(yh[:, t % 2, k, :, :]), ALU.subtract).then_inc(hl_done, 1)

            for t in range(NT):
                dve.wait_ge(sq_done, 2 * (t + 1))
                chain.done(dve.reduce_sum(ms[:, :, :], sq[:, :, :].rearrange("p k (h d) -> p k h d", h=H0), axis=AX))
                wait(dve, sd_done, t)
                dve.tensor_scalar(ms[:, :, :], ms[:, :, :], 1.0 / HD, RMS_EPS, ALU.mult, ALU.add).then_inc(ms_done, 1)
                if t >= 1:
                    low(t - 1)
                dve.wait_ge(sd_done, t + 1)
                chain.done(dve.reciprocal(rs[:, :, :], sd[:, :, :]))
                for k in range(2):
                    dve.tensor_tensor(qn[:, k, :].rearrange("p (h d) -> p h d", h=H0),
                                      G.ps[2 * (t % 2) + k].rearrange("p (h d) -> p h d", h=H0),
                                      rs[:, k, :].unsqueeze(2).to_broadcast([P, H0, HD]), ALU.mult).then_inc(qn_done, 1)
                for k in range(2):
                    dve.wait_ge(qn_done, 2 * t + k + 1)
                    wait(dve, yt_mm, 2 * (t - 1) + k + 1)
                    q4 = qn[:, k, :].rearrange("p (h d) -> p h d", h=H0)
                    r4 = t2[:, k, :].rearrange("p (h d) -> p h d", h=H0)
                    half = HD // 2
                    for m in range(2):
                        sin = tab[:, k, 1, t, m * half:(m + 1) * half].unsqueeze(1).to_broadcast([P, H0, half])
                        last = dve.tensor_tensor(r4[:, :, m * half:(m + 1) * half],
                                                 q4[:, :, (1 - m) * half:(2 - m) * half], sin, ALU.mult)
                    last.then_inc(t2_done, 1)
                for k in range(2):
                    dve.wait_ge(t2_done, 2 * t + k + 1)
                    dve.wait_ge(t1_done, 2 * t + k + 1)
                    dve.tensor_tensor(t2[:, k, :], t2[:, k, :], t1[:, k, :], ALU.add).then_inc(y_done, 1)
            low(NT - 1)


class Plan:

    def __init__(self, b):
        back = WINDOW // P
        q0, q1 = b * BT, (b + 1) * BT
        keys = [(kt, max(q0, kt), min(q1 - 1, kt + back)) for kt in range(max(0, q0 - back), q1)]
        self.keys = sorted(keys, key=lambda k: -(k[2] - k[1]))
        self.maxima = []
        for qt in range(q0, q1):
            first = max(0, qt - back)
            count = qt - first + 1
            pieces = -(-count // BT)
            cuts = [first + count * k // pieces for k in range(pieces + 1)]
            self.maxima.append((qt, list(zip(cuts, cuts[1:]))))
        self.chunks = 2 * sum(len(c) for _, c in self.maxima)
        self.back = back


def stage_attend1(nc, G, I, S):
    K3 = 3 * HD
    KM = K3 + 2
    plans = [Plan(b) for b in range(NB)]
    PAIRS = H0 // 2
    keys_before = [sum(len(p.keys) for p in plans[:b]) for b in range(NB)]
    KEYS = sum(len(p.keys) for p in plans)
    chunks_before = [sum(p.chunks for p in plans[:b]) for b in range(NB)]
    CHUNKS = sum(p.chunks for p in plans)
    scale = 1.0 / float(np.sqrt(HD))
    s_mm, p_done, av_mm, a_mm, a_red, m_done, mr_mm, mr_sb, o_sb, kones, link = (G.sem("l1_" + n) for n in (
        "s_mm", "p", "av_mm", "a_mm", "a_red", "m", "mr_mm", "mr_sb", "o_sb", "kones", "link"))
    q_in, k_in, v_in = ([G.sem(f"l1_{n}{k}") for k in range(2)] for n in ("q_in", "k_in", "v_in"))
    o_out = [G.sem(f"l1_o_out{k}") for k in range(2)]
    nm_done, mh_done = G.sem("l1_nm"), G.sem("l1_mh")
    sr_in, iota_done, se_link, sel_done, pos_mm, oh_done, pick_mm = (G.sem("se_" + n) for n in (
        "sr_in", "iota", "link", "sel", "pos_mm", "oh", "pick_mm"))
    PR = 2
    LEAD = 36
    PLACES, PICKS = 2, 6
    with ExitStack() as stack:
        M = Memory(nc, stack, "l1_")
        q, k = M.sb("q", [P, 2, 2, T], F32R), M.sb("k", [P, 2, 2, T], F32R)
        v = M.sb("v", [P, 2, NT, 2, 2 * HD])
        pt = M.sb("pt", [P, PR, 2, TB])
        mx, nm = M.sb("mx", [P, 2, BT, 3]), M.sb("nm", [P, 2, BT])
        mrow = M.sb("mrow", [P, 2, BT, KM], F32R)
        ob = M.sb("ob", [P, 2, TB])
        zero = M.sb("zero", [P, KM])
        sr, junk, same = M.sb("sr", [P, T]), M.sb("junk", [P, 2, T], BF16), M.sb("same", [P, 2, P])
        count, rank, sel = M.sb("count", [P, NT, 3]), M.sb("rank", [P, NT]), M.sb("sel", [P, NT])
        place, numi, ordi = M.sb("place", [P, NT]), M.sb("numi", [P, NT], I32), M.sb("ordi", [P, SEL], I32)
        order, before = M.sb("order", [P, SEL]), M.sb("before", [P, P])
        onehot = M.sb("onehot", [P, NT, SEL])
        block = stack.enter_context(nc.Block())

        def unit(i, u):
            par, b = (u // NB) % 2, u % NB
            pair = i * 2 + u // NB
            return par, b, pair * KEYS + keys_before[b], pair * CHUNKS + chunks_before[b], pair * NB + b

        @block.sync
        def _(sp):
            def load(pair, par, early):
                if not early:
                    sp.wait_ge(av_mm, (pair - 1) * KEYS)
                rows = bass.ds(pair * 2 * HD, 2 * HD)
                for dst, which, sem in ((q, 0, q_in[par]), (k, 1, k_in[par])):
                    for n, part in enumerate((0, which, 1 - which)):
                        sp.dma_start(raw(dst[n * HD:(n + 1) * HD, par, :, :]),
                                     S.qk[which, part, rows, :].rearrange("(h d) t -> d h t", h=2)).then_inc(sem, 16)
                sp.dma_start(v[:, par, :, :, :].rearrange("p t h n -> p (t h n)"),
                             S.v[bass.ds(pair, 1), :, :, :].rearrange("a p t n -> (a p) (t n)")).then_inc(v_in[par], 16)

            def store(unit_no, pair, b):
                sp.wait_ge(o_sb, unit_no + 1)
                for h in range(2):
                    rows = slice(h * 2 * HD, h * 2 * HD + HD)
                    sp.dma_start(S.o[bass.ds(pair * 2 * HD + h * HD, HD), b * TB:(b + 1) * TB], ob[rows, b % 2, :]
                                 ).then_inc(o_out[b % 2], 16)
                    one = slice(h * 2 * HD + HD, h * 2 * HD + HD + 1)
                    sp.dma_start(S.den[bass.ds(pair * 2 + h, 1), b * TB:(b + 1) * TB], ob[one, b % 2, :]
                                 ).then_inc(o_out[b % 2], 16)

            load(0, 0, True)
            load(1, 1, True)
            sp.dma_start(sr[:, :], S.score.partition_broadcast(P)).then_inc(sr_in, 16)
            load_routed_qkv(sp, G, I)

            def body(i, first, last):
                for u in range(2 * NB):
                    par, b, _, _, no = unit(i, u)
                    store(no, i * 2 + par, b)
                    if b == NB - 1 and not last:
                        load(i * 2 + 2 + par, par, False)

            looped(sp, PAIRS // 2, body)
            for n in range(2):
                sp.wait_ge(o_out[n], 64 * PAIRS * NB // 2)

        assert KEYS % 2 == 0

        def position(u, j):
            return (u // NB) * KEYS + keys_before[u % NB] + j

        def step_slot(b, j):
            return (keys_before[b] + j) % 2

        sequence, late = [], []
        for u in range(2 * NB):
            chunks = [(u, "chunk", h, m, c, k0, k1) for h in range(2)
                      for m, (qt, cuts) in enumerate(plans[u % NB].maxima) for c, (k0, k1) in enumerate(cuts)]
            sequence += chunks[:3] + late + chunks[3:]
            late = [(u, "rows", 0), (u, "rows", 1)]
        sequence += late
        SEQ = len(sequence)
        assert SEQ % 2 == 0
        chunks_upto = [sum(e[1] == "chunk" for e in sequence[:n + 1]) for n in range(SEQ)]
        rows_upto = [n + 1 - c for n, c in enumerate(chunks_upto)]

        def released(i, n):
            if n < 2:
                if isinstance(i, int) and i == 0:
                    return None
                i, n = i - 1, n + SEQ
            if sequence[n - 2][1] == "chunk":
                return a_red, i * 2 * CHUNKS + chunks_upto[n - 2]
            return mr_sb, i * 4 * NB + rows_upto[n - 2]

        def due(i, pos, last):
            def upto(p):
                return LEAD + SEQ * (p + 1) // (2 * KEYS)
            for n in range(0 if pos < 0 else upto(pos - 1), upto(pos)):
                if n < SEQ:
                    yield i, n
                elif not last:
                    yield i + 1, n - SEQ

        @block.tensor
        def _(pe):
            def maximum(i, n):
                u, kind, h = sequence[n][:3]
                par, b, _, _, no = unit(i, u)
                bank = G.ps[6 + n % 2]
                before = released(i, n)
                if before:
                    wait(pe, *before)
                if kind == "chunk":
                    _, _, _, m, c, k0, k1 = sequence[n]
                    if b == 0 and h == 0 and m == 0 and c == 0:
                        pe.wait_ge(q_in[par], (i + 1) * 48)
                        pe.wait_ge(k_in[par], (i + 1) * 48)
                    qt = b * BT + m
                    out = bank[:, 0:(k1 - k0) * P]
                    diag, edge = k1 == qt + 1, qt >= plans[b].back and k0 == qt - plans[b].back
                    last = pe.matmul(out, q[0:K3, par, h, qt * P:(qt + 1) * P], k[0:K3, par, h, k0 * P:k1 * P],
                                     start=True, stop=not (diag or edge))
                    if diag:
                        last = pe.matmul(bank[:, (k1 - 1 - k0) * P:(k1 - k0) * P], G.identb[:, :], G.lower[:, :],
                                         start=False, stop=not edge)
                    if edge:
                        last = pe.matmul(bank[:, 0:P], G.identb[:, :], G.upper[:, :], start=False, stop=True)
                    last.then_inc(a_mm, 1)
                else:
                    pe.wait_ge(m_done, no + 1)
                    for m in range(BT):
                        last = pe.matmul(bank[0:KM, m * P:(m + 1) * P], mrow[:, h, m, :], G.identr[:, :],
                                         start=True, stop=True)
                    last.then_inc(mr_mm, 1)

            def scores(i, u, j):
                par, b, keys, _, no = unit(i, u)
                kt, qa, qz = plans[b].keys[j]
                n = keys + j
                wait(pe, p_done, n - 1)
                if j == 0:
                    pe.wait_ge(mr_sb, 2 * no + 2)
                width = (qz - qa + 1) * P
                slot = step_slot(b, j)
                diag, edge = kt == qa, kt + plans[b].back == qz
                for h in range(2):
                    bank = G.ps[2 * slot + h]
                    last = pe.matmul(bank[:, 0:width], k[0:KM, par, h, kt * P:(kt + 1) * P],
                                     q[0:KM, par, h, qa * P:(qz + 1) * P], start=True, stop=not (diag or edge))
                    if diag:
                        last = pe.matmul(bank[:, 0:P], G.identb[:, :], G.upper[:, :], start=False, stop=not edge)
                    if edge:
                        last = pe.matmul(bank[:, width - P:width], G.identb[:, :], G.lower[:, :], start=False, stop=True)
                last.then_inc(s_mm, 1)

            def places():
                pe.wait_ge(sel_done, 1)
                pe.wait_ge(a_red, PAIRS * CHUNKS)
                pe.wait_ge(mr_sb, PAIRS * NB * 2)
                pe.matmul(G.ps[6][:, 0:NT], G.strict[:, :], sel[:, :], start=True, stop=False, skip_group_check=True)
                for t in range(NT - 1):
                    last = pe.matmul(G.ps[6][:, t + 1:NT], G.ones[:, :], sel[:, t:t + 1].to_broadcast([P, NT - 1 - t]),
                                     start=False, stop=t == NT - 2, skip_group_check=True)
                last.then_inc(pos_mm, 1)

            def picks():
                for m in range(NS):
                    for t in range(NT):
                        pe.wait_ge(oh_done, t + 1)
                        last = pe.matmul(G.ps[7][:, 2 * m:2 * m + 2], onehot[:, t, m * P:(m + 1) * P], G.pair[:, t, :],
                                         start=t == 0, stop=t == NT - 1)
                last.then_inc(pick_mm, 1)

            def values(i, u, j):
                par, b, keys, _, no = unit(i, u)
                kt, qa, qz = plans[b].keys[j]
                n = keys + j
                pe.wait_ge(p_done, n + 1)
                if j == 0:
                    wait(pe, o_sb, no - 1)
                    if b == 0:
                        pe.wait_ge(v_in[par], (i + 1) * 16)
                bank = G.ps[4 + b % 2]
                for h in range(2):
                    last = pe.matmul(bank[h * 2 * HD:(h + 1) * 2 * HD, (qa - b * BT) * P:(qz + 1 - b * BT) * P],
                                     v[:, par, kt, h, :], pt[:, step_slot(b, j), h, 0:(qz - qa + 1) * P],
                                     start=j == 0, stop=j == len(plans[b].keys) - 1)
                last.then_inc(av_mm, 1)

            for at in due(0, -1, False):
                maximum(*at)
            scores(0, 0, 0)

            def body(i, first, last):
                for u in range(2 * NB):
                    b = u % NB
                    end = last and u == 2 * NB - 1
                    steps = len(plans[b].keys)
                    for j in range(steps):
                        for at in due(i, position(u, j), last):
                            maximum(*at)
                        if end and j == PLACES:
                            places()
                        if end and j == PICKS:
                            picks()
                        if j + 1 < steps:
                            scores(i, u, j + 1)
                        elif not end:
                            scores(i, u + 1, 0)
                        values(i, u, j)

            looped(pe, PAIRS // 2, body)

        @block.gpsimd
        def _(pool):
            pool.memset(before[:, :], 1.0).then_inc(iota_done, 1)
            pool.iota(numi[:, :], [[P, NT]], base=0, channel_multiplier=1).then_inc(iota_done, 1)
            pool.iota(ordi[:, :], [[1, SEL]], base=1, channel_multiplier=0).then_inc(iota_done, 1)
            pool.wait_ge(iota_done, 3)
            pool.affine_select(out=before[:, :], in_=before[:, :], compare_op=ALU.is_gt, fill=0.0, base=0,
                               pattern=[[-1, P]], channel_multiplier=1).then_inc(iota_done, 1)

        @block.scalar
        def _(act):
            act.wait_ge(kones, 1)

            def exponentials(i, u, j):
                par, b, keys, _, no = unit(i, u)
                kt, qa, qz = plans[b].keys[j]
                n = keys + j
                width = (qz - qa + 1) * P
                slot = step_slot(b, j)
                act.wait_ge(s_mm, n + 1)
                wait(act, av_mm, n - 1)
                act.activation(pt[:, step_slot(b, j), :, 0:width],
                               G.banks[:, 2 * slot:2 * slot + 2, 0:width], ACT.Exp, scale=scale).then_inc(p_done, 1)

            def rows(i, n):
                u, kind, h = sequence[n][:3]
                if kind == "rows":
                    par, b, _, _, no = unit(i, u)
                    act.wait_ge(mr_mm, 2 * no + h + 1)
                    act.activation(q[K3:KM, par, h, b * TB:(b + 1) * TB], G.ps[6 + n % 2][K3:KM, :], ACT.Copy
                                   ).then_inc(mr_sb, 1)

            for at in due(0, -1, False):
                rows(*at)

            def body(i, first, last):
                for u in range(2 * NB):
                    for j in range(len(plans[u % NB].keys)):
                        exponentials(i, u, j)
                        for at in due(i, position(u, j), last):
                            rows(*at)

            looped(act, PAIRS // 2, body)

        @block.vector
        def _(dve):
            chain = Chain(dve, link)
            chain.done(dve.memset(zero[:, :], 0.0))
            for h in range(2):
                for m in range(BT):
                    dve.tensor_copy(mrow[:, h, m, :], zero[:, :])
            for par in range(2):
                for h in range(2):
                    last = dve.tensor_copy(k[K3:KM, par, h, :].rearrange("p (a n) -> p a n", n=P),
                                           G.ones[K3:KM, :].unsqueeze(1).to_broadcast([2, NT, P]))
            chain.done(last)
            dve.memset(mx[:, :, :, :], NEG).then_inc(kones, 1)
            dve.wait_ge(kones, 1)

            def reduce(i, n):
                if sequence[n][1] == "rows":
                    return
                u, _, h, m, c, k0, k1 = sequence[n]
                dve.wait_ge(a_mm, i * 2 * CHUNKS + chunks_upto[n])
                dve.reduce_max(mx[:, h, m, c:c + 1], G.ps[6 + n % 2][:, 0:(k1 - k0) * P], axis=AX).then_inc(a_red, 1)
                if chunks_upto[n] == (u // NB) * CHUNKS + chunks_before[u % NB] + plans[u % NB].chunks:
                    negate(i, u)

            def negate(i, u):
                par, b, _, chunks, no = unit(i, u)
                pieces = max(len(c) for _, c in plans[b].maxima)
                dve.wait_ge(a_red, chunks + plans[b].chunks)
                dve.tensor_reduce(nm[:, :, :], mx[:, :, :, 0:pieces], AX, ALU.max, negate=True).then_inc(nm_done, 1)
                dve.wait_ge(nm_done, no + 1)
                wait(dve, mr_mm, 2 * no)
                dve.tensor_copy(mrow[:, :, :, K3:K3 + 1], nm[:, :, :].unsqueeze(3)).then_inc(mh_done, 1)
                dve.wait_ge(mh_done, no + 1)
                dve.tensor_tensor(mrow[:, :, :, K3 + 1:KM], nm[:, :, :].unsqueeze(3), raw(mrow[:, :, :, K3:K3 + 1]),
                                  ALU.subtract).then_inc(m_done, 1)

            def output(i, u):
                par, b, keys, _, no = unit(i, u)
                dve.wait_ge(av_mm, keys + len(plans[b].keys))
                if i_at_least(i, u, 2):
                    dve.wait_ge(o_out[b % 2], (i * 4 + (u // 2)) * 64)
                dve.tensor_copy(ob[:, b % 2, :], G.ps[4 + b % 2]).then_inc(o_sb, 1)

            def i_at_least(i, u, n):
                return not isinstance(i, int) or i * 2 * NB + u >= n

            tokens = Chain(dve, se_link)

            def ranks(t):
                own = G.pair[:, t, 1:2]
                if t == 0:
                    dve.memset(count[:, :, :], 0.0)
                    dve.wait_ge(iota_done, 4)
                    dve.tensor_copy(G.pair[:, :, 0], numi[:, :])
                    tokens.done(dve.tensor_copy(order[:, :], ordi[:, :]))
                    dve.wait_ge(sr_in, 16)
                else:
                    dve.tensor_scalar(junk[:, t % 2, 0:t * P], sr[:, 0:t * P], own, 0.0, ALU.is_ge, ALU.add,
                                      accum_out=count[:, t, 0:1])
                dve.tensor_scalar(junk[:, t % 2, t * P:T], sr[:, t * P:T], own, 0.0, ALU.is_gt, ALU.add,
                                  accum_out=count[:, t, 1:2])
                tokens.done(dve.scalar_tensor_tensor(same[:, t % 2, :], sr[:, t * P:(t + 1) * P], own, before[:, :],
                                                     ALU.is_equal, ALU.mult, accum_out=count[:, t, 2:3]))
                if t == NT - 1:
                    tokens.done(dve.reduce_sum(rank[:, :], count[:, :, :], axis=AX))
                    dve.tensor_scalar(sel[:, :], rank[:, :], float(SEL), None, ALU.is_lt).then_inc(sel_done, 1)
                    dve.wait_ge(sel_done, 1)

            def onehots():
                dve.wait_ge(pos_mm, 1)
                tokens.done(dve.scalar_tensor_tensor(place[:, :], G.ps[6][:, 0:NT], 1.0, sel[:, :], ALU.add, ALU.mult))
                for t in range(NT):
                    dve.tensor_scalar(onehot[:, t, :], order[:, :], place[:, t:t + 1], None, ALU.is_equal
                                      ).then_inc(oh_done, 1)

            def chosen():
                dve.wait_ge(pick_mm, 1)
                picked = G.ps[7][:, 0:2 * NS].rearrange("p (m n) -> p m n", n=2)
                dve.tensor_copy(G.idx[:, :], picked[:, :, 0])
                dve.tensor_copy(G.selscore[:, :], picked[:, :, 1])

            for at in due(0, -1, False):
                reduce(*at)

            def body(i, first, last):
                for u in range(2 * NB):
                    for j in range(len(plans[u % NB].keys)):
                        for at in due(i, position(u, j), last):
                            reduce(*at)
                        if first and position(u, j) % 4 == 3 and position(u, j) // 4 < NT:
                            ranks(position(u, j) // 4)
                    if last and u == 2 * NB - 1:
                        onehots()
                        chosen()
                    output(i, u)

            looped(dve, PAIRS // 2, body)


def stage_output1(nc, G, I, S, out):
    ohi, olo, on, o_mm, res = (G.sem("o1_" + n) for n in ("hi", "lo", "on", "mm", "res"))
    o_in, rb_in, r_in, stored = ([G.sem(f"o1_{n}{k}") for k in range(2)] for n in ("o_in", "rb_in", "r_in", "stored"))
    with ExitStack() as stack:
        M = Memory(nc, stack, "o1_")
        wh, wl = M.sb("wh", [P, NC * D], F32R), M.sb("wl", [P, NC * D], F32R)
        split_weights(nc, G, "o1w_", [(wh[:, :], wl[:, :], I["w_out"].rearrange("(c p) n -> p c n", p=P))], NC * D)
        o, rb = M.sb("o", [P, 2, NC, TB]), M.sb("rb", [P, 2, NC, TB])
        oh, ol = M.sb("oh", [P, 2, NC, TB], F32R), M.sb("ol", [P, 2, NC, TB], F32R)
        r = M.sb("r", [P, 2, D])
        block = stack.enter_context(nc.Block())

        @block.sync
        def _(sp):
            for b in range(NB):
                cols = slice(b * TB, (b + 1) * TB)
                wait(sp, olo, (b - 1) * NC)
                sp.dma_start(o[:, b % 2, :, :], S.o[:, cols].rearrange("(g p) t -> p g t", p=P)).then_inc(o_in[b % 2], 16)
                for h in range(H0):
                    g, j = h // NC, h % NC
                    sp.dma_start(rb[j * HD:(j + 1) * HD, b % 2, g, :], S.rden[h, cols].partition_broadcast(HD)
                                 ).then_inc(rb_in[b % 2], 16)

        @block.gpsimd
        def _(pool):
            for t in range(NT):
                if t >= 2:
                    pool.wait_ge(stored[t % 2], 16 * (t // 2))
                pool.dma_start(r[:, t % 2, :], S.r[t * P:(t + 1) * P, :]).then_inc(r_in[t % 2], 16)

        @block.scalar
        def _(act):
            for b in range(NB):
                for g in range(NC):
                    act.wait_ge(on, b * NC + g + 1)
                    wait(act, o_mm, (b - 1) * BT)
                    act.activation(oh[:, b % 2, g, :], o[:, b % 2, g, :], ACT.Copy).then_inc(ohi, 1)
                for k in range(BT):
                    t = b * BT + k
                    act.wait_ge(res, t + 1)
                    act.dma_start(out[t * P:(t + 1) * P, :], r[:, t % 2, :]).then_inc(stored[t % 2], 16)
            for k in range(2):
                act.wait_ge(stored[k], 16 * NT // 2)

        @block.vector
        def _(dve):
            for b in range(NB):
                dve.wait_ge(o_in[b % 2], 16 * (b // 2 + 1))
                dve.wait_ge(rb_in[b % 2], 256 * (b // 2 + 1))
                for g in range(NC):
                    dve.tensor_tensor(o[:, b % 2, g, :], o[:, b % 2, g, :], rb[:, b % 2, g, :], ALU.mult).then_inc(on, 1)
                for g in range(NC):
                    dve.wait_ge(ohi, b * NC + g + 1)
                    dve.tensor_tensor(ol[:, b % 2, g, :], o[:, b % 2, g, :], raw(oh[:, b % 2, g, :]), ALU.subtract).then_inc(olo, 1)
                for k in range(BT):
                    t = b * BT + k
                    dve.wait_ge(o_mm, t + 1)
                    dve.wait_ge(r_in[t % 2], 16 * (t // 2 + 1))
                    dve.tensor_tensor(r[:, t % 2, :], G.ps[t % 2], r[:, t % 2, :], ALU.add).then_inc(res, 1)

        @block.tensor
        def _(pe):
            for t in range(NT):
                b, k = t // BT, t % BT
                pe.wait_ge(olo, (b + 1) * NC)
                wait(pe, res, t - 1)
                rows = slice(k * P, (k + 1) * P)
                mm3(pe, G.ps[t % 2], [((oh[:, b % 2, g, rows], ol[:, b % 2, g, rows]),
                                       (wh[:, g * D:(g + 1) * D], wl[:, g * D:(g + 1) * D])) for g in range(NC)]
                    ).then_inc(o_mm, 1)


def routed_qkv(G):
    cut = lambda a, n: G.WA[:, NC * a:NC * (a + n)].rearrange("p (c n) -> p c n", c=NC)
    FQ, FK = NHQ * HDF, NHK * HDF
    return cut(0, FQ), cut(FQ, FK), cut(FQ + FK, FK)


def load_routed_qkv(queue, G, I):
    wq, wk, wv = routed_qkv(G)
    for w, name in ((wk, "wk"), (wq, "wq"), (wv, "wv")):
        queue.dma_start(w, I[name].rearrange("(c p) n -> p c n", p=P)).then_inc(G.wqkv_in, 16)


def stage_routed(nc, G, I, S):
    names = ("gath", "sq", "ms", "sd", "hn", "hT_mm", "hT", "qk_mm", "qb", "t1", "y", "yt_mm", "yt", "v_mm", "v", "link")
    gath, sq_done, ms_done, sd_done, hn_done, hT_mm, hT_done, qk_mm, qb_done, t1_done, y_done, yt_mm, yt_done, v_mm, v_done, link = (
        G.sem("ro_" + n) for n in names)
    names = ("s_mm", "nm", "p", "pn", "pt_mm", "pt", "av_mm", "o", "wo_mm", "x1", "gu_mm", "sig", "m", "dn_mm", "delta", "gate")
    s_mm, nm_done, p_done, pn_done, pt_mm, pt_done, av_mm, o_done, wo_mm, x1_done, gu_mm, sig_done, m_done, dn_mm, delta_done, gate_done = (
        G.sem("ro_" + n) for n in names)
    b_in, ln_in, wo_in, wgu_in, wd_in, added = (G.sem("ro_" + n) for n in (
        "b_in", "ln_in", "wo_in", "wgu_in", "wd_in", "added"))
    den_in, rden, rden_out = (G.sem("ro_" + n) for n in ("den_in", "rden", "rden_out"))
    FQ, FK = NHQ * HDF, NHK * HDF
    QU, KU = FQ // BANK, FK // BANK
    HB = BANK // HDF
    NF = INTER // P
    scale = 1.0 / float(np.sqrt(HDF))
    with ExitStack() as stack:
        M = Memory(nc, stack, "ro_")
        WA = G.WA
        WB = M.sb("WB", [P, NHQ * D])
        wq, wk, wv = routed_qkv(G)
        wg = WA[:, 0:NC * INTER].rearrange("p (c n) -> p c n", c=NC)
        wu = WA[:, NC * INTER:2 * NC * INTER].rearrange("p (c n) -> p c n", c=NC)
        wb = WB[:, :].rearrange("p (h n) -> p h n", n=D)
        bias = M.sb("bias", [P, FQ + 2 * FK])
        oT = bias[:, :].rearrange("p (h n) -> p h n", h=NHQ)
        qT = M.sb("qT", [P, NHQ, SEL])
        kT, v = M.sb("kT", [P, NHK, SEL]), M.sb("v", [P, NS, FK])
        xs, x1 = M.sb("xs", [P, NS, D]), M.sb("x1", [P, NS, D])
        hn, hT = M.sb("hn", [P, NS, D]), M.sb("hT", [P, NC, SEL])
        cs = [M.sb("cos", [P, NS, HDF]), M.sb("sin", [P, NS, HDF])]
        ln = M.sb("ln", [P, 2, NC])
        ms, sd, rs = (M.sb(n, [P, NS]) for n in ("ms", "sd", "rs"))
        qb, t1, y = (M.sb(n, [P, 2, BANK]) for n in ("qb", "t1", "y"))
        nm, ssum, rsum = (M.sb(n, [P, 2, NS]) for n in ("nm", "ssum", "rsum"))
        pr, pt = M.sb("pr", [P, 2, 3 * P]), M.sb("pt", [P, 2, 3 * P])
        sig = M.sb("sig", [P, 2, SEL])
        gate, dn = M.sb("gate", [P, NS]), M.sb("dn", [P, H0 * T // P])
        block = stack.enter_context(nc.Block())

        units = [(wq, 0, u, m, qT) for u in range(QU) for m in range(NS)]
        units = [(wk, FQ, u, m, kT) for u in range(KU) for m in range(NS)] + units
        vunits = [(u, m) for u in range(KU) for m in range(NS)]

        @block.sync
        def _(sp):
            view = lambda name: I[name].rearrange("(c p) n -> p c n", p=P)
            sp.dma_start(ln[:, 0, :], I["ln1_w"]).then_inc(ln_in, 16)
            sp.dma_start(ln[:, 1, :], I["ln2_w"]).then_inc(ln_in, 16)
            for a, name, n in ((FQ, "bk", FK), (0, "bq", FQ), (FQ + FK, "bv", FK)):
                sp.dma_start(bias[:, a:a + n], I[name].partition_broadcast(P)).then_inc(b_in, 16)
            flat = lambda ap: ap.rearrange("h (a n) -> (h a) n", n=H0 * T // P)
            sp.dma_start(dn[:, :], flat(S.den)).then_inc(den_in, 16)
            sp.wait_ge(rden, 1)
            sp.dma_start(flat(S.rden), dn[:, :]).then_inc(rden_out, 16)
            sp.dma_start(wb, I["wo"].rearrange("(h p) n -> p h n", p=P)).then_inc(wo_in, 16)
            sp.wait_ge(qk_mm, len(units))
            sp.wait_ge(v_mm, len(vunits))
            sp.dma_start(wg, view("w_gate")).then_inc(wgu_in, 16)
            sp.dma_start(wu, view("w_up")).then_inc(wgu_in, 16)
            sp.wait_ge(wo_mm, NS)
            sp.dma_start(wb, I["w_down"].rearrange("(h p) n -> p h n", p=P)).then_inc(wd_in, 16)
            sp.wait_ge(rden_out, 16)

        @block.gpsimd
        def _(pool):
            for m in range(NS):
                where = bass.IndirectOffsetOnAxis(G.idx[:, m:m + 1], 0)
                pool.indirect_dma_start(xs[:, m, :], None, S.xn, where).then_inc(gath, 16)
            for m in range(NS):
                where = bass.IndirectOffsetOnAxis(G.idx[:, m:m + 1], 0)
                for n, name in enumerate(("cos128", "sin128")):
                    pool.indirect_dma_start(cs[n][:, m, :], None, I[name], where).then_inc(gath, 16)
            pool.wait_ge(gath, 16 * 3 * NS)
            for n, (w, off, u, m, dst) in enumerate(units):
                pool.wait_ge(qb_done, n + 1)
                wait(pool, y_done, n - 1)
                pool.tensor_tensor(t1[:, n % 2, :].rearrange("p (h d) -> p h d", d=HDF),
                                   qb[:, n % 2, :].rearrange("p (h d) -> p h d", d=HDF),
                                   cs[0][:, m, :].unsqueeze(1).to_broadcast([P, HB, HDF]), ALU.mult).then_inc(t1_done, 1)
            for m in range(NS):
                pool.wait_ge(delta_done, m + 1)
                where = bass.IndirectOffsetOnAxis(G.idx[:, m:m + 1], 0)
                pool.indirect_dma_start(S.r, where, hn[:, m, :], None, compute_op=ALU.add).then_inc(added, 16)
                pool.wait_ge(added, 16 * (m + 1))

        @block.tensor
        def _(pe):
            def normed(first):
                for m in range(NS):
                    pe.wait_ge(hn_done, first + m + 1)
                    for c in range(NC):
                        last = pe.transpose(G.ps[6 + m][:, c * P:(c + 1) * P], hn[:, m, c * P:(c + 1) * P], G.ident[:, :])
                    last.then_inc(hT_mm, 1)

            normed(0)
            pe.wait_ge(hT_done, NS)

            def transposes(n):
                pe.wait_ge(y_done, n + 1)
                wait(pe, yt_done, n - 1)
                for j in range(HB):
                    last = pe.transpose(G.ps[2 + n % 2][:, j * P:(j + 1) * P], y[:, n % 2, j * P:(j + 1) * P], G.ident[:, :])
                last.then_inc(yt_mm, 1)

            def values(n):
                u, m = vunits[n]
                wait(pe, v_done, n - 1)
                mm32(pe, G.ps[4 + n % 2], [(hT[:, c, m * P:(m + 1) * P], wv[:, c, u * BANK:(u + 1) * BANK])
                                           for c in range(NC)]).then_inc(v_mm, 1)

            for n, (w, off, u, m, dst) in enumerate(units):
                if n == 0:
                    pe.wait_ge(G.wqkv_in, 48)
                wait(pe, qb_done, n - 1)
                mm32(pe, G.ps[n % 2], [(hT[:, c, m * P:(m + 1) * P], w[:, c, u * BANK:(u + 1) * BANK])
                                       for c in range(NC)]).then_inc(qk_mm, 1)
                if n >= 1:
                    transposes(n - 1)
            for n in range(len(vunits)):
                values(n)
                if n == 0:
                    transposes(len(units) - 1)

            def scores(h):
                wait(pe, p_done, NS * (h - 1))
                bank = G.ps[h % 2]
                for m in range(NS):
                    out = bank[:, m * P:(2 * m + 1) * P]
                    pe.matmul(out, qT[:, h, m * P:(m + 1) * P], kT[:, h * NHK // NHQ, 0:(m + 1) * P],
                              start=m == 0, stop=False, skip_group_check=True)
                    last = pe.matmul(bank[:, 2 * m * P:(2 * m + 1) * P], G.identb[:, :], G.lower[:, :],
                                     start=False, stop=True, skip_group_check=True)
                last.then_inc(s_mm, 1)

            def spread(h):
                pe.wait_ge(pn_done, h + 1)
                wait(pe, pt_done, h - 1)
                for j in range(3):
                    last = pe.transpose(G.ps[2 + h % 2][:, j * P:(j + 1) * P], pr[:, h % 2, j * P:(j + 1) * P], G.ident[:, :])
                last.then_inc(pt_mm, 1)

            def attend(h):
                pe.wait_ge(pt_done, h + 1)
                wait(pe, o_done, h - 1)
                cols = slice((h * NHK // NHQ) * HDF, (h * NHK // NHQ + 1) * HDF)
                out = G.ps[4 + h % 2]
                pe.matmul(out[:, 0:2 * P], v[:, 0, cols], pt[:, h % 2, 0:2 * P], start=True, stop=False, skip_group_check=True)
                pe.matmul(out[:, P:2 * P], v[:, 1, cols], pt[:, h % 2, 2 * P:3 * P], start=False, stop=True,
                          skip_group_check=True).then_inc(av_mm, 1)

            pe.wait_ge(yt_done, len(units))
            pe.wait_ge(qb_done, len(units))
            pe.wait_ge(v_done, len(vunits))
            scores(0)
            for h in range(NHQ):
                if h + 1 < NHQ:
                    scores(h + 1)
                spread(h)
                if h >= 1:
                    attend(h - 1)
            attend(NHQ - 1)
            pe.wait_ge(wo_in, 16)
            pe.wait_ge(o_done, NHQ)
            for m in range(NS):
                mm32(pe, G.ps[m], [(oT[:, h, m * P:(m + 1) * P], wb[:, h, :]) for h in range(NHQ)]).then_inc(wo_mm, 1)
            normed(NS)
            pe.wait_ge(hT_done, 2 * NS)
            pe.wait_ge(wgu_in, 32)
            for f in range(NF):
                wait(pe, m_done, f - 1)
                for n, w in enumerate((wg, wu)):
                    last = mm32(pe, G.ps[2 + f % 2][:, n * SEL:(n + 1) * SEL],
                                [(w[:, c, f * P:(f + 1) * P], hT[:, c, :]) for c in range(NC)])
                last.then_inc(gu_mm, 1)
            pe.wait_ge(wd_in, 16)
            for m in range(NS):
                for f in range(NF):
                    pe.wait_ge(m_done, f + 1)
                    last = pe.matmul(G.ps[4 + m], qT[:, f, m * P:(m + 1) * P], wb[:, f, :], start=f == 0, stop=f == NF - 1)
                last.then_inc(dn_mm, 1)

        @block.scalar
        def _(act):
            def root(n):
                act.wait_ge(ms_done, n + 1)
                act.activation(sd[:, :], ms[:, :], ACT.Sqrt).then_inc(sd_done, 1)

            root(0)
            def rotated(n):
                w, off, u, m, dst = units[n]
                act.wait_ge(yt_mm, n + 1)
                act.activation(dst[:, u * HB:(u + 1) * HB, m * P:(m + 1) * P],
                               G.ps[2 + n % 2].rearrange("p (h n) -> p h n", h=HB), ACT.Copy).then_inc(yt_done, 1)

            for n in range(len(units)):
                rotated(n)

            def probabilities(h):
                for m in range(NS):
                    act.wait_ge(nm_done, NS * h + m + 1)
                    if m == 0:
                        wait(act, pt_mm, h - 1)
                    act.activation(pr[:, h % 2, m * P:(2 * m + 1) * P], G.ps[h % 2][:, m * P:(2 * m + 1) * P], ACT.Exp,
                                   bias=nm[:, h % 2, m:m + 1], scale=scale,
                                   accum_out=ssum[:, h % 2, m:m + 1]).then_inc(p_done, 1)

            def spread(h):
                act.wait_ge(pt_mm, h + 1)
                wait(act, av_mm, h - 1)
                act.activation(pt[:, h % 2, :], G.ps[2 + h % 2][:, 0:3 * P], ACT.Copy).then_inc(pt_done, 1)

            def output(h):
                act.wait_ge(av_mm, h + 1)
                act.activation(oT[:, h, :], G.ps[4 + h % 2][:, 0:SEL], ACT.Copy).then_inc(o_done, 1)

            probabilities(0)
            for h in range(NHQ):
                if h + 1 < NHQ:
                    probabilities(h + 1)
                spread(h)
                if h >= 1:
                    output(h - 1)
            output(NHQ - 1)
            root(1)
            act.activation(gate[:, :], G.selscore[:, :], ACT.Sigmoid).then_inc(gate_done, 1)
            for f in range(NF):
                act.wait_ge(gu_mm, f + 1)
                wait(act, m_done, f - 1)
                act.activation(sig[:, f % 2, :], G.ps[2 + f % 2][:, 0:SEL], ACT.Sigmoid).then_inc(sig_done, 1)

        @block.vector
        def _(dve):
            chain = Chain(dve, link)

            def norm(x, k):
                dve.tensor_tensor(hn[:, :, :], x, x, ALU.mult).then_inc(sq_done, 1)
                dve.wait_ge(sq_done, k + 1)
                chain.done(dve.reduce_sum(ms[:, :], hn[:, :, :], axis=AX))
                dve.tensor_scalar(ms[:, :], ms[:, :], 1.0 / D, RMS_EPS, ALU.mult, ALU.add).then_inc(ms_done, 1)
                dve.wait_ge(sd_done, k + 1)
                chain.done(dve.reciprocal(rs[:, :], sd[:, :]))
                for m in range(NS):
                    dve.tensor_scalar(hn[:, m, :], x[:, m, :], rs[:, m:m + 1], None, ALU.mult).then_inc(hn_done, 1)
                dve.wait_ge(ln_in, 32)
                for m in range(NS):
                    dve.wait_ge(hT_mm, k * NS + m + 1)
                    dve.tensor_tensor(hT[:, :, m * P:(m + 1) * P], G.ps[6 + m].rearrange("p (c n) -> p c n", c=NC),
                                      ln[:, k, :].unsqueeze(2).to_broadcast([P, NC, P]), ALU.mult).then_inc(hT_done, 1)

            dve.wait_ge(den_in, 16)
            dve.reciprocal(dn[:, :], dn[:, :]).then_inc(rden, 1)
            dve.wait_ge(gath, 16 * 3 * NS)
            norm(xs[:, :, :], 0)
            dve.wait_ge(b_in, 48)
            for n, (w, off, u, m, dst) in enumerate(units):
                dve.wait_ge(qk_mm, n + 1)
                wait(dve, t1_done, n - 1)
                a = off + u * BANK
                dve.tensor_tensor(qb[:, n % 2, :], G.ps[n % 2], bias[:, a:a + BANK], ALU.add).then_inc(qb_done, 1)
                dve.wait_ge(qb_done, n + 1)
                wait(dve, yt_mm, n - 1)
                q4 = qb[:, n % 2, :].rearrange("p (h d) -> p h d", d=HDF)
                y4 = y[:, n % 2, :].rearrange("p (h d) -> p h d", d=HDF)
                half = HDF // 2
                for k in range(2):
                    last = dve.tensor_tensor(y4[:, :, k * half:(k + 1) * half], q4[:, :, (1 - k) * half:(2 - k) * half],
                                             cs[1][:, m, k * half:(k + 1) * half].unsqueeze(1).to_broadcast([P, HB, half]),
                                             ALU.mult)
                chain.done(last)
                dve.wait_ge(t1_done, n + 1)
                dve.tensor_tensor(y[:, n % 2, :], y[:, n % 2, :], t1[:, n % 2, :], ALU.add).then_inc(y_done, 1)
            for n, (u, m) in enumerate(vunits):
                dve.wait_ge(v_mm, n + 1)
                dve.tensor_tensor(v[:, m, u * BANK:(u + 1) * BANK], G.ps[4 + n % 2],
                                  bias[:, FQ + FK + u * BANK:FQ + FK + (u + 1) * BANK], ALU.add).then_inc(v_done, 1)

            def maxima(h):
                dve.wait_ge(s_mm, h + 1)
                wait(dve, p_done, NS * (h - 1))
                for m in range(NS):
                    dve.tensor_reduce(nm[:, h % 2, m:m + 1], G.ps[h % 2][:, m * P:(2 * m + 1) * P], AX, ALU.max, negate=True
                                      ).then_inc(link, 1)
                    chain.n += 1
                dve.wait_ge(link, chain.n)
                dve.tensor_scalar(nm[:, h % 2, :], nm[:, h % 2, :], scale, None, ALU.mult).then_inc(nm_done, NS)

            def normalised(h):
                dve.wait_ge(p_done, NS * (h + 1))
                chain.done(dve.reciprocal(rsum[:, h % 2, :], ssum[:, h % 2, :]))
                for m in range(NS):
                    cols = slice(m * P, (2 * m + 1) * P)
                    last = dve.tensor_scalar(pr[:, h % 2, cols], pr[:, h % 2, cols], rsum[:, h % 2, m:m + 1], None, ALU.mult)
                last.then_inc(pn_done, 1)

            maxima(0)
            for h in range(NHQ):
                if h + 1 < NHQ:
                    maxima(h + 1)
                normalised(h)
            for m in range(NS):
                dve.wait_ge(wo_mm, m + 1)
                dve.tensor_tensor(x1[:, m, :], G.ps[m], xs[:, m, :], ALU.add).then_inc(x1_done, 1)
            dve.wait_ge(x1_done, NS)
            norm(x1[:, :, :], 1)
            for f in range(NF):
                dve.wait_ge(sig_done, f + 1)
                chain.done(dve.tensor_tensor(sig[:, f % 2, :], G.ps[2 + f % 2][:, 0:SEL], sig[:, f % 2, :], ALU.mult))
                dve.tensor_tensor(qT[:, f, :], G.ps[2 + f % 2][:, SEL:2 * SEL], sig[:, f % 2, :], ALU.mult).then_inc(m_done, 1)
            dve.wait_ge(gate_done, 1)
            dve.tensor_tensor(x1[:, :, :], x1[:, :, :], xs[:, :, :], ALU.subtract).then_inc(x1_done, 1)
            dve.wait_ge(x1_done, NS + 1)
            for m in range(NS):
                dve.wait_ge(dn_mm, m + 1)
                chain.done(dve.tensor_tensor(hn[:, m, :], G.ps[4 + m], x1[:, m, :], ALU.add))
                dve.tensor_scalar(hn[:, m, :], hn[:, m, :], gate[:, m:m + 1], None, ALU.mult).then_inc(delta_done, 1)


class Scratch:

    def __init__(self, nc):
        def dram(name, shape, dt=F32):
            return nc.dram_tensor(name, shape, dt, kind="Internal").ap()
        self.wscr = dram("gates_by_expert", [EXPERTS, T])
        self.xn = dram("layer1_xn", [T, D])
        self.r = dram("layer1_residual", [T, D])
        self.qk = dram("layer1_qk", [2, 2, D, T])
        self.v = dram("layer1_v", [H0 // 2, P, NT, 4 * HD])
        self.o = dram("layer1_o", [D, T])
        self.den = dram("layer1_sums", [H0, T])
        self.score = dram("layer1_scores", [T])
        self.rden = dram("layer1_inverse_sums", [H0, T])


class Globals:
    def __init__(self, nc, stack):
        self.nc, self.stack = nc, stack
        M = Memory(nc, stack)
        self.banks = stack.enter_context(nc.psum_tensor("banks", [P, 8, BANK], F32))
        self.ps = [self.banks[:, i, :] for i in range(8)]
        self.ident, self.identb = M.sb("ident", [P, P]), M.sb("identb", [P, P], BF16)
        self.identr = M.sb("identr", [P, P], F32R)
        self.upper, self.lower = M.sb("upper", [P, P], BF16), M.sb("lower", [P, P], BF16)
        self.strict, self.headmask = M.sb("strict", [P, P]), M.sb("headmask", [P, P])
        self.ones = M.sb("ones", [P, P])
        self.kvb, self.ksb = M.sb("kvb", [P, NC, P]), M.sb("ksb", [P, NC, H0])
        self.pair = M.sb("pair", [P, NT, 2])
        self.idx, self.selscore = M.sb("idx", [P, NS], U32), M.sb("selscore", [P, NS])
        self.headsel = M.sb("headsel", [P, NC, P], F32R)

        self.sems = []

    def sem(self, name):
        self.sems.append(self.nc.alloc_semaphore(name=name))
        return self.sems[-1]

    def give_back_semaphores(self):
        self.nc.clear_and_free_semaphores(self.sems)
        self.nc.all_engine_barrier()
        self.sems = []


STOP = None


def program(nc, I, out):
    S = Scratch(nc)
    with ExitStack() as stack:
        G = Globals(nc, stack)
        stage_constants(nc, G)
        with ExitStack() as features:
            M = Memory(nc, features)
            G.xTh, G.xTl = M.sb("xTh", [P, NC, T], F32R), M.sb("xTl", [P, NC, T], F32R)
            with ExitStack() as tokens:
                G.X = Memory(nc, tokens).sb("X", [P, NT, D])
                stage_normalize(nc, G, "a_", I["x"], None, None)
                stage_kv(nc, G, I, S)
                if STOP == "kv":
                    return
                with ExitStack() as inner:
                    M0 = Memory(nc, inner)
                    G.acch, G.accl = M0.sb("acch", [P, T], F32R), M0.sb("accl", [P, T], F32R)
                    stage_experts(nc, G, I, S)
                    if STOP == "ex":
                        return
                    stage_attend0(nc, G, I)
                    if STOP == "at":
                        return
                    stage_output0(nc, G, I)
                    if STOP == "o0":
                        return
                G.give_back_semaphores()
                stage_normalize(nc, G, "b_", None, S.xn, S.r, I["w_router"], S.score)
            stage_qkv(nc, G, I, S)
            if STOP == "qkv":
                return
        G.give_back_semaphores()
        with ExitStack() as routed:
            G.WA = Memory(nc, routed).sb("WA", [P, NC * (NHQ + 2 * NHK) * HDF])
            G.wqkv_in = G.sem("wqkv_in")
            stage_attend1(nc, G, I, S)
            if STOP == "l1":
                return
            stage_routed(nc, G, I, S)
            if STOP == "ro":
                return
        stage_output1(nc, G, I, S, out)


def halves(g):
    return np.stack([g, np.roll(g, g.shape[0] // 2)])


def rotary(width):
    inv = np.float32(1.0) / np.float32(10000.0) ** (np.arange(0, width, 2, dtype=np.float32) / np.float32(width))
    ang = np.arange(T, dtype=np.float32)[:, None] * inv[None, :].astype(np.float32)
    return np.concatenate([np.cos(ang), np.cos(ang)], 1), np.concatenate([-np.sin(ang), np.sin(ang)], 1)


def constants():
    c32, s32 = rotary(HD)
    c128, s128 = rotary(HDF)
    return {"cos32": c32, "sin32": s32, "cos128": c128, "sin128": s128}


LAYOUT = {
    "x": lambda a: a["L0_attn_hidden_states"][0],
    "qT": lambda a: a["L0_attn_q_w"].T,
    "kT": lambda a: a["L0_attn_k_w"].T,
    "vT": lambda a: a["L0_attn_v_w"].T,
    "oT": lambda a: a["L0_attn_o_w"].T,
    "q_b": lambda a: a["L0_attn_q_b"].reshape(NC, P).T,
    "k_b": lambda a: a["L0_attn_k_b"],
    "v_b": lambda a: a["L0_attn_v_b"],
    "o_b": lambda a: a["L0_attn_o_b"],
    "wgT": lambda a: a["L0_ffn_Wg"].T,
    "biases": lambda a: a["L0_ffn_biases"],
    "wdT": lambda a: a["L0_ffn_Wdown"].T,
    "wupT": lambda a: a["L0_ffn_Wup"].T,
    "sw1T": lambda a: a["L0_ffn_sw1"].T,
    "swgT": lambda a: a["L0_ffn_swg"].T,
    "sw2T": lambda a: a["L0_ffn_sw2"].T,
    "w_qkv": lambda a: a["L1_attn_w_qkv"],
    "w_out": lambda a: a["L1_attn_w_out"],
    "q_gamma": lambda a: halves(a["L1_attn_q_gamma"]),
    "k_gamma": lambda a: halves(a["L1_attn_k_gamma"]),
    "w_router": lambda a: a["L1_ffn_w_router"].reshape(NC, P).T,
    "ln1_w": lambda a: a["L1_ffn_ln1_w"].reshape(NC, P).T,
    "ln2_w": lambda a: a["L1_ffn_ln2_w"].reshape(NC, P).T,
    **{n: (lambda a, n=n: a["L1_ffn_" + n])
       for n in ("wq", "bq", "wk", "bk", "wv", "bv", "wo", "w_gate", "w_up", "w_down")},
    "ew": lambda a: np.concatenate([a["L0_ffn_rw1"].transpose(0, 2, 1), a["L0_ffn_rwg"].transpose(0, 2, 1),
                                    a["L0_ffn_rw2"].transpose(0, 2, 1)[:, :P], a["L0_ffn_rw2"].transpose(0, 2, 1)[:, P:]],
                                   axis=2),
}


def kernel(**inputs):
    import concourse.bacc as bacc
    from concourse.bass_utils import run_bass_kernel_spmd

    arrays = {name: np.ascontiguousarray(view(inputs)) for name, view in LAYOUT.items()}
    arrays.update(constants())
    nc = bacc.Bacc("TRN2", target_bir_lowering=False, num_devices=1)
    dram = {name: nc.dram_tensor(name + "_in", a.shape, mybir.dt.from_np(a.dtype), kind="ExternalInput").ap()
            for name, a in arrays.items()}
    out = nc.dram_tensor("out", [T, D], F32, kind="ExternalOutput").ap()
    program(nc, dram, out)
    nc.finalize()
    res = run_bass_kernel_spmd(nc, [{name + "_in": a for name, a in arrays.items()}], core_ids=[0])
    return res.results[0]["out"].reshape(1, T, D)
```

```python
from contextlib import ExitStack

import numpy as np

import concourse.bass as bass
from concourse import mybir

P = 128
F32 = mybir.dt.float32
F32R = mybir.dt.float32r
BF16 = mybir.dt.bfloat16
U32 = mybir.dt.uint32
I32 = mybir.dt.int32
ALU = mybir.AluOpType
ACT = mybir.ActivationFunctionType
AX = mybir.AxisListType.X

T = 2048
D = 512
NT = T // P
NC = D // P
TB = 512
NB = T // TB
BT = TB // P
BANK = 512
LN_EPS = 1e-5
RMS_EPS = 1e-6
NEG = -1e30

H0, HD = 16, 32
EXPERTS, TOPK, LAT, HID = 16, 8, 128, 256
ROUTE_SCALE = 2.5
WINDOW = 1024

SEL = T // 8
NS = SEL // P
NHQ, NHK, HDF = 16, 8, 128
INTER = 2048


def raw(ap):
    return ap.bitcast(F32)


class Chain:

    def __init__(self, eng, sem):
        self.eng, self.sem, self.n = eng, sem, 0

    def done(self, ins):
        self.n += 1
        ins.then_inc(self.sem, 1)
        self.eng.wait_ge(self.sem, self.n)


def mm3(pe, out, parts, start=True, stop=True, **kw):
    last = None
    for n, ((ah, al), (bh, bl)) in enumerate(parts):
        end = n == len(parts) - 1
        pe.matmul(out, ah, bh, start=start and n == 0, stop=False, **kw)
        pe.matmul(out, ah, bl, start=False, stop=False, **kw)
        last = pe.matmul(out, al, bh, start=False, stop=stop and end, **kw)
    return last


def mm32(pe, out, parts, start=True, stop=True, **kw):
    last = None
    for n, (a, b) in enumerate(parts):
        last = pe.matmul(out, a, b, start=start and n == 0, stop=stop and n == len(parts) - 1, **kw)
    return last


class Memory:

    def __init__(self, nc, stack, tag=""):
        self.nc, self.stack, self.tag = nc, stack, tag

    def sb(self, name, shape, dt=F32):
        return self.stack.enter_context(self.nc.sbuf_tensor(self.tag + name, shape, dt))


class Shared:
    pass


def stage_constants(nc, G):
    zeroed, made, blocks = G.sem("const_zeroed"), G.sem("const_made"), G.sem("const_blocks")
    with nc.sbuf_tensor("headsel32", [P, NC, P], F32) as headsel, nc.Block() as block:

        @block.gpsimd
        def _(pool):
            pool.memset(G.ident[:, :], 0.0)
            pool.memset(headsel[:, :, :], 0.0)
            pool.memset(G.upper[:, :], 0.0)
            pool.memset(G.strict[:, :], 1.0)
            pool.memset(G.lower[:, :], 0.0).then_inc(zeroed, 1)
            pool.wait_ge(zeroed, 1)
            pool.affine_select(out=G.ident[:, :], in_=G.ident[:, :], compare_op=ALU.not_equal, fill=1.0,
                               base=0, pattern=[[-1, P]], channel_multiplier=1).then_inc(made, 1)
            pool.affine_select(out=G.upper[:, :], in_=G.upper[:, :], compare_op=ALU.is_ge, fill=NEG,
                               base=0, pattern=[[1, P]], channel_multiplier=-1).then_inc(made, 1)
            pool.affine_select(out=G.lower[:, :], in_=G.lower[:, :], compare_op=ALU.is_ge, fill=NEG,
                               base=0, pattern=[[-1, P]], channel_multiplier=1).then_inc(made, 1)
            hs = headsel[:, :, :].rearrange("p g (j d) -> p g j d", d=HD)
            pool.affine_select(out=hs, in_=hs, compare_op=ALU.not_equal, fill=1.0, base=0,
                               pattern=[[P // HD, NC], [1, P // HD], [0, HD]], channel_multiplier=-1).then_inc(made, 1)
            pool.affine_select(out=G.strict[:, :], in_=G.strict[:, :], compare_op=ALU.is_gt, fill=0.0,
                               base=0, pattern=[[1, P]], channel_multiplier=-1).then_inc(made, 1)

        @block.vector
        def _(dve):
            dve.memset(G.headmask[:, :], 0.0).then_inc(blocks, 1)
            dve.memset(G.ones[:, :], 1.0)
            dve.memset(G.ksb[:, :, :], 0.0)
            dve.wait_ge(blocks, 1)
            for j in range(P // HD):
                dve.memset(G.headmask[j * HD:(j + 1) * HD, j * HD:(j + 1) * HD], 1.0)
            dve.wait_ge(made, 5)
            dve.tensor_copy(G.headsel[:, :, :], headsel[:, :, :])
            dve.tensor_copy(G.identb[:, :], G.ident[:, :])
            dve.tensor_copy(G.identr[:, :], G.ident[:, :]).then_inc(blocks, 1)
            dve.wait_ge(blocks, 2)


def stage_normalize(nc, G, tag, x_dram, xn_dram, r_dram, router=None, score_dram=None, weights=None):
    wr_in, wrh_done, wr_done, sc_mm, row_sb, pair_mm, pair_sb = (G.sem(tag + n) for n in (
        "wr_in", "wrh", "wr", "sc_mm", "row_sb", "pair_mm", "pair_sb"))
    x_in = [G.sem(f"{tag}x_in{g}") for g in range(NB)]
    var_ready, sd_ready, rstd_ready = (G.sem(tag + n) for n in ("var_ready", "sd_ready", "rstd_ready"))
    xn_ready, xt_ready = G.sem(tag + "xn_ready"), G.sem(tag + "xt_ready")
    hi_ready, lo_ready, link = G.sem(tag + "hi_ready"), G.sem(tag + "lo_ready"), G.sem(tag + "ln_link")
    RING = 4
    res_ready, r_stored = G.sem(tag + "res_ready"), G.sem(tag + "r_stored")
    xn_stored = [G.sem(f"{tag}xn_stored{n}") for n in range(RING)]
    X, xTh, xTl = G.X, G.xTh, G.xTl
    with ExitStack() as stack:
        M = Memory(nc, stack, tag)
        stats, mv = M.sb("stats", [P, NT, 6]), M.sb("mv", [P, NT, 2])
        ve, sd, rstd, shift = (M.sb(n, [P, NT]) for n in ("ve", "sd", "rstd", "shift"))
        xn = M.sb("xn", [P, RING, D])
        wr, wrh, wrl = M.sb("wr", [P, NC]), M.sb("wrh", [P, NC, 2], F32R), M.sb("wrl", [P, NC, 2], F32R)
        row = M.sb("row", [2, T])
        block = stack.enter_context(nc.Block())

        @block.sync
        def _(sp):
            if x_dram is not None:
                for g in range(NB):
                    sp.dma_start(X[:, g * BT:(g + 1) * BT, :],
                                 x_dram.rearrange("(t p) d -> p t d", p=P)[:, g * BT:(g + 1) * BT, :]
                                 ).then_inc(x_in[g], 16)
            if weights:
                weights.load(sp)
            if xn_dram is not None:
                sp.dma_start(wr[:, :], router).then_inc(wr_in, 16)
                for t in range(NT):
                    sp.wait_ge(xn_ready, t + 1)
                    sp.dma_start(xn_dram[t * P:(t + 1) * P, :], xn[:, t % RING, :]).then_inc(xn_stored[t % RING], 16)
                    sp.wait_ge(res_ready, t + 1)
                    sp.dma_start(r_dram[t * P:(t + 1) * P, :], X[:, t, :]).then_inc(r_stored, 16)
                sp.wait_ge(row_sb, NB)
                sp.dma_start(score_dram.unsqueeze(0), row[0:1, :]).then_inc(r_stored, 16)
                sp.wait_ge(r_stored, (NT + 1) * 16)
                for n in range(RING):
                    sp.wait_ge(xn_stored[n], 16 * NT // RING)

        @block.vector
        def _(dve):
            chain = Chain(dve, link)
            if xn_dram is not None:
                dve.wait_ge(wr_in, 16)
                for n in range(2):
                    last = dve.tensor_copy(wrh[:, :, n:n + 1], wr[:, :].unsqueeze(2))
                last.then_inc(wrh_done, 1)
                dve.wait_ge(wrh_done, 1)
                for n in range(2):
                    last = dve.tensor_tensor(wrl[:, :, n:n + 1], wr[:, :].unsqueeze(2), raw(wrh[:, :, n:n + 1]),
                                             ALU.subtract)
                last.then_inc(wr_done, 1)

            def statistics(g):
                cols = slice(g * BT, (g + 1) * BT)
                if x_dram is not None:
                    dve.wait_ge(x_in[g], 16)
                for t in range(g * BT, (g + 1) * BT):
                    last = dve.bn_stats(stats[:, t, :], X[:, t, :])
                chain.done(last)
                for t in range(g * BT, (g + 1) * BT):
                    last = dve.bn_aggr(mv[:, t, :], stats[:, t, :])
                chain.done(last)
                dve.tensor_scalar_add(ve[:, cols], mv[:, cols, 1], LN_EPS).then_inc(var_ready, 1)

            def low(t):
                dve.wait_ge(hi_ready, t + 1)
                cols = slice(t * P, (t + 1) * P)
                dve.tensor_tensor(xTl[:, :, cols], G.ps[t % RING][:, :].rearrange("p (c n) -> p c n", c=NC),
                                  raw(xTh[:, :, cols]), ALU.subtract).then_inc(lo_ready, 1)

            def scales(g):
                cols = slice(g * BT, (g + 1) * BT)
                dve.wait_ge(sd_ready, g + 1)
                chain.done(dve.reciprocal(rstd[:, cols], sd[:, cols]))
                dve.scalar_tensor_tensor(shift[:, cols], mv[:, cols, 0], -1.0, rstd[:, cols], ALU.mult, ALU.mult
                                         ).then_inc(rstd_ready, 1)

            statistics(0)
            scales(0)
            for g in range(NB):
                if g + 1 < NB:
                    statistics(g + 1)
                for t in range(g * BT, (g + 1) * BT):
                    if t % BT == BT - 1 and g + 1 < NB:
                        scales(g + 1)
                    low(t)
            if xn_dram is not None:
                dve.wait_ge(pair_mm, 1)
                dve.tensor_copy(G.score[:, :], G.ps[RING + 2][:, 0:2 * NT].rearrange("p (t n) -> p t n", n=2)[:, :, 0]
                                ).then_inc(pair_sb, 1)
                dve.wait_ge(pair_sb, 1)
            if weights:
                weights.low(dve)

        if xn_dram is not None:
            @block.gpsimd
            def _(pool):
                for t in range(NT):
                    pool.wait_ge(xn_ready, t + 1)
                    pool.tensor_tensor(X[:, t, :], X[:, t, :], xn[:, t % RING, :], ALU.add).then_inc(res_ready, 1)

        @block.tensor
        def _(pe):
            def scores(b):
                pe.wait_ge(wr_done, 1)
                pe.wait_ge(lo_ready, (b + 1) * BT)
                if b >= 2:
                    pe.wait_ge(row_sb, b - 1)
                cols = slice(b * TB, (b + 1) * TB)
                mm3(pe, G.ps[RING + b % 2][0:2, :], [((wrh[:, c, :], wrl[:, c, :]), (xTh[:, c, cols], xTl[:, c, cols]))
                                                     for c in range(NC)]).then_inc(sc_mm, 1)

            for t in range(NT):
                pe.wait_ge(xn_ready, t + 1)
                if t >= RING:
                    pe.wait_ge(lo_ready, t - RING + 1)
                for c in range(NC):
                    last = pe.transpose(G.ps[t % RING][:, c * P:(c + 1) * P],
                                        xn[:, t % RING, c * P:(c + 1) * P], G.ident[:, :])
                last.then_inc(xt_ready, 1)
                if xn_dram is not None and t % BT == BT - 1:
                    scores(t // BT)
            if xn_dram is not None:
                for t in range(NT):
                    pe.wait_ge(row_sb, t // BT + 1)
                    last = pe.transpose(G.ps[RING + 2][:, 2 * t:2 * t + 2], row[:, t * P:(t + 1) * P], G.ident[0:2, 0:2])
                last.then_inc(pair_mm, 1)

        @block.scalar
        def _(act):
            def score_row(b):
                act.wait_ge(sc_mm, b + 1)
                act.activation(row[:, b * TB:(b + 1) * TB], G.ps[RING + b % 2][0:2, :], ACT.Copy).then_inc(row_sb, 1)

            def root(g):
                act.wait_ge(var_ready, g + 1)
                act.activation(sd[:, g * BT:(g + 1) * BT], ve[:, g * BT:(g + 1) * BT], ACT.Sqrt).then_inc(sd_ready, 1)

            def normal(t):
                if t % BT == 0:
                    act.wait_ge(rstd_ready, t // BT + 1)
                if t >= RING:
                    act.wait_ge(xt_ready, t - RING + 1)
                    if xn_dram is not None:
                        act.wait_ge(xn_stored[t % RING], 16 * (t // RING))
                        act.wait_ge(res_ready, t - RING + 1)
                act.activation(xn[:, t % RING, :], X[:, t, :], ACT.Identity, bias=shift[:, t:t + 1],
                               scale=rstd[:, t:t + 1]).then_inc(xn_ready, 1)

            def high(t):
                act.wait_ge(xt_ready, t + 1)
                act.activation(xTh[:, :, t * P:(t + 1) * P], G.ps[t % RING][:, :].rearrange("p (c n) -> p c n", c=NC),
                               ACT.Copy).then_inc(hi_ready, 1)

            root(0)
            for t in range(NT):
                normal(t)
                if t % BT == BT - 1 and t + 1 < NT:
                    root(t // BT + 1)
                if t >= 1:
                    high(t - 1)
                if xn_dram is not None and t % BT == 2 and t > BT:
                    score_row(t // BT - 1)
            high(NT - 1)
            if xn_dram is not None:
                score_row(NB - 1)
            if weights:
                weights.high(act)


class SplitWeights:

    def __init__(self, G, M, tag, jobs, cols=1024):
        self.w_in = [G.sem(f"{tag}w_in{n}") for n in range(2)]
        self.w_hi, self.w_lo = G.sem(tag + "w_hi"), G.sem(tag + "w_lo")
        self.pieces, self.upto = [], []
        for hi, lo, src in jobs:
            chunks, n = src.shape[1], src.shape[2]
            step = max(1, min(chunks, cols // n))
            for c in range(0, chunks, step):
                part = slice(c * n, (c + step) * n)
                self.pieces.append((hi[:, part], lo[:, part], src[:, c:c + step, :]))
            self.upto.append(len(self.pieces))
        self.stage = M.sb(tag + "stage", [P, 2, max(p[0].shape[1] for p in self.pieces)])

    def at(self, n):
        return self.stage[:, n % 2, 0:self.pieces[n][0].shape[1]]

    def load(self, queue):
        for n, (hi, lo, src) in enumerate(self.pieces):
            if n >= 2:
                queue.wait_ge(self.w_lo, n - 1)
            queue.dma_start(self.at(n).rearrange("p (c n) -> p c n", c=src.shape[1]), src
                            ).then_inc(self.w_in[n % 2], 16)

    def high(self, act):
        for n, (hi, lo, src) in enumerate(self.pieces):
            act.wait_ge(self.w_in[n % 2], 16 * (n // 2 + 1))
            act.activation(hi, self.at(n), ACT.Copy).then_inc(self.w_hi, 1)

    def low(self, dve):
        for n, (hi, lo, src) in enumerate(self.pieces):
            dve.wait_ge(self.w_hi, n + 1)
            dve.tensor_tensor(lo, self.at(n), raw(hi), ALU.subtract).then_inc(self.w_lo, 1)

    def ready(self, pe, job):
        pe.wait_ge(self.w_lo, self.upto[job])


def stage_kv(nc, G, I, S):
    logit_ready, p1 = G.sem("kv_logit"), G.sem("kv_exp")
    k_mm, v_mm, kx_ready, e_ready, r_ready = (G.sem("kv_" + n) for n in ("k_mm", "v_mm", "kx", "e", "r"))
    kp_ready, v_ready, kv_done, link = (G.sem("kv_" + n) for n in ("kp", "v", "done", "link"))
    bias_in, gate_done, wt_mm, wt_sb, wt_out, sums = (G.sem("kv_" + n) for n in
                                                   ("bias", "gate", "wtmm", "wtsb", "wtout", "sums"))
    n_ready, ez_mm = G.sem("kv_n"), G.sem("kv_ez")
    pss, xTh, xTl = G.ps, G.xTh, G.xTl
    with ExitStack() as stack:
        M = Memory(nc, stack, "kv_")
        kbb, vbb, gb = M.sb("kbb", [P, D]), M.sb("vbb", [P, D]), M.sb("gb", [P, EXPERTS])
        kx, ke, kr = M.sb("kx", [P, 2, D]), M.sb("ke", [P, 2, D]), M.sb("kr", [P, 2, D])
        kp, vv = M.sb("kp", [P, 2, D]), M.sb("vv", [P, 2, D])
        gz, gp = M.sb("gz", [P, NT, EXPERTS]), M.sb("gp", [P, NT, EXPERTS])
        gbias, grep = M.sb("gbias", [P, NT, EXPERTS]), M.sb("grep", [P, NT, EXPERTS])
        top = M.sb("top", [P, NT, 8])
        gw, gsum, ginv = M.sb("gw", [P, NT, EXPERTS]), M.sb("gsum", [P, NT]), M.sb("ginv", [P, NT])
        eT, wT = M.sb("eT", [EXPERTS, T]), M.sb("wT", [EXPERTS, T])
        def w(n, c):
            h, l = G.kvw[n]
            k = h.shape[1] // NC
            return h[:, c * k:(c + 1) * k], l[:, c * k:(c + 1) * k]

        def x(t, c):
            cols = slice(t * P, (t + 1) * P)
            return xTh[:, c, cols], xTl[:, c, cols]

        block = stack.enter_context(nc.Block())

        @block.sync
        def _(sp):
            sp.dma_start(kbb[:, :], I["k_b"].partition_broadcast(P)).then_inc(bias_in, 16)
            sp.dma_start(vbb[:, :], I["v_b"].partition_broadcast(P)).then_inc(bias_in, 16)
            sp.dma_start(gb[:, :], I["biases"].partition_broadcast(P)).then_inc(bias_in, 16)
            sp.wait_ge(wt_sb, 4)
            sp.dma_start(S.wscr, wT[:, :]).then_inc(wt_out, 16)
            sp.wait_ge(wt_out, 16)

        @block.tensor
        def _(pe):
            for b in range(NB):
                cols = slice(b * TB, (b + 1) * TB)
                mm3(pe, pss[b][0:EXPERTS, :], [(w("g", c), (xTh[:, c, cols], xTl[:, c, cols])) for c in range(NC)]
                    ).then_inc(logit_ready, 1)

            def sums_of(t):
                pe.wait_ge(kp_ready, t + 1)
                pe.wait_ge(v_ready, t + 1)
                for g in range(NC):
                    first = t == 0 and g == 0
                    pe.matmul(pss[4][:, g * P:(g + 1) * P], kp[:, t % 2, g * P:(g + 1) * P],
                              vv[:, t % 2, g * P:(g + 1) * P], start=first, stop=t == NT - 1,
                              skip_group_check=True)
                    last = pe.matmul(pss[5][:, 2 * g:2 * g + 2], kp[:, t % 2, g * P:(g + 1) * P],
                                     G.ones[:, 0:2], start=first, stop=t == NT - 1, skip_group_check=True)
                last.then_inc(kv_done, 1)

            for t in range(NT):
                if t < 2:
                    pe.wait_ge(p1, NB)
                else:
                    pe.wait_ge(kx_ready, t - 1)
                mm3(pe, pss[t % 2][:, :], [(x(t, c), w("k", c)) for c in range(NC)]).then_inc(k_mm, 1)
                if t >= 2:
                    pe.wait_ge(v_ready, t - 1)
                mm3(pe, pss[2 + t % 2][:, :], [(x(t, c), w("v", c)) for c in range(NC)]).then_inc(v_mm, 1)
                if t == 0:
                    for n in range(NT):
                        last = pe.transpose(pss[6][:, n * EXPERTS:(n + 1) * EXPERTS], eT[:, n * P:(n + 1) * P],
                                            G.ident[0:EXPERTS, 0:EXPERTS])
                    last.then_inc(ez_mm, 1)
                if t >= 1:
                    sums_of(t - 1)
            sums_of(NT - 1)
            pe.wait_ge(gate_done, 1)
            pe.wait_ge(kx_ready, NT)
            pe.wait_ge(v_ready, NT)
            for t in range(NT):
                last = pe.transpose(pss[t // BT][0:EXPERTS, (t % BT) * P:(t % BT + 1) * P], gw[:, t, :],
                                    G.ident[:, :])
                if t % BT == BT - 1:
                    last.then_inc(wt_mm, 1)

        @block.scalar
        def _(act):
            for b in range(NB):
                act.wait_ge(logit_ready, b + 1)
                act.activation(eT[:, b * TB:(b + 1) * TB], pss[b][0:EXPERTS, :], ACT.Exp, scale=-1.0).then_inc(p1, 1)
            for t in range(NT):
                act.wait_ge(kx_ready, t + 1)
                if t >= 2:
                    act.wait_ge(kp_ready, t - 1)
                act.activation(ke[:, t % 2, :], kx[:, t % 2, :], ACT.Relu, scale=-1.0).then_inc(n_ready, 1)
                act.wait_ge(n_ready, t + 1)
                act.activation(ke[:, t % 2, :], ke[:, t % 2, :], ACT.Exp, scale=-1.0).then_inc(e_ready, 1)
                act.activation(kr[:, t % 2, :], kx[:, t % 2, :], ACT.Relu).then_inc(r_ready, 1)
            for g in range(NB):
                act.wait_ge(wt_mm, g + 1)
                act.activation(wT[:, g * TB:(g + 1) * TB], pss[g][0:EXPERTS, :], ACT.Copy).then_inc(wt_sb, 1)

        @block.vector
        def _(dve):
            chain = Chain(dve, link)
            dve.wait_ge(bias_in, 48)

            def gates():
                dve.wait_ge(ez_mm, 1)
                chain.done(dve.tensor_scalar_add(gz[:, :, :], pss[6][:, 0:NT * EXPERTS].rearrange(
                    "p (t e) -> p t e", t=NT), 1.0))
                chain.done(dve.reciprocal(gp[:, :, :], gz[:, :, :]))
                chain.done(dve.tensor_tensor(gbias[:, :, :], gp[:, :, :],
                                             gb[:, :].unsqueeze(1).to_broadcast([P, NT, EXPERTS]), ALU.add))
                for t in range(NT):
                    last = dve.max(top[:, t, :], gbias[:, t, :])
                chain.done(last)
                for t in range(NT):
                    last = dve.match_replace(grep[:, t, :], top[:, t, :], gbias[:, t, :], NEG)
                chain.done(last)
                chain.done(dve.tensor_tensor(grep[:, :, :], grep[:, :, :], gbias[:, :, :], ALU.not_equal))
                chain.done(dve.tensor_tensor(gw[:, :, :], gp[:, :, :], grep[:, :, :], ALU.mult))
                chain.done(dve.reduce_sum(gsum[:, :], gw[:, :, :], axis=AX))
                chain.done(dve.reciprocal(ginv[:, :], gsum[:, :]))
                chain.done(dve.tensor_scalar(ginv[:, :], ginv[:, :], ROUTE_SCALE, None, ALU.mult))
                dve.tensor_tensor(gw[:, :, :], gw[:, :, :], ginv[:, :].unsqueeze(2).to_broadcast([P, NT, EXPERTS]),
                                  ALU.mult).then_inc(gate_done, 1)

            for t in range(NT):
                dve.wait_ge(k_mm, t + 1)
                if t >= 2:
                    dve.wait_ge(r_ready, t - 1)
                dve.tensor_tensor(kx[:, t % 2, :], pss[t % 2][:, :], kbb[:, :], ALU.add).then_inc(kx_ready, 1)
                dve.wait_ge(v_mm, t + 1)
                if t >= 2:
                    dve.wait_ge(kv_done, t - 1)
                dve.tensor_tensor(vv[:, t % 2, :], pss[2 + t % 2][:, :], vbb[:, :], ALU.add).then_inc(v_ready, 1)
                dve.wait_ge(e_ready, t + 1)
                dve.wait_ge(r_ready, t + 1)
                dve.tensor_tensor(kp[:, t % 2, :], ke[:, t % 2, :], kr[:, t % 2, :], ALU.add).then_inc(kp_ready, 1)
                if t == 2:
                    gates()
            dve.wait_ge(kv_done, NT)
            for g in range(NC):
                dve.tensor_tensor(G.kvb[:, g, :], pss[4][:, g * P:(g + 1) * P], G.headmask[:, :], ALU.mult)
            for g in range(NC):
                for j in range(P // HD):
                    rows = slice(j * HD, (j + 1) * HD)
                    h = g * (P // HD) + j
                    last = dve.tensor_copy(G.ksb[rows, g, h:h + 1], pss[5][rows, 2 * g:2 * g + 1])
            last.then_inc(sums, 1)
            dve.wait_ge(sums, 1)


def wait(eng, sem, value):
    if not isinstance(value, int) or value > 0:
        eng.wait_ge(sem, value)


def looped(eng, iterations, body):
    body(0, True, False)
    with eng.Fori(1, iterations - 1) as i:
        body(i, False, False)
    body(iterations - 1, False, True)


def stage_experts(nc, G, I, S):
    xl_mm, xl_hi, xl_lo = (G.sem("ex_" + n) for n in ("xl_mm", "xl_hi", "xl_lo"))
    w_in, wb_in = ([G.sem(f"ex_{n}{k}") for k in range(2)] for n in ("w_in", "wb_in"))
    w_hi, w_lo, g_mm, u_mm, r_done, rw_done = (G.sem("ex_" + n) for n in
                                              ("w_hi", "w_lo", "g_mm", "u_mm", "relu", "rw"))
    t_done, h_done, hh_done, hl_done, down_done = (G.sem("ex_" + n) for n in ("t", "h", "hh", "hl", "down"))
    acc_hi, acc_lo = G.sem("ex_acc_hi"), G.sem("ex_acc_lo")
    U = 2 * NB
    W = 2 * HID + 2 * LAT
    RING = 4
    LATE = 3
    with ExitStack() as stack:
        M = Memory(nc, stack, "ex_")
        xlh, xll = M.sb("xlh", [P, T], F32R), M.sb("xll", [P, T], F32R)
        wdh, wdl = M.sb("wdh", [P, NC * LAT], F32R), M.sb("wdl", [P, NC * LAT], F32R)
        weights = SplitWeights(G, M, "exw_", [(wdh[:, :], wdl[:, :], I["wdT"].rearrange("(c p) n -> p c n", p=P))])
        ws = M.sb("ws", [P, 2, W])
        wh, wl = M.sb("wh", [P, 2, W], F32R), M.sb("wl", [P, 2, W], F32R)
        wb = M.sb("wb", [P, 2, T])
        r, rw, tt, h = (M.sb(n, [P, 2, TB]) for n in ("r", "rw", "t", "h"))
        hh, hl = M.sb("hh", [P, RING, TB], F32R), M.sb("hl", [P, RING, TB], F32R)
        block = stack.enter_context(nc.Block())
        acc = [G.ps[b] for b in range(NB)]
        gate = [G.ps[NB + k] for k in range(2)]
        up = [G.ps[NB + 2 + k] for k in range(2)]

        def where(k):
            return k // U, (k % U) // 2, k % 2

        @block.sync
        def _(sp):
            weights.load(sp)
            def load(e, par, early):
                if not early:
                    sp.wait_ge(w_lo, e - 1)
                sp.dma_start(ws[:, par, :], I["ew"][bass.ds(e, 1), :, :].rearrange("a p n -> (a p) n")
                             ).then_inc(w_in[par], 16)
                if not early:
                    sp.wait_ge(rw_done, (e - 1) * U)
                sp.dma_start(wb[:, par, :], S.wscr[bass.ds(e, 1), :].rearrange("a n -> (a n)").partition_broadcast(P)
                             ).then_inc(wb_in[par], 16)

            load(0, 0, True)
            load(1, 1, True)
            with sp.Fori(1, EXPERTS // 2) as i:
                for par in range(2):
                    load(i * 2 + par, par, False)

        @block.tensor
        def _(pe):
            weights.ready(pe, 0)
            for b in range(NB):
                cols = slice(b * TB, (b + 1) * TB)
                mm3(pe, acc[b][:, :], [((wdh[:, c * LAT:(c + 1) * LAT], wdl[:, c * LAT:(c + 1) * LAT]),
                                        (G.xTh[:, c, cols], G.xTl[:, c, cols])) for c in range(NC)]
                    ).then_inc(xl_mm, 1)
            pe.wait_ge(xl_lo, NB)

            def w(par, col):
                return wh[:, par, col:col + P], wl[:, par, col:col + P]

            def xl(b):
                return xlh[:, b * TB:(b + 1) * TB], xll[:, b * TB:(b + 1) * TB]

            def gates(i, k):
                n = i * 2 * U + k
                par, b, half = where(k % (2 * U))
                if k % U == 0:
                    wait(pe, w_lo, i * 2 + k // U + 1)
                wait(pe, r_done, n - 1)
                mm3(pe, gate[k % 2][:, :], [(w(par, HID + half * P), xl(b))]).then_inc(g_mm, 1)

            def ups(i, k):
                n = i * 2 * U + k
                par, b, half = where(k)
                wait(pe, h_done, n - 1)
                mm3(pe, up[k % 2][:, :], [(w(par, half * P), xl(b))]).then_inc(u_mm, 1)

            def downs(i, k, first, last):
                n = i * 2 * U + k
                par, b, half = where(k % (2 * U))
                wait(pe, hl_done, n + 1)
                s = k % RING
                mm3(pe, acc[b][:, :], [(w(par, 2 * HID + half * P), (hh[:, s, :], hl[:, s, :]))],
                    start=first and 0 <= k < U and half == 0, stop=last and k >= U and half == 1,
                    skip_group_check=True).then_inc(down_done, 1)

            gates(0, 0)

            def body(i, first, last):
                for k in range(2 * U):
                    if not (last and k == 2 * U - 1):
                        gates(i, k + 1)
                    ups(i, k)
                    if not (first and k < LATE):
                        downs(i, k - LATE, first, last)

            looped(pe, EXPERTS // 2, body)
            for k in range(2 * U - LATE, 2 * U):
                downs(EXPERTS // 2 - 1, k, False, True)

        @block.scalar
        def _(act):
            weights.high(act)
            for b in range(NB):
                act.wait_ge(xl_mm, b + 1)
                act.activation(xlh[:, b * TB:(b + 1) * TB], acc[b][:, :], ACT.Copy).then_inc(xl_hi, 1)

            def split(i, e):
                n = i * 2 + e
                act.wait_ge(w_in[e % 2], i * 16 + 16 * (e // 2) + 16)
                wait(act, down_done, (n - 1) * U)
                act.activation(wh[:, e % 2, :], ws[:, e % 2, :], ACT.Copy).then_inc(w_hi, 1)

            def relu(i, k):
                n = i * 2 * U + k
                act.wait_ge(g_mm, n + 1)
                wait(act, t_done, n - 1)
                act.activation(r[:, k % 2, :], gate[k % 2][:, :], ACT.Relu).then_inc(r_done, 1)

            def high(i, k):
                n = i * 2 * U + k
                act.wait_ge(h_done, n + 1)
                wait(act, down_done, n - RING + 1)
                act.activation(hh[:, k % RING, :], h[:, k % 2, :], ACT.Copy).then_inc(hh_done, 1)

            split(0, 0)
            relu(0, 0)

            def body(i, first, last):
                for k in range(2 * U):
                    if not (last and k == 2 * U - 1):
                        relu(i, k + 1)
                    high(i, k)
                    if k % U == 3 and not (last and k > U):
                        split(i, k // U + 1)

            looped(act, EXPERTS // 2, body)
            for b in range(NB):
                act.wait_ge(down_done, EXPERTS * U)
                act.activation(G.acch[:, b * TB:(b + 1) * TB], acc[b][:, :], ACT.Copy).then_inc(acc_hi, 1)

        @block.gpsimd
        def _(pool):
            def split(i, e):
                n = i * 2 + e
                pool.wait_ge(w_hi, n + 1)
                pool.tensor_tensor(wl[:, e % 2, :], ws[:, e % 2, :], raw(wh[:, e % 2, :]), ALU.subtract).then_inc(w_lo, 1)

            def weigh(i, k):
                n = i * 2 * U + k
                par, b, half = where(k)
                if k % U == 0:
                    pool.wait_ge(wb_in[par], i * 16 + 16)
                pool.wait_ge(r_done, n + 1)
                wait(pool, t_done, n - 1)
                pool.tensor_tensor(rw[:, k % 2, :], r[:, k % 2, :], wb[:, par, b * TB:(b + 1) * TB],
                                   ALU.mult).then_inc(rw_done, 1)

            split(0, 0)

            def body(i, first, last):
                for k in range(2 * U):
                    weigh(i, k)
                    if k % U == 4 and not (last and k > U):
                        split(i, k // U + 1)

            looped(pool, EXPERTS // 2, body)

        @block.vector
        def _(dve):
            weights.low(dve)
            for b in range(NB):
                cols = slice(b * TB, (b + 1) * TB)
                dve.wait_ge(xl_hi, b + 1)
                dve.tensor_tensor(xll[:, cols], acc[b][:, :], raw(xlh[:, cols]), ALU.subtract).then_inc(xl_lo, 1)

            def square(i, k):
                n = i * 2 * U + k
                dve.wait_ge(rw_done, n + 1)
                wait(dve, h_done, n - 1)
                dve.tensor_tensor(tt[:, k % 2, :], r[:, k % 2, :], rw[:, k % 2, :], ALU.mult).then_inc(t_done, 1)

            def hidden(i, k):
                n = i * 2 * U + k
                dve.wait_ge(u_mm, n + 1)
                dve.wait_ge(t_done, n + 1)
                wait(dve, hl_done, n - 1)
                dve.tensor_tensor(h[:, k % 2, :], up[k % 2][:, :], tt[:, k % 2, :], ALU.mult).then_inc(h_done, 1)

            def low(i, k):
                n = i * 2 * U + k
                dve.wait_ge(hh_done, n + 1)
                wait(dve, down_done, n - RING + 1)
                dve.tensor_tensor(hl[:, k % RING, :], h[:, k % 2, :], raw(hh[:, k % RING, :]), ALU.subtract
                                  ).then_inc(hl_done, 1)

            square(0, 0)

            def body(i, first, last):
                for k in range(2 * U):
                    hidden(i, k)
                    if not (last and k == 2 * U - 1):
                        square(i, k + 1)
                    low(i, k)

            looped(dve, EXPERTS // 2, body)
            for b in range(NB):
                cols = slice(b * TB, (b + 1) * TB)
                dve.wait_ge(acc_hi, b + 1)
                dve.tensor_tensor(G.accl[:, cols], acc[b][:, :], raw(G.acch[:, cols]), ALU.subtract).then_inc(acc_lo, 1)


def stage_attend0(nc, G, I):
    q_mm, e_done, r_done, qp_done, z_mm, zi_done, zs_mm, zs_sb, a_mm, at_done, link, b_in = (
        G.sem("at_" + n) for n in ("q_mm", "e", "r", "qp", "z_mm", "zi", "zs_mm", "zs_sb", "a_mm", "at", "link", "b_in"))
    n_done, nqb_done = G.sem("at_n"), G.sem("at_nqb")
    with ExitStack() as stack:
        M = Memory(nc, stack, "at_")
        qh, ql = M.sb("qh", [P, NC * D], F32R), M.sb("ql", [P, NC * D], F32R)
        weights = SplitWeights(G, M, "atw_", [(qh[:, :], ql[:, :], I["qT"].rearrange("(c p) n -> p c n", p=P))])
        qb, nqb = M.sb("qb", [P, NC]), M.sb("nqb", [P, NC])
        e, r, qp = M.sb("e", [P, 2, TB]), M.sb("r", [P, 2, TB]), M.sb("qp", [P, 2 * NC, TB])
        zi, zs = M.sb("zi", [H0, TB]), M.sb("zs", [P, 2, TB])
        zh, zl = M.sb("zh", [P, 2, TB], F32R), M.sb("zl", [P, 2, TB], F32R)
        zz = M.sb("zz", [P, TB])
        block = stack.enter_context(nc.Block())
        UN = NB * NC

        @block.sync
        def _(sp):
            weights.load(sp)
            sp.dma_start(qb[:, :], I["q_b"]).then_inc(b_in, 16)

        @block.tensor
        def _(pe):
            def queries(b):
                cols = slice(b * TB, (b + 1) * TB)
                for g in range(NC):
                    n = b * NC + g
                    wait(pe, e_done, n - 1)
                    wait(pe, r_done, n - 1)
                    mm3(pe, G.ps[n % 2][:, :], [((qh[:, c * D + g * P:c * D + (g + 1) * P], ql[:, c * D + g * P:c * D + (g + 1) * P]),
                                                 (G.xTh[:, c, cols], G.xTl[:, c, cols])) for c in range(NC)]).then_inc(q_mm, 1)

            def attend(b):
                wait(pe, zi_done, b - 1)
                for g in range(NC):
                    n = b * NC + g
                    pe.wait_ge(qp_done, n + 1)
                    last = pe.matmul(G.ps[6 + b % 2][0:H0, :], G.ksb[:, g, :], qp[:, n % (2 * NC), :],
                                     start=g == 0, stop=g == NC - 1)
                last.then_inc(z_mm, 1)
                for g in range(NC):
                    n = b * NC + g
                    wait(pe, at_done, n - 1)
                    pe.matmul(G.ps[2 + n % 2][:, :], G.kvb[:, g, :], qp[:, n % (2 * NC), :],
                              start=True, stop=True).then_inc(a_mm, 1)
                    if g == 0:
                        pe.wait_ge(zi_done, b + 1)
                    wait(pe, zs_sb, n - 1)
                    for m, z in enumerate((zh, zl)):
                        last = pe.matmul(G.ps[4 + n % 2][:, :], G.headsel[:, g, :], z[:, b % 2, :],
                                         start=m == 0, stop=m == 1)
                    last.then_inc(zs_mm, 1)

            weights.ready(pe, 0)
            queries(0)
            for b in range(NB):
                if b + 1 < NB:
                    queries(b + 1)
                attend(b)

        @block.scalar
        def _(act):
            weights.high(act)
            act.wait_ge(b_in, 16)
            act.mul(nqb[:, :], qb[:, :], -1.0).then_inc(nqb_done, 1)
            act.wait_ge(nqb_done, 1)
            def features(b):
                for g in range(NC):
                    n = b * NC + g
                    act.wait_ge(q_mm, n + 1)
                    wait(act, qp_done, n - 1)
                    act.activation(e[:, n % 2, :], G.ps[n % 2][:, :], ACT.Relu, bias=nqb[:, g:g + 1],
                                   scale=-1.0).then_inc(n_done, 1)
                    act.wait_ge(n_done, n + 1)
                    act.activation(e[:, n % 2, :], e[:, n % 2, :], ACT.Exp, scale=-1.0).then_inc(e_done, 1)
                    act.activation(r[:, n % 2, :], G.ps[n % 2][:, :], ACT.Relu, bias=qb[:, g:g + 1]).then_inc(r_done, 1)

            features(0)
            for b in range(NB):
                if b + 1 < NB:
                    features(b + 1)
                for g in range(NC):
                    n = b * NC + g
                    act.wait_ge(zs_mm, n + 1)
                    wait(act, at_done, n - 1)
                    act.activation(zs[:, n % 2, :], G.ps[4 + n % 2][:, :], ACT.Copy).then_inc(zs_sb, 1)

        @block.vector
        def _(dve):
            weights.low(dve)
            chain = Chain(dve, link)
            chain.done(dve.memset(zz[:, :], 0.0))
            for s in range(2):
                dve.tensor_copy(zh[:, s, :], zz[:, :])
                last = dve.tensor_copy(zl[:, s, :], zz[:, :])
            chain.done(last)
            def features(b):
                for g in range(NC):
                    n = b * NC + g
                    dve.wait_ge(e_done, n + 1)
                    dve.wait_ge(r_done, n + 1)
                    wait(dve, a_mm, n - 2 * NC + 1)
                    dve.tensor_tensor(qp[:, n % (2 * NC), :], e[:, n % 2, :], r[:, n % 2, :], ALU.add).then_inc(qp_done, 1)

            features(0)
            for b in range(NB):
                if b + 1 < NB:
                    features(b + 1)
                dve.wait_ge(z_mm, b + 1)
                wait(dve, zs_mm, (b - 1) * NC)
                chain.done(dve.tensor_scalar_add(zi[:, :], G.ps[6 + b % 2][0:H0, :], RMS_EPS))
                chain.done(dve.reciprocal(zi[:, :], zi[:, :]))
                chain.done(dve.tensor_copy(zh[0:H0, b % 2, :], zi[:, :]))
                dve.tensor_tensor(zl[0:H0, b % 2, :], zi[:, :], raw(zh[0:H0, b % 2, :]),
                                  ALU.subtract).then_inc(zi_done, 1)
                for g in range(NC):
                    n = b * NC + g
                    dve.wait_ge(a_mm, n + 1)
                    dve.wait_ge(zs_sb, n + 1)
                    dve.tensor_tensor(G.X[:, n, :], G.ps[2 + n % 2][:, :], zs[:, n % 2, :], ALU.mult).then_inc(at_done, 1)


def stage_output0(nc, G, I):
    names = ("u_mm", "r", "t", "h", "hh", "hl", "ath", "atl", "o_mm", "x1")
    u_mm, r_done, t_done, h_done, hh_done, hl_done, ath_done, atl_done, o_mm, x1_done = (G.sem("o0_" + n) for n in names)
    x_in = [G.sem(f"o0_x_in{n}") for n in range(2)]
    xb_done, b_in = G.sem("o0_xb"), G.sem("o0_b_in")
    with ExitStack() as stack:
        M = Memory(nc, stack, "o0_")
        w = {}
        jobs = []
        for name, src, cols in (("sw1", "sw1T", NC * HID), ("swg", "swgT", NC * HID), ("o", "oT", NC * D),
                                ("sw2", "sw2T", 2 * D), ("up", "wupT", D)):
            w[name] = (M.sb(name + "h", [P, cols], F32R), M.sb(name + "l", [P, cols], F32R))
            jobs.append((w[name][0][:, :], w[name][1][:, :], I[src].rearrange("(c p) n -> p c n", p=P)))
        weights = SplitWeights(G, M, "o0w_", jobs)
        ob = M.sb("ob", [P, D])
        ath, atl = M.sb("ath", [P, NC, TB], F32R), M.sb("atl", [P, NC, TB], F32R)
        hsh, hsl = M.sb("hsh", [P, 2, TB], F32R), M.sb("hsl", [P, 2, TB], F32R)
        r, h = M.sb("r", [P, TB]), M.sb("h", [P, TB])
        xr = M.sb("xr", [P, 2, D])
        block = stack.enter_context(nc.Block())

        def cut(name, width, c, col, n):
            a = c * width + col
            return w[name][0][:, a:a + n], w[name][1][:, a:a + n]

        @block.sync
        def _(sp):
            weights.load(sp)
            sp.dma_start(ob[:, :], I["o_b"].partition_broadcast(P)).then_inc(b_in, 16)
            for t in range(NT):
                wait(sp, x1_done, t - 1)
                sp.dma_start(xr[:, t % 2, :], I["x"][t * P:(t + 1) * P, :]).then_inc(x_in[t % 2], 16)

        @block.gpsimd
        def _(pool):
            pool.wait_ge(b_in, 16)
            for t in range(NT):
                pool.wait_ge(x_in[t % 2], 16 * (t // 2 + 1))
                pool.tensor_tensor(xr[:, t % 2, :], xr[:, t % 2, :], ob[:, :], ALU.add).then_inc(xb_done, 1)

        @block.tensor
        def _(pe):
            def shared(b):
                cols = slice(b * TB, (b + 1) * TB)
                for half in range(2):
                    n = 2 * b + half
                    wait(pe, h_done, n - 1)
                    for k, name in enumerate(("swg", "sw1")):
                        mm3(pe, G.ps[2 * (n % 2) + k][:, :], [(cut(name, HID, c, half * P, P), (G.xTh[:, c, cols], G.xTl[:, c, cols]))
                                                              for c in range(NC)]).then_inc(u_mm, 1)

            def outputs(b):
                pe.wait_ge(atl_done, (b + 1) * NC)
                pe.wait_ge(hl_done, 2 * (b + 1))
                for k in range(BT):
                    t = b * BT + k
                    wait(pe, x1_done, t - 1)
                    rows = slice(k * P, (k + 1) * P)
                    parts = [((ath[:, g, rows], atl[:, g, rows]), cut("o", D, g, 0, D)) for g in range(NC)]
                    parts += [((hsh[:, c, rows], hsl[:, c, rows]), cut("sw2", D, c, 0, D)) for c in range(2)]
                    parts += [((G.acch[:, t * P:(t + 1) * P], G.accl[:, t * P:(t + 1) * P]), cut("up", D, 0, 0, D))]
                    mm3(pe, G.ps[4 + t % 2][:, :], parts).then_inc(o_mm, 1)

            weights.ready(pe, 1)
            shared(0)
            for b in range(NB):
                if b + 1 < NB:
                    shared(b + 1)
                if b == 0:
                    weights.ready(pe, 4)
                outputs(b)

        @block.scalar
        def _(act):
            weights.high(act)
            for b in range(NB):
                for half in range(2):
                    n = 2 * b + half
                    act.wait_ge(u_mm, 2 * n + 1)
                    wait(act, h_done, n)
                    act.activation(r[:, :], G.ps[2 * (n % 2)][:, :], ACT.Relu).then_inc(r_done, 1)
                    act.wait_ge(h_done, n + 1)
                    wait(act, o_mm, b * BT)
                    act.activation(hsh[:, half, :], h[:, :], ACT.Copy).then_inc(hh_done, 1)
                wait(act, o_mm, b * BT)
                for g in range(NC):
                    act.activation(ath[:, g, :], G.X[:, b * NC + g, :], ACT.Copy).then_inc(ath_done, 1)

        @block.vector
        def _(dve):
            weights.low(dve)
            for step in range(NB + 1):
                b = step
                if step < NB:
                    for half in range(2):
                        n = 2 * b + half
                        dve.wait_ge(r_done, n + 1)
                        wait(dve, hl_done, n)
                        dve.tensor_tensor(r[:, :], r[:, :], r[:, :], ALU.mult).then_inc(t_done, 1)
                        dve.wait_ge(t_done, n + 1)
                        dve.wait_ge(u_mm, 2 * n + 2)
                        dve.tensor_tensor(h[:, :], G.ps[2 * (n % 2) + 1][:, :], r[:, :], ALU.mult).then_inc(h_done, 1)
                        dve.wait_ge(hh_done, n + 1)
                        wait(dve, o_mm, b * BT)
                        dve.tensor_tensor(hsl[:, half, :], h[:, :], raw(hsh[:, half, :]), ALU.subtract).then_inc(hl_done, 1)
                    for g in range(NC):
                        dve.wait_ge(ath_done, b * NC + g + 1)
                        dve.tensor_tensor(atl[:, g, :], G.X[:, b * NC + g, :], raw(ath[:, g, :]), ALU.subtract).then_inc(atl_done, 1)
                    dve.wait_ge(atl_done, (b + 1) * NC)
                    for k in range(BT):
                        t = b * BT + k
                        dve.wait_ge(o_mm, t + 1)
                        dve.wait_ge(xb_done, t + 1)
                        dve.tensor_tensor(G.X[:, t, :], G.ps[4 + t % 2][:, :], xr[:, t % 2, :], ALU.add).then_inc(x1_done, 1)


def stage_qkv(nc, G, I, S):
    names = ("qk_mm", "v_mm", "sq", "ms", "sd", "qn", "t1", "t2", "y", "yt_mm", "hh", "hl", "v_sb", "link", "tables", "ones")
    qk_mm, v_mm, sq_done, ms_done, sd_done, qn_done, t1_done, t2_done, y_done, yt_mm, hh_done, hl_done, v_sb, link, tables, ones_done = (
        G.sem("qkv_" + n) for n in names)
    tab_in = G.sem("qkv_tab_in")
    qk_out, v_out = ([G.sem(f"qkv_{n}{k}") for k in range(2)] for n in ("qk_out", "v_out"))
    with ExitStack() as stack:
        M = Memory(nc, stack, "qkv_")
        w = {n: (M.sb(n + "h", [P, NC * D], F32R), M.sb(n + "l", [P, NC * D], F32R)) for n in "qkv"}
        weights = SplitWeights(G, M, "qkvw_", [
            (w[n][0][:, :], w[n][1][:, :], I["w_qkv"][:, k * D:(k + 1) * D].rearrange("(c p) n -> p c n", p=P))
            for k, n in enumerate("qkv")])
        cs = [M.sb("cos", [P, NT, HD]), M.sb("sin", [P, NT, HD])]
        gam = M.sb("gam", [P, 2, 2, HD])
        tab = M.sb("tab", [P, 2, 2, NT, HD])
        sq = M.sb("sq", [P, 2, D])
        ms, sd, rs = (M.sb(n, [P, 2, H0]) for n in ("ms", "sd", "rs"))
        qn, t1, t2 = (M.sb(n, [P, 2, D]) for n in ("qn", "t1", "t2"))
        yh, yl = M.sb("yh", [P, 2, 2, NC, P], F32R), M.sb("yl", [P, 2, 2, NC, P], F32R)
        vs = M.sb("vs", [P, 2, H0, 2 * HD])
        block = stack.enter_context(nc.Block())

        @block.sync
        def _(sp):
            weights.load(sp)
            for k, n in enumerate(("cos32", "sin32")):
                sp.dma_start(cs[k][:, :, :], I[n].rearrange("(t p) d -> p t d", p=P)).then_inc(tab_in, 16)
            for k, n in enumerate(("q_gamma", "k_gamma")):
                for m in range(2):
                    sp.dma_start(gam[:, k, m, :], I[n][m, :].partition_broadcast(P)).then_inc(tab_in, 16)
            for t in range(NT):
                rows = slice(t * P, (t + 1) * P)
                sp.wait_ge(v_sb, t + 1)
                sp.dma_start(S.v[:, :, t, :].rearrange("r p n -> p r n"),
                             vs[:, t % 2, :, :].rearrange("p (r h) n -> p r (h n)", h=2)).then_inc(v_out[t % 2], 16)
                sp.wait_ge(hl_done, 2 * (t + 1))
                for k in range(2):
                    for part, y in enumerate((yh, yl)):
                        sp.dma_start(S.qk[k, part, :, rows].rearrange("(g p) t -> p g t", p=P),
                                     raw(y[:, t % 2, k, :, :])).then_inc(qk_out[t % 2], 16)
            for k in range(2):
                sp.wait_ge(v_out[k], 16 * NT // 2)
                sp.wait_ge(qk_out[k], 64 * NT // 2)

        @block.tensor
        def _(pe):
            def x(t, c):
                cols = slice(t * P, (t + 1) * P)
                return G.xTh[:, c, cols], G.xTl[:, c, cols]

            def product(t, n, bank):
                return mm3(pe, G.ps[bank], [(x(t, c), (w[n][0][:, c * D:(c + 1) * D], w[n][1][:, c * D:(c + 1) * D]))
                                            for c in range(NC)])

            def transposes(t):
                for k in range(2):
                    pe.wait_ge(y_done, 2 * t + k + 1)
                    wait(pe, hl_done, 2 * (t - 1) + k + 1)
                    for g in range(NC):
                        last = pe.transpose(G.ps[6 + k][:, g * P:(g + 1) * P], t2[:, k, g * P:(g + 1) * P], G.ident[:, :])
                    last.then_inc(yt_mm, 1)

            for t in range(NT):
                for k in range(2):
                    if t == 0:
                        weights.ready(pe, k)
                    wait(pe, qn_done, 2 * (t - 2) + k + 1)
                    product(t, "qk"[k], 2 * (t % 2) + k).then_inc(qk_mm, 1)
                if t >= 1:
                    transposes(t - 1)
                if t == 0:
                    weights.ready(pe, 2)
                wait(pe, v_sb, t - 1)
                product(t, "v", 4 + t % 2).then_inc(v_mm, 1)
            transposes(NT - 1)

        @block.scalar
        def _(act):
            weights.high(act)
            def high(t):
                for k in range(2):
                    act.wait_ge(yt_mm, 2 * t + k + 1)
                    if t >= 2:
                        act.wait_ge(qk_out[t % 2], 64 * (t // 2))
                    act.activation(yh[:, t % 2, k, :, :], G.ps[6 + k].rearrange("p (g n) -> p g n", g=NC),
                                   ACT.Copy).then_inc(hh_done, 1)

            act.wait_ge(ones_done, 1)
            for t in range(NT):
                for k in range(2):
                    act.wait_ge(qk_mm, 2 * t + k + 1)
                    wait(act, ms_done, t)
                    act.activation(sq[:, k, :], G.ps[2 * (t % 2) + k], ACT.Square).then_inc(sq_done, 1)
                act.wait_ge(ms_done, t + 1)
                act.activation(sd[:, :, :], ms[:, :, :], ACT.Sqrt).then_inc(sd_done, 1)
                if t >= 1:
                    high(t - 1)
                act.wait_ge(v_mm, t + 1)
                if t >= 2:
                    act.wait_ge(v_out[t % 2], 16 * (t // 2))
                act.activation(vs[:, t % 2, :, 0:HD], G.ps[4 + t % 2].rearrange("p (h d) -> p h d", h=H0),
                               ACT.Copy).then_inc(v_sb, 1)
            high(NT - 1)

        @block.gpsimd
        def _(pool):
            pool.memset(vs[:, :, :, HD:2 * HD], 1.0).then_inc(ones_done, 1)
            pool.wait_ge(tables, 1)
            for t in range(NT):
                for k in range(2):
                    pool.wait_ge(qn_done, 2 * t + k + 1)
                    wait(pool, y_done, 2 * (t - 1) + k + 1)
                    pool.tensor_tensor(t1[:, k, :].rearrange("p (h d) -> p h d", h=H0),
                                       qn[:, k, :].rearrange("p (h d) -> p h d", h=H0),
                                       tab[:, k, 0, t, :].unsqueeze(1).to_broadcast([P, H0, HD]), ALU.mult).then_inc(t1_done, 1)

        @block.vector
        def _(dve):
            weights.low(dve)
            chain = Chain(dve, link)
            dve.wait_ge(tab_in, 96)
            for k in range(2):
                for m in range(2):
                    last = dve.tensor_tensor(tab[:, k, m, :, :], cs[m][:, :, :],
                                             gam[:, k, m, :].unsqueeze(1).to_broadcast([P, NT, HD]), ALU.mult)
            last.then_inc(tables, 1)
            dve.wait_ge(tables, 1)

            def low(t):
                for k in range(2):
                    dve.wait_ge(hh_done, 2 * t + k + 1)
                    dve.tensor_tensor(yl[:, t % 2, k, :, :], G.ps[6 + k].rearrange("p (g n) -> p g n", g=NC),
                                      raw(yh[:, t % 2, k, :, :]), ALU.subtract).then_inc(hl_done, 1)

            for t in range(NT):
                dve.wait_ge(sq_done, 2 * (t + 1))
                chain.done(dve.reduce_sum(ms[:, :, :], sq[:, :, :].rearrange("p k (h d) -> p k h d", h=H0), axis=AX))
                wait(dve, sd_done, t)
                dve.tensor_scalar(ms[:, :, :], ms[:, :, :], 1.0 / HD, RMS_EPS, ALU.mult, ALU.add).then_inc(ms_done, 1)
                if t >= 1:
                    low(t - 1)
                dve.wait_ge(sd_done, t + 1)
                chain.done(dve.reciprocal(rs[:, :, :], sd[:, :, :]))
                for k in range(2):
                    dve.tensor_tensor(qn[:, k, :].rearrange("p (h d) -> p h d", h=H0),
                                      G.ps[2 * (t % 2) + k].rearrange("p (h d) -> p h d", h=H0),
                                      rs[:, k, :].unsqueeze(2).to_broadcast([P, H0, HD]), ALU.mult).then_inc(qn_done, 1)
                for k in range(2):
                    dve.wait_ge(qn_done, 2 * t + k + 1)
                    wait(dve, yt_mm, 2 * (t - 1) + k + 1)
                    q4 = qn[:, k, :].rearrange("p (h d) -> p h d", h=H0)
                    r4 = t2[:, k, :].rearrange("p (h d) -> p h d", h=H0)
                    half = HD // 2
                    for m in range(2):
                        sin = tab[:, k, 1, t, m * half:(m + 1) * half].unsqueeze(1).to_broadcast([P, H0, half])
                        last = dve.tensor_tensor(r4[:, :, m * half:(m + 1) * half],
                                                 q4[:, :, (1 - m) * half:(2 - m) * half], sin, ALU.mult)
                    last.then_inc(t2_done, 1)
                for k in range(2):
                    dve.wait_ge(t2_done, 2 * t + k + 1)
                    dve.wait_ge(t1_done, 2 * t + k + 1)
                    dve.tensor_tensor(t2[:, k, :], t2[:, k, :], t1[:, k, :], ALU.add).then_inc(y_done, 1)
            low(NT - 1)


class Plan:

    def __init__(self, b):
        back = WINDOW // P
        q0, q1 = b * BT, (b + 1) * BT
        keys = [(kt, max(q0, kt), min(q1 - 1, kt + back)) for kt in range(max(0, q0 - back), q1)]
        self.keys = sorted(keys, key=lambda k: -(k[2] - k[1]))
        self.maxima = []
        for qt in range(q0, q1):
            first = max(0, qt - back)
            count = qt - first + 1
            pieces = -(-count // BT)
            cuts = [first + count * k // pieces for k in range(pieces + 1)]
            self.maxima.append((qt, list(zip(cuts, cuts[1:]))))
        self.chunks = 2 * sum(len(c) for _, c in self.maxima)
        self.back = back


def stage_attend1(nc, G, I, S):
    K3 = 3 * HD
    KM = K3 + 2
    plans = [Plan(b) for b in range(NB)]
    PAIRS = H0 // 2
    keys_before = [sum(len(p.keys) for p in plans[:b]) for b in range(NB)]
    KEYS = sum(len(p.keys) for p in plans)
    chunks_before = [sum(p.chunks for p in plans[:b]) for b in range(NB)]
    CHUNKS = sum(p.chunks for p in plans)
    scale = 1.0 / float(np.sqrt(HD))
    s_mm, p_done, av_mm, a_mm, a_red, m_done, mr_mm, mr_sb, o_sb, kones, link = (G.sem("l1_" + n) for n in (
        "s_mm", "p", "av_mm", "a_mm", "a_red", "m", "mr_mm", "mr_sb", "o_sb", "kones", "link"))
    q_in, k_in, v_in = ([G.sem(f"l1_{n}{k}") for k in range(2)] for n in ("q_in", "k_in", "v_in"))
    o_out = [G.sem(f"l1_o_out{k}") for k in range(2)]
    first_in = [G.sem(f"l1_first_in{b}") for b in range(NB)]
    nm_done, mh_done = G.sem("l1_nm"), G.sem("l1_mh")
    sr_in, iota_done, se_link, sel_done, pos_mm, oh_done, pick_mm = (G.sem("se_" + n) for n in (
        "sr_in", "iota", "link", "sel", "pos_mm", "oh", "pick_mm"))
    PR = 2
    LEAD = 36
    PLACES, PICKS = 2, 6
    with ExitStack() as stack:
        M = Memory(nc, stack, "l1_")
        q, k = M.sb("q", [P, 2, 2, T], F32R), M.sb("k", [P, 2, 2, T], F32R)
        v = M.sb("v", [P, 2, NT, 2, 2 * HD])
        pt = M.sb("pt", [P, PR, 2, TB])
        mx, nm = M.sb("mx", [P, 2, BT, 3]), M.sb("nm", [P, 2, BT])
        mrow = M.sb("mrow", [P, 2, BT, KM], F32R)
        ob = M.sb("ob", [P, 2, TB])
        zero = M.sb("zero", [P, KM])
        sr, junk, same = M.sb("sr", [P, T]), M.sb("junk", [P, 2, T], BF16), M.sb("same", [P, 2, P])
        count, rank, sel = M.sb("count", [P, NT, 3]), M.sb("rank", [P, NT]), M.sb("sel", [P, NT], BF16)
        place, numi, ordi = M.sb("place", [P, NT]), M.sb("numi", [P, NT], I32), M.sb("ordi", [P, SEL], I32)
        order, before = M.sb("order", [P, SEL]), M.sb("before", [P, P])
        onehot, number = M.sb("onehot", [P, NT, SEL], BF16), M.sb("number", [P, NT, 2], BF16)
        onesb, strictb, parti = M.sb("onesb", [P, P], BF16), M.sb("strictb", [P, P], BF16), M.sb("parti", [P, NT], I32)
        picked = M.sb("picked", [P, NS, 2])
        block = stack.enter_context(nc.Block())

        def unit(i, u):
            par, b = (u // NB) % 2, u % NB
            pair = i * 2 + u // NB
            return par, b, pair * KEYS + keys_before[b], pair * CHUNKS + chunks_before[b], pair * NB + b

        @block.sync
        def _(sp):
            def load(pair, par, early):
                if not early:
                    sp.wait_ge(av_mm, (pair - 1) * KEYS)
                rows = bass.ds(pair * 2 * HD, 2 * HD)
                for dst, which, sem in ((q, 0, q_in[par]), (k, 1, k_in[par])):
                    for n, part in enumerate((0, which, 1 - which)):
                        sp.dma_start(raw(dst[n * HD:(n + 1) * HD, par, :, :]),
                                     S.qk[which, part, rows, :].rearrange("(h d) t -> d h t", h=2)).then_inc(sem, 16)
                load_values(pair, par)

            def load_values(pair, par):
                sp.dma_start(v[:, par, :, :, :].rearrange("p t h n -> p (t h n)"),
                             S.v[bass.ds(pair, 1), :, :, :].rearrange("a p t n -> (a p) (t n)")).then_inc(v_in[par], 16)

            def store(unit_no, pair, b):
                sp.wait_ge(o_sb, unit_no + 1)
                for h in range(2):
                    rows = slice(h * 2 * HD, h * 2 * HD + HD)
                    sp.dma_start(S.o[bass.ds(pair * 2 * HD + h * HD, HD), b * TB:(b + 1) * TB], ob[rows, b % 2, :]
                                 ).then_inc(o_out[b % 2], 16)
                    one = slice(h * 2 * HD + HD, h * 2 * HD + HD + 1)
                    sp.dma_start(S.den[bass.ds(pair * 2 + h, 1), b * TB:(b + 1) * TB], ob[one, b % 2, :]
                                 ).then_inc(o_out[b % 2], 16)

            for b in range(NB):
                cols = slice(b * TB, (b + 1) * TB)
                for dst, which in ((q, 0), (k, 1)):
                    for n, part in enumerate((0, which, 1 - which)):
                        sp.dma_start(raw(dst[n * HD:(n + 1) * HD, 0, :, cols]),
                                     S.qk[which, part, 0:2 * HD, cols].rearrange("(h d) t -> d h t", h=2)
                                     ).then_inc(first_in[b], 16)
                if b == 0:
                    load_values(0, 0)
            load(1, 1, True)
            sp.dma_start(sr[:, :], S.score.partition_broadcast(P)).then_inc(sr_in, 16)
            load_routed_qkv(sp, G, I)

            def body(i, first, last):
                for u in range(2 * NB):
                    par, b, _, _, no = unit(i, u)
                    store(no, i * 2 + par, b)
                    if b == NB - 1 and not last:
                        load(i * 2 + 2 + par, par, False)

            looped(sp, PAIRS // 2, body)
            for n in range(2):
                sp.wait_ge(o_out[n], 64 * PAIRS * NB // 2)

        assert KEYS % 2 == 0

        def position(u, j):
            return (u // NB) * KEYS + keys_before[u % NB] + j

        def step_slot(b, j):
            return (keys_before[b] + j) % 2

        sequence, late = [], []
        for u in range(2 * NB):
            chunks = [(u, "chunk", h, m, c, k0, k1) for h in range(2)
                      for m, (qt, cuts) in enumerate(plans[u % NB].maxima) for c, (k0, k1) in enumerate(cuts)]
            sequence += chunks[:3] + late + chunks[3:]
            late = [(u, "rows", 0), (u, "rows", 1)]
        sequence += late
        SEQ = len(sequence)
        assert SEQ % 2 == 0
        chunks_upto = [sum(e[1] == "chunk" for e in sequence[:n + 1]) for n in range(SEQ)]
        rows_upto = [n + 1 - c for n, c in enumerate(chunks_upto)]

        def released(i, n):
            if n < 2:
                if isinstance(i, int) and i == 0:
                    return None
                i, n = i - 1, n + SEQ
            if sequence[n - 2][1] == "chunk":
                return a_red, i * 2 * CHUNKS + chunks_upto[n - 2]
            return mr_sb, i * 4 * NB + rows_upto[n - 2]

        def due(i, pos, last):
            def upto(p):
                even = LEAD + SEQ * (p + 1) // (2 * KEYS)
                return min(even, 14 + 8 * (p + 1)) if isinstance(i, int) and i == 0 else even
            for n in range(0 if pos < 0 else upto(pos - 1), upto(pos)):
                if n < SEQ:
                    yield i, n
                elif not last:
                    yield i + 1, n - SEQ

        @block.tensor
        def _(pe):
            def maximum(i, n):
                u, kind, h = sequence[n][:3]
                par, b, _, _, no = unit(i, u)
                bank = G.ps[6 + n % 2]
                before = released(i, n)
                if before:
                    wait(pe, *before)
                if kind == "chunk":
                    _, _, _, m, c, k0, k1 = sequence[n]
                    if h == 0 and m == 0 and c == 0:
                        if par == 0 and isinstance(i, int) and i == 0:
                            pe.wait_ge(first_in[b], 96)
                        elif b == 0:
                            pe.wait_ge(q_in[par], (i + par) * 48)
                            pe.wait_ge(k_in[par], (i + par) * 48)
                    qt = b * BT + m
                    out = bank[:, 0:(k1 - k0) * P]
                    diag, edge = k1 == qt + 1, qt >= plans[b].back and k0 == qt - plans[b].back
                    last = pe.matmul(out, q[0:K3, par, h, qt * P:(qt + 1) * P], k[0:K3, par, h, k0 * P:k1 * P],
                                     start=True, stop=not (diag or edge))
                    if diag:
                        last = pe.matmul(bank[:, (k1 - 1 - k0) * P:(k1 - k0) * P], G.identb[:, :], G.lower[:, :],
                                         start=False, stop=not edge)
                    if edge:
                        last = pe.matmul(bank[:, 0:P], G.identb[:, :], G.upper[:, :], start=False, stop=True)
                    last.then_inc(a_mm, 1)
                else:
                    pe.wait_ge(m_done, no + 1)
                    for m in range(BT):
                        last = pe.matmul(bank[0:KM, m * P:(m + 1) * P], mrow[:, h, m, :], G.identr[:, :],
                                         start=True, stop=True)
                    last.then_inc(mr_mm, 1)

            def scores(i, u, j):
                par, b, keys, _, no = unit(i, u)
                kt, qa, qz = plans[b].keys[j]
                n = keys + j
                wait(pe, p_done, n - 1)
                if j == 0:
                    pe.wait_ge(mr_sb, 2 * no + 2)
                width = (qz - qa + 1) * P
                slot = step_slot(b, j)
                diag, edge = kt == qa, kt + plans[b].back == qz
                for h in range(2):
                    bank = G.ps[2 * slot + h]
                    last = pe.matmul(bank[:, 0:width], k[0:KM, par, h, kt * P:(kt + 1) * P],
                                     q[0:KM, par, h, qa * P:(qz + 1) * P], start=True, stop=not (diag or edge))
                    if diag:
                        last = pe.matmul(bank[:, 0:P], G.identb[:, :], G.upper[:, :], start=False, stop=not edge)
                    if edge:
                        last = pe.matmul(bank[:, width - P:width], G.identb[:, :], G.lower[:, :], start=False, stop=True)
                last.then_inc(s_mm, 1)

            def places():
                pe.wait_ge(sel_done, 1)
                pe.wait_ge(a_red, PAIRS * CHUNKS)
                pe.wait_ge(mr_sb, PAIRS * NB * 2)
                pe.matmul(G.ps[6][:, 0:NT], strictb[:, :], sel[:, :], start=True, stop=False, skip_group_check=True)
                for t in range(NT - 1):
                    last = pe.matmul(G.ps[6][:, t + 1:NT], onesb[:, :], sel[:, t:t + 1].to_broadcast([P, NT - 1 - t]),
                                     start=False, stop=t == NT - 2, skip_group_check=True)
                last.then_inc(pos_mm, 1)

            def picks():
                for m in range(NS):
                    for t in range(NT):
                        pe.wait_ge(oh_done, t + 1)
                        last = pe.matmul(G.ps[7][:, 2 * m:2 * m + 2], onehot[:, t, m * P:(m + 1) * P], number[:, t, :],
                                         start=t == 0, stop=t == NT - 1)
                last.then_inc(pick_mm, 1)

            def values(i, u, j):
                par, b, keys, _, no = unit(i, u)
                kt, qa, qz = plans[b].keys[j]
                n = keys + j
                pe.wait_ge(p_done, n + 1)
                if j == 0:
                    wait(pe, o_sb, no - 1)
                    if b == 0:
                        pe.wait_ge(v_in[par], (i + 1) * 16)
                bank = G.ps[4 + b % 2]
                for h in range(2):
                    last = pe.matmul(bank[h * 2 * HD:(h + 1) * 2 * HD, (qa - b * BT) * P:(qz + 1 - b * BT) * P],
                                     v[:, par, kt, h, :], pt[:, step_slot(b, j), h, 0:(qz - qa + 1) * P],
                                     start=j == 0, stop=j == len(plans[b].keys) - 1)
                last.then_inc(av_mm, 1)

            for at in due(0, -1, False):
                maximum(*at)
            scores(0, 0, 0)

            def body(i, first, last):
                for u in range(2 * NB):
                    b = u % NB
                    end = last and u == 2 * NB - 1
                    steps = len(plans[b].keys)
                    for j in range(steps):
                        for at in due(i, position(u, j), last):
                            maximum(*at)
                        if end and j == PLACES:
                            places()
                        if end and j == PICKS:
                            picks()
                        if j + 1 < steps:
                            scores(i, u, j + 1)
                        elif not end:
                            scores(i, u + 1, 0)
                        values(i, u, j)

            looped(pe, PAIRS // 2, body)

        @block.gpsimd
        def _(pool):
            pool.memset(before[:, :], 1.0).then_inc(iota_done, 1)
            pool.iota(numi[:, :], [[1, NT]], base=0, channel_multiplier=0).then_inc(iota_done, 1)
            pool.iota(parti[:, :], [[0, NT]], base=0, channel_multiplier=1).then_inc(iota_done, 1)
            pool.iota(ordi[:, :], [[1, SEL]], base=1, channel_multiplier=0).then_inc(iota_done, 1)
            pool.wait_ge(iota_done, 4)
            pool.affine_select(out=before[:, :], in_=before[:, :], compare_op=ALU.is_gt, fill=0.0, base=0,
                               pattern=[[-1, P]], channel_multiplier=1).then_inc(iota_done, 1)

        @block.scalar
        def _(act):
            act.wait_ge(kones, 1)

            def exponentials(i, u, j):
                par, b, keys, _, no = unit(i, u)
                kt, qa, qz = plans[b].keys[j]
                n = keys + j
                width = (qz - qa + 1) * P
                slot = step_slot(b, j)
                act.wait_ge(s_mm, n + 1)
                wait(act, av_mm, n - 1)
                act.activation(pt[:, step_slot(b, j), :, 0:width],
                               G.banks[:, 2 * slot:2 * slot + 2, 0:width], ACT.Exp, scale=scale).then_inc(p_done, 1)

            def rows(i, n):
                u, kind, h = sequence[n][:3]
                if kind == "rows":
                    par, b, _, _, no = unit(i, u)
                    act.wait_ge(mr_mm, 2 * no + h + 1)
                    act.activation(q[K3:KM, par, h, b * TB:(b + 1) * TB], G.ps[6 + n % 2][K3:KM, :], ACT.Copy
                                   ).then_inc(mr_sb, 1)

            for at in due(0, -1, False):
                rows(*at)

            def body(i, first, last):
                for u in range(2 * NB):
                    for j in range(len(plans[u % NB].keys)):
                        exponentials(i, u, j)
                        for at in due(i, position(u, j), last):
                            rows(*at)

            looped(act, PAIRS // 2, body)

        @block.vector
        def _(dve):
            chain = Chain(dve, link)
            chain.done(dve.memset(zero[:, :], 0.0))
            for h in range(2):
                for m in range(BT):
                    dve.tensor_copy(mrow[:, h, m, :], zero[:, :])
            for par in range(2):
                for h in range(2):
                    last = dve.tensor_copy(k[K3:KM, par, h, :].rearrange("p (a n) -> p a n", n=P),
                                           G.ones[K3:KM, :].unsqueeze(1).to_broadcast([2, NT, P]))
            chain.done(last)
            dve.memset(mx[:, :, :, :], NEG).then_inc(kones, 1)
            dve.wait_ge(kones, 1)

            def reduce(i, n):
                if sequence[n][1] == "rows":
                    return
                u, _, h, m, c, k0, k1 = sequence[n]
                dve.wait_ge(a_mm, i * 2 * CHUNKS + chunks_upto[n])
                dve.reduce_max(mx[:, h, m, c:c + 1], G.ps[6 + n % 2][:, 0:(k1 - k0) * P], axis=AX).then_inc(a_red, 1)
                if chunks_upto[n] == (u // NB) * CHUNKS + chunks_before[u % NB] + plans[u % NB].chunks:
                    negate(i, u)

            def negate(i, u):
                par, b, _, chunks, no = unit(i, u)
                pieces = max(len(c) for _, c in plans[b].maxima)
                dve.wait_ge(a_red, chunks + plans[b].chunks)
                dve.tensor_reduce(nm[:, :, :], mx[:, :, :, 0:pieces], AX, ALU.max, negate=True).then_inc(nm_done, 1)
                dve.wait_ge(nm_done, no + 1)
                wait(dve, mr_mm, 2 * no)
                dve.tensor_copy(mrow[:, :, :, K3:K3 + 1], nm[:, :, :].unsqueeze(3)).then_inc(mh_done, 1)
                dve.wait_ge(mh_done, no + 1)
                dve.tensor_tensor(mrow[:, :, :, K3 + 1:KM], nm[:, :, :].unsqueeze(3), raw(mrow[:, :, :, K3:K3 + 1]),
                                  ALU.subtract).then_inc(m_done, 1)

            def output(i, u):
                par, b, keys, _, no = unit(i, u)
                dve.wait_ge(av_mm, keys + len(plans[b].keys))
                if i_at_least(i, u, 2):
                    dve.wait_ge(o_out[b % 2], (i * 4 + (u // 2)) * 64)
                dve.tensor_copy(ob[:, b % 2, :], G.ps[4 + b % 2]).then_inc(o_sb, 1)

            def i_at_least(i, u, n):
                return not isinstance(i, int) or i * 2 * NB + u >= n

            tokens = Chain(dve, se_link)

            def ranks(t):
                own = G.score[:, t:t + 1]
                if t == 0:
                    dve.memset(count[:, :, :], 0.0)
                    dve.wait_ge(iota_done, 5)
                    dve.tensor_copy(number[:, :, 0], numi[:, :])
                    dve.tensor_copy(number[:, :, 1], parti[:, :])
                    dve.tensor_copy(onesb[:, :], G.ones[:, :])
                    dve.tensor_copy(strictb[:, :], G.strict[:, :])
                    tokens.done(dve.tensor_copy(order[:, :], ordi[:, :]))
                    dve.wait_ge(sr_in, 16)
                else:
                    dve.tensor_scalar(junk[:, t % 2, 0:t * P], sr[:, 0:t * P], own, 0.0, ALU.is_ge, ALU.add,
                                      accum_out=count[:, t, 0:1])
                dve.tensor_scalar(junk[:, t % 2, t * P:T], sr[:, t * P:T], own, 0.0, ALU.is_gt, ALU.add,
                                  accum_out=count[:, t, 1:2])
                tokens.done(dve.scalar_tensor_tensor(same[:, t % 2, :], sr[:, t * P:(t + 1) * P], own, before[:, :],
                                                     ALU.is_equal, ALU.mult, accum_out=count[:, t, 2:3]))
                if t == NT - 1:
                    tokens.done(dve.reduce_sum(rank[:, :], count[:, :, :], axis=AX))
                    dve.tensor_scalar(sel[:, :], rank[:, :], float(SEL), None, ALU.is_lt).then_inc(sel_done, 1)
                    dve.wait_ge(sel_done, 1)

            def onehots():
                dve.wait_ge(pos_mm, 1)
                tokens.done(dve.scalar_tensor_tensor(place[:, :], G.ps[6][:, 0:NT], 1.0, sel[:, :], ALU.add, ALU.mult))
                for t in range(NT):
                    dve.tensor_scalar(onehot[:, t, :], order[:, :], place[:, t:t + 1], None, ALU.is_equal
                                      ).then_inc(oh_done, 1)

            def chosen():
                dve.wait_ge(pick_mm, 1)
                tokens.done(dve.tensor_copy(picked[:, :, :], G.ps[7][:, 0:2 * NS].rearrange("p (m n) -> p m n", n=2)))
                tokens.done(dve.scalar_tensor_tensor(G.idx[:, :], picked[:, :, 0], float(P), picked[:, :, 1],
                                                     ALU.mult, ALU.add))

            for at in due(0, -1, False):
                reduce(*at)

            def body(i, first, last):
                for u in range(2 * NB):
                    for j in range(len(plans[u % NB].keys)):
                        for at in due(i, position(u, j), last):
                            reduce(*at)
                        if first and position(u, j) % 4 == 3 and position(u, j) // 4 < NT:
                            ranks(position(u, j) // 4)
                    if last and u == 2 * NB - 1:
                        onehots()
                        chosen()
                    output(i, u)

            looped(dve, PAIRS // 2, body)


def stage_output1(nc, G, I, S, out):
    ohi, olo, on, o_mm, res = (G.sem("o1_" + n) for n in ("hi", "lo", "on", "mm", "res"))
    o_in, rb_in, r_in, stored = ([G.sem(f"o1_{n}{k}") for k in range(2)] for n in ("o_in", "rb_in", "r_in", "stored"))
    with ExitStack() as stack:
        M = Memory(nc, stack, "o1_")
        wh, wl = M.sb("wh", [P, NC * D], F32R), M.sb("wl", [P, NC * D], F32R)
        weights = SplitWeights(G, M, "o1w_", [(wh[:, :], wl[:, :], I["w_out"].rearrange("(c p) n -> p c n", p=P))])
        o, rb = M.sb("o", [P, 2, NC, TB]), M.sb("rb", [P, 2, NC, TB])
        oh, ol = M.sb("oh", [P, 2, NC, TB], F32R), M.sb("ol", [P, 2, NC, TB], F32R)
        r = M.sb("r", [P, 2, D])
        block = stack.enter_context(nc.Block())

        @block.sync
        def _(sp):
            weights.load(sp)
            for b in range(NB):
                cols = slice(b * TB, (b + 1) * TB)
                wait(sp, olo, (b - 1) * NC)
                sp.dma_start(o[:, b % 2, :, :], S.o[:, cols].rearrange("(g p) t -> p g t", p=P)).then_inc(o_in[b % 2], 16)
                for h in range(H0):
                    g, j = h // NC, h % NC
                    sp.dma_start(rb[j * HD:(j + 1) * HD, b % 2, g, :], S.rden[h, cols].partition_broadcast(HD)
                                 ).then_inc(rb_in[b % 2], 16)

        @block.gpsimd
        def _(pool):
            for t in range(NT):
                if t >= 2:
                    pool.wait_ge(stored[t % 2], 16 * (t // 2))
                pool.dma_start(r[:, t % 2, :], S.r[t * P:(t + 1) * P, :]).then_inc(r_in[t % 2], 16)

        @block.scalar
        def _(act):
            weights.high(act)
            for b in range(NB):
                for g in range(NC):
                    act.wait_ge(on, b * NC + g + 1)
                    wait(act, o_mm, (b - 1) * BT)
                    act.activation(oh[:, b % 2, g, :], o[:, b % 2, g, :], ACT.Copy).then_inc(ohi, 1)
                for k in range(BT):
                    t = b * BT + k
                    act.wait_ge(res, t + 1)
                    act.dma_start(out[t * P:(t + 1) * P, :], r[:, t % 2, :]).then_inc(stored[t % 2], 16)
            for k in range(2):
                act.wait_ge(stored[k], 16 * NT // 2)

        @block.vector
        def _(dve):
            weights.low(dve)
            for b in range(NB):
                dve.wait_ge(o_in[b % 2], 16 * (b // 2 + 1))
                dve.wait_ge(rb_in[b % 2], 256 * (b // 2 + 1))
                for g in range(NC):
                    dve.tensor_tensor(o[:, b % 2, g, :], o[:, b % 2, g, :], rb[:, b % 2, g, :], ALU.mult).then_inc(on, 1)
                for g in range(NC):
                    dve.wait_ge(ohi, b * NC + g + 1)
                    dve.tensor_tensor(ol[:, b % 2, g, :], o[:, b % 2, g, :], raw(oh[:, b % 2, g, :]), ALU.subtract).then_inc(olo, 1)
                for k in range(BT):
                    t = b * BT + k
                    dve.wait_ge(o_mm, t + 1)
                    dve.wait_ge(r_in[t % 2], 16 * (t // 2 + 1))
                    dve.tensor_tensor(r[:, t % 2, :], G.ps[t % 2], r[:, t % 2, :], ALU.add).then_inc(res, 1)

        @block.tensor
        def _(pe):
            weights.ready(pe, 0)
            for t in range(NT):
                b, k = t // BT, t % BT
                pe.wait_ge(olo, (b + 1) * NC)
                wait(pe, res, t - 1)
                rows = slice(k * P, (k + 1) * P)
                mm3(pe, G.ps[t % 2], [((oh[:, b % 2, g, rows], ol[:, b % 2, g, rows]),
                                       (wh[:, g * D:(g + 1) * D], wl[:, g * D:(g + 1) * D])) for g in range(NC)]
                    ).then_inc(o_mm, 1)


def routed_qkv(G):
    cut = lambda a, n: G.WA[:, NC * a:NC * (a + n)].rearrange("p (c n) -> p c n", c=NC)
    FQ, FK = NHQ * HDF, NHK * HDF
    return cut(0, FQ), cut(FQ, FK), cut(FQ + FK, FK)


def load_routed_qkv(queue, G, I):
    wq, wk, wv = routed_qkv(G)
    for w, name in ((wk, "wk"), (wq, "wq"), (wv, "wv")):
        queue.dma_start(w, I[name].rearrange("(c p) n -> p c n", p=P)).then_inc(G.wqkv_in, 16)


def stage_routed(nc, G, I, S):
    names = ("gath", "sq", "ms", "sd", "hn", "hT_mm", "hT", "qk_mm", "qb", "t1", "y", "yt_mm", "yt", "v_mm", "v", "link")
    gath, sq_done, ms_done, sd_done, hn_done, hT_mm, hT_done, qk_mm, qb_done, t1_done, y_done, yt_mm, yt_done, v_mm, v_done, link = (
        G.sem("ro_" + n) for n in names)
    names = ("s_mm", "nm", "p", "pn", "pt_mm", "pt", "av_mm", "o", "wo_mm", "x1", "gu_mm", "sig", "m", "dn_mm", "delta", "gate")
    s_mm, nm_done, p_done, pn_done, pt_mm, pt_done, av_mm, o_done, wo_mm, x1_done, gu_mm, sig_done, m_done, dn_mm, delta_done, gate_done = (
        G.sem("ro_" + n) for n in names)
    ln_in, wo_in, wgu_in, wd_in, added, xs_in, sc_in = (G.sem("ro_" + n) for n in (
        "ln_in", "wo_in", "wgu_in", "wd_in", "added", "xs_in", "sc_in"))
    b_in = [G.sem(f"ro_b_in{k}") for k in range(3)]
    den_in, rden, rden_out = (G.sem("ro_" + n) for n in ("den_in", "rden", "rden_out"))
    FQ, FK = NHQ * HDF, NHK * HDF
    QU, KU = FQ // BANK, FK // BANK
    HB = BANK // HDF
    NF = INTER // P
    scale = 1.0 / float(np.sqrt(HDF))
    with ExitStack() as stack:
        M = Memory(nc, stack, "ro_")
        WA = G.WA
        WB = M.sb("WB", [P, NHQ * D])
        wq, wk, wv = routed_qkv(G)
        wg = WA[:, 0:NC * INTER].rearrange("p (c n) -> p c n", c=NC)
        wu = WA[:, NC * INTER:2 * NC * INTER].rearrange("p (c n) -> p c n", c=NC)
        wb = WB[:, :].rearrange("p (h n) -> p h n", n=D)
        bias = M.sb("bias", [P, FQ + 2 * FK])
        oT = bias[:, :].rearrange("p (h n) -> p h n", h=NHQ)
        qT = M.sb("qT", [P, NHQ, SEL])
        kT, v = M.sb("kT", [P, NHK, SEL]), M.sb("v", [P, NS, FK])
        xs, x1 = M.sb("xs", [P, NS, D]), M.sb("x1", [P, NS, D])
        hn, hT = M.sb("hn", [P, NS, D]), M.sb("hT", [P, NC, SEL])
        cs = [M.sb("cos", [P, NS, HDF]), M.sb("sin", [P, NS, HDF])]
        ln = M.sb("ln", [P, 2, NC])
        ms, sd, rs = (M.sb(n, [P, NS]) for n in ("ms", "sd", "rs"))
        qb, t1, y = (M.sb(n, [P, 2, BANK]) for n in ("qb", "t1", "y"))
        nm, ssum, rsum = (M.sb(n, [P, 3, NS]) for n in ("nm", "ssum", "rsum"))
        SB = (0, 1, 6)
        pr, pt = M.sb("pr", [P, 3, 3 * P]), M.sb("pt", [P, 2, 3 * P])
        sig = M.sb("sig", [P, 2, SEL])
        sc = M.sb("sc", [P, NS])
        gate, dn = M.sb("gate", [P, NS]), M.sb("dn", [P, H0 * T // P])
        block = stack.enter_context(nc.Block())

        units = [(wq, 0, u, m, qT) for u in range(QU) for m in range(NS)]
        units = [(wk, FQ, u, m, kT) for u in range(KU) for m in range(NS)] + units
        vunits = [(u, m) for u in range(KU) for m in range(NS)]

        @block.sync
        def _(sp):
            view = lambda name: I[name].rearrange("(c p) n -> p c n", p=P)
            sp.dma_start(ln[:, 0, :], I["ln1_w"]).then_inc(ln_in, 16)
            sp.dma_start(ln[:, 1, :], I["ln2_w"]).then_inc(ln_in, 16)
            for k, (a, name, n) in enumerate(((FQ, "bk", FK), (0, "bq", FQ), (FQ + FK, "bv", FK))):
                if k == 1:
                    sp.wait_ge(gath, 16 * 2 * NS)
                sp.dma_start(bias[:, a:a + n], I[name].partition_broadcast(P)).then_inc(b_in[k], 16)
            flat = lambda ap: ap.rearrange("h (a n) -> (h a) n", n=H0 * T // P)
            sp.dma_start(dn[:, :], flat(S.den)).then_inc(den_in, 16)
            sp.wait_ge(rden, 1)
            sp.dma_start(flat(S.rden), dn[:, :]).then_inc(rden_out, 16)
            sp.dma_start(wb, I["wo"].rearrange("(h p) n -> p h n", p=P)).then_inc(wo_in, 16)
            sp.wait_ge(qk_mm, len(units))
            sp.wait_ge(v_mm, len(vunits))
            sp.dma_start(wg, view("w_gate")).then_inc(wgu_in, 16)
            sp.dma_start(wu, view("w_up")).then_inc(wgu_in, 16)
            sp.wait_ge(wo_mm, NS)
            sp.dma_start(wb, I["w_down"].rearrange("(h p) n -> p h n", p=P)).then_inc(wd_in, 16)
            sp.wait_ge(rden_out, 16)

        @block.gpsimd
        def _(pool):
            for m in range(NS):
                where = bass.IndirectOffsetOnAxis(G.idx[:, m:m + 1], 0)
                pool.indirect_dma_start(xs[:, m, :], None, S.xn, where).then_inc(xs_in, 16)
            for m in range(NS):
                where = bass.IndirectOffsetOnAxis(G.idx[:, m:m + 1], 0)
                for n, name in enumerate(("cos128", "sin128")):
                    pool.indirect_dma_start(cs[n][:, m, :], None, I[name], where).then_inc(gath, 16)
            for m in range(NS):
                where = bass.IndirectOffsetOnAxis(G.idx[:, m:m + 1], 0)
                pool.indirect_dma_start(sc[:, m:m + 1], None, S.score.unsqueeze(1), where).then_inc(sc_in, 16)
            pool.wait_ge(gath, 16 * 2 * NS)
            for n, (w, off, u, m, dst) in enumerate(units):
                pool.wait_ge(qb_done, n + 1)
                wait(pool, y_done, n - 1)
                pool.tensor_tensor(t1[:, n % 2, :].rearrange("p (h d) -> p h d", d=HDF),
                                   qb[:, n % 2, :].rearrange("p (h d) -> p h d", d=HDF),
                                   cs[0][:, m, :].unsqueeze(1).to_broadcast([P, HB, HDF]), ALU.mult).then_inc(t1_done, 1)
            for m in range(NS):
                pool.wait_ge(delta_done, m + 1)
                where = bass.IndirectOffsetOnAxis(G.idx[:, m:m + 1], 0)
                pool.indirect_dma_start(S.r, where, hn[:, m, :], None, compute_op=ALU.add).then_inc(added, 16)
                pool.wait_ge(added, 16 * (m + 1))

        @block.tensor
        def _(pe):
            def normed(first):
                for m in range(NS):
                    pe.wait_ge(hn_done, first + m + 1)
                    for c in range(NC):
                        last = pe.transpose(G.ps[6 + m][:, c * P:(c + 1) * P], hn[:, m, c * P:(c + 1) * P], G.ident[:, :])
                    last.then_inc(hT_mm, 1)

            normed(0)
            pe.wait_ge(hT_done, NS)

            def transposes(n):
                pe.wait_ge(y_done, n + 1)
                wait(pe, yt_done, n - 1)
                for j in range(HB):
                    last = pe.transpose(G.ps[2 + n % 2][:, j * P:(j + 1) * P], y[:, n % 2, j * P:(j + 1) * P], G.ident[:, :])
                last.then_inc(yt_mm, 1)

            def values(n):
                u, m = vunits[n]
                wait(pe, v_done, n - 1)
                mm32(pe, G.ps[4 + n % 2], [(hT[:, c, m * P:(m + 1) * P], wv[:, c, u * BANK:(u + 1) * BANK])
                                           for c in range(NC)]).then_inc(v_mm, 1)

            for n, (w, off, u, m, dst) in enumerate(units):
                if n == 0:
                    pe.wait_ge(G.wqkv_in, 48)
                wait(pe, qb_done, n - 1)
                mm32(pe, G.ps[n % 2], [(hT[:, c, m * P:(m + 1) * P], w[:, c, u * BANK:(u + 1) * BANK])
                                       for c in range(NC)]).then_inc(qk_mm, 1)
                if n >= 1:
                    transposes(n - 1)
            for n in range(len(vunits)):
                values(n)
                if n == 0:
                    transposes(len(units) - 1)

            def scores(h):
                wait(pe, p_done, NS * (h - 2))
                bank = G.ps[SB[h % 3]]
                for m in range(NS):
                    out = bank[:, m * P:(2 * m + 1) * P]
                    pe.matmul(out, qT[:, h, m * P:(m + 1) * P], kT[:, h * NHK // NHQ, 0:(m + 1) * P],
                              start=m == 0, stop=False, skip_group_check=True)
                    last = pe.matmul(bank[:, 2 * m * P:(2 * m + 1) * P], G.identb[:, :], G.lower[:, :],
                                     start=False, stop=True, skip_group_check=True)
                last.then_inc(s_mm, 1)

            def spread(h):
                pe.wait_ge(pn_done, h + 1)
                wait(pe, pt_done, h - 1)
                for j in range(3):
                    last = pe.transpose(G.ps[2 + h % 2][:, j * P:(j + 1) * P], pr[:, h % 3, j * P:(j + 1) * P], G.ident[:, :])
                last.then_inc(pt_mm, 1)

            def attend(h):
                pe.wait_ge(pt_done, h + 1)
                wait(pe, o_done, h - 1)
                cols = slice((h * NHK // NHQ) * HDF, (h * NHK // NHQ + 1) * HDF)
                out = G.ps[4 + h % 2]
                pe.matmul(out[:, 0:2 * P], v[:, 0, cols], pt[:, h % 2, 0:2 * P], start=True, stop=False, skip_group_check=True)
                pe.matmul(out[:, P:2 * P], v[:, 1, cols], pt[:, h % 2, 2 * P:3 * P], start=False, stop=True,
                          skip_group_check=True).then_inc(av_mm, 1)

            pe.wait_ge(yt_done, len(units))
            pe.wait_ge(qb_done, len(units))
            pe.wait_ge(v_done, len(vunits))
            scores(0)
            scores(1)
            for h in range(NHQ):
                if h + 2 < NHQ:
                    scores(h + 2)
                spread(h)
                if h >= 1:
                    attend(h - 1)
            attend(NHQ - 1)
            pe.wait_ge(wo_in, 16)
            pe.wait_ge(o_done, NHQ)
            for m in range(NS):
                mm32(pe, G.ps[m], [(oT[:, h, m * P:(m + 1) * P], wb[:, h, :]) for h in range(NHQ)]).then_inc(wo_mm, 1)
            normed(NS)
            pe.wait_ge(hT_done, 2 * NS)
            pe.wait_ge(wgu_in, 32)
            for f in range(NF):
                wait(pe, m_done, f - 1)
                for n, w in enumerate((wg, wu)):
                    last = mm32(pe, G.ps[2 + f % 2][:, n * SEL:(n + 1) * SEL],
                                [(w[:, c, f * P:(f + 1) * P], hT[:, c, :]) for c in range(NC)])
                last.then_inc(gu_mm, 1)
            pe.wait_ge(wd_in, 16)
            for m in range(NS):
                for f in range(NF):
                    pe.wait_ge(m_done, f + 1)
                    last = pe.matmul(G.ps[4 + m], qT[:, f, m * P:(m + 1) * P], wb[:, f, :], start=f == 0, stop=f == NF - 1)
                last.then_inc(dn_mm, 1)

        @block.scalar
        def _(act):
            def root(n):
                act.wait_ge(ms_done, n + 1)
                act.activation(sd[:, :], ms[:, :], ACT.Sqrt).then_inc(sd_done, 1)

            root(0)
            def rotated(n):
                w, off, u, m, dst = units[n]
                act.wait_ge(yt_mm, n + 1)
                act.activation(dst[:, u * HB:(u + 1) * HB, m * P:(m + 1) * P],
                               G.ps[2 + n % 2].rearrange("p (h n) -> p h n", h=HB), ACT.Copy).then_inc(yt_done, 1)

            for n in range(len(units)):
                rotated(n)

            def probabilities(h):
                for m in range(NS):
                    act.wait_ge(nm_done, NS * h + m + 1)
                    if m == 0:
                        wait(act, pt_mm, h - 2)
                    act.activation(pr[:, h % 3, m * P:(2 * m + 1) * P], G.ps[SB[h % 3]][:, m * P:(2 * m + 1) * P], ACT.Exp,
                                   bias=nm[:, h % 3, m:m + 1], scale=scale,
                                   accum_out=ssum[:, h % 3, m:m + 1]).then_inc(p_done, 1)

            def spread(h):
                act.wait_ge(pt_mm, h + 1)
                wait(act, av_mm, h - 1)
                act.activation(pt[:, h % 2, :], G.ps[2 + h % 2][:, 0:3 * P], ACT.Copy).then_inc(pt_done, 1)

            def output(h):
                act.wait_ge(av_mm, h + 1)
                act.activation(oT[:, h, :], G.ps[4 + h % 2][:, 0:SEL], ACT.Copy).then_inc(o_done, 1)

            probabilities(0)
            probabilities(1)
            for h in range(NHQ):
                if h + 2 < NHQ:
                    probabilities(h + 2)
                spread(h)
                if h >= 1:
                    output(h - 1)
            output(NHQ - 1)
            root(1)
            act.wait_ge(sc_in, 16 * NS)
            act.activation(gate[:, :], sc[:, :], ACT.Sigmoid).then_inc(gate_done, 1)
            for f in range(NF):
                act.wait_ge(gu_mm, f + 1)
                wait(act, m_done, f - 1)
                act.activation(sig[:, f % 2, :], G.ps[2 + f % 2][:, 0:SEL], ACT.Sigmoid).then_inc(sig_done, 1)

        @block.vector
        def _(dve):
            chain = Chain(dve, link)

            def norm(x, k):
                dve.tensor_tensor(hn[:, :, :], x, x, ALU.mult).then_inc(sq_done, 1)
                dve.wait_ge(sq_done, k + 1)
                chain.done(dve.reduce_sum(ms[:, :], hn[:, :, :], axis=AX))
                dve.tensor_scalar(ms[:, :], ms[:, :], 1.0 / D, RMS_EPS, ALU.mult, ALU.add).then_inc(ms_done, 1)
                dve.wait_ge(sd_done, k + 1)
                chain.done(dve.reciprocal(rs[:, :], sd[:, :]))
                for m in range(NS):
                    dve.tensor_scalar(hn[:, m, :], x[:, m, :], rs[:, m:m + 1], None, ALU.mult).then_inc(hn_done, 1)
                dve.wait_ge(ln_in, 32)
                for m in range(NS):
                    dve.wait_ge(hT_mm, k * NS + m + 1)
                    dve.tensor_tensor(hT[:, :, m * P:(m + 1) * P], G.ps[6 + m].rearrange("p (c n) -> p c n", c=NC),
                                      ln[:, k, :].unsqueeze(2).to_broadcast([P, NC, P]), ALU.mult).then_inc(hT_done, 1)

            dve.wait_ge(den_in, 16)
            dve.reciprocal(dn[:, :], dn[:, :]).then_inc(rden, 1)
            dve.wait_ge(xs_in, 16 * NS)
            norm(xs[:, :, :], 0)
            dve.wait_ge(gath, 16 * 2 * NS)
            dve.wait_ge(b_in[0], 16)
            for n, (w, off, u, m, dst) in enumerate(units):
                dve.wait_ge(qk_mm, n + 1)
                wait(dve, t1_done, n - 1)
                if w is wq and u == 0 and m == 0:
                    dve.wait_ge(b_in[1], 16)
                a = off + u * BANK
                dve.tensor_tensor(qb[:, n % 2, :], G.ps[n % 2], bias[:, a:a + BANK], ALU.add).then_inc(qb_done, 1)
                dve.wait_ge(qb_done, n + 1)
                wait(dve, yt_mm, n - 1)
                q4 = qb[:, n % 2, :].rearrange("p (h d) -> p h d", d=HDF)
                y4 = y[:, n % 2, :].rearrange("p (h d) -> p h d", d=HDF)
                half = HDF // 2
                for k in range(2):
                    last = dve.tensor_tensor(y4[:, :, k * half:(k + 1) * half], q4[:, :, (1 - k) * half:(2 - k) * half],
                                             cs[1][:, m, k * half:(k + 1) * half].unsqueeze(1).to_broadcast([P, HB, half]),
                                             ALU.mult)
                chain.done(last)
                dve.wait_ge(t1_done, n + 1)
                dve.tensor_tensor(y[:, n % 2, :], y[:, n % 2, :], t1[:, n % 2, :], ALU.add).then_inc(y_done, 1)
            dve.wait_ge(b_in[2], 16)
            for n, (u, m) in enumerate(vunits):
                dve.wait_ge(v_mm, n + 1)
                dve.tensor_tensor(v[:, m, u * BANK:(u + 1) * BANK], G.ps[4 + n % 2],
                                  bias[:, FQ + FK + u * BANK:FQ + FK + (u + 1) * BANK], ALU.add).then_inc(v_done, 1)

            def maxima(h):
                dve.wait_ge(s_mm, h + 1)
                wait(dve, p_done, NS * (h - 2))
                for m in range(NS):
                    dve.tensor_reduce(nm[:, h % 3, m:m + 1], G.ps[SB[h % 3]][:, m * P:(2 * m + 1) * P], AX, ALU.max, negate=True
                                      ).then_inc(link, 1)
                    chain.n += 1
                dve.wait_ge(link, chain.n)
                dve.tensor_scalar(nm[:, h % 3, :], nm[:, h % 3, :], scale, None, ALU.mult).then_inc(nm_done, NS)

            def normalised(h):
                dve.wait_ge(p_done, NS * (h + 1))
                chain.done(dve.reciprocal(rsum[:, h % 3, :], ssum[:, h % 3, :]))
                for m in range(NS):
                    cols = slice(m * P, (2 * m + 1) * P)
                    last = dve.tensor_scalar(pr[:, h % 3, cols], pr[:, h % 3, cols], rsum[:, h % 3, m:m + 1], None, ALU.mult)
                last.then_inc(pn_done, 1)

            maxima(0)
            maxima(1)
            for h in range(NHQ):
                if h + 2 < NHQ:
                    maxima(h + 2)
                normalised(h)
            for m in range(NS):
                dve.wait_ge(wo_mm, m + 1)
                dve.tensor_tensor(x1[:, m, :], G.ps[m], xs[:, m, :], ALU.add).then_inc(x1_done, 1)
            dve.wait_ge(x1_done, NS)
            norm(x1[:, :, :], 1)
            for f in range(NF):
                dve.wait_ge(sig_done, f + 1)
                chain.done(dve.tensor_tensor(sig[:, f % 2, :], G.ps[2 + f % 2][:, 0:SEL], sig[:, f % 2, :], ALU.mult))
                dve.tensor_tensor(qT[:, f, :], G.ps[2 + f % 2][:, SEL:2 * SEL], sig[:, f % 2, :], ALU.mult).then_inc(m_done, 1)
            dve.wait_ge(gate_done, 1)
            dve.tensor_tensor(x1[:, :, :], x1[:, :, :], xs[:, :, :], ALU.subtract).then_inc(x1_done, 1)
            dve.wait_ge(x1_done, NS + 1)
            for m in range(NS):
                dve.wait_ge(dn_mm, m + 1)
                chain.done(dve.tensor_tensor(hn[:, m, :], G.ps[4 + m], x1[:, m, :], ALU.add))
                dve.tensor_scalar(hn[:, m, :], hn[:, m, :], gate[:, m:m + 1], None, ALU.mult).then_inc(delta_done, 1)


class Scratch:

    def __init__(self, nc):
        def dram(name, shape, dt=F32):
            return nc.dram_tensor(name, shape, dt, kind="Internal").ap()
        self.wscr = dram("gates_by_expert", [EXPERTS, T])
        self.xn = dram("layer1_xn", [T, D])
        self.r = dram("layer1_residual", [T, D])
        self.qk = dram("layer1_qk", [2, 2, D, T])
        self.v = dram("layer1_v", [H0 // 2, P, NT, 4 * HD])
        self.o = dram("layer1_o", [D, T])
        self.den = dram("layer1_sums", [H0, T])
        self.score = dram("layer1_scores", [T])
        self.rden = dram("layer1_inverse_sums", [H0, T])


class Globals:
    def __init__(self, nc, stack):
        self.nc, self.stack = nc, stack
        M = Memory(nc, stack)
        self.banks = stack.enter_context(nc.psum_tensor("banks", [P, 8, BANK], F32))
        self.ps = [self.banks[:, i, :] for i in range(8)]
        self.ident, self.identb = M.sb("ident", [P, P]), M.sb("identb", [P, P], BF16)
        self.identr = M.sb("identr", [P, P], F32R)
        self.upper, self.lower = M.sb("upper", [P, P], BF16), M.sb("lower", [P, P], BF16)
        self.strict, self.headmask = M.sb("strict", [P, P]), M.sb("headmask", [P, P])
        self.ones = M.sb("ones", [P, P])
        self.kvb, self.ksb = M.sb("kvb", [P, NC, P]), M.sb("ksb", [P, NC, H0])
        self.score = M.sb("score", [P, NT])
        self.idx = M.sb("idx", [P, NS], U32)
        self.headsel = M.sb("headsel", [P, NC, P], F32R)

        self.sems = []

    def sem(self, name):
        self.sems.append(self.nc.alloc_semaphore(name=name))
        return self.sems[-1]

    def give_back_semaphores(self):
        self.nc.clear_and_free_semaphores(self.sems)
        self.nc.all_engine_barrier()
        self.sems = []


STOP = None


def program(nc, I, out):
    S = Scratch(nc)
    with ExitStack() as stack:
        G = Globals(nc, stack)
        stage_constants(nc, G)
        with ExitStack() as features:
            M = Memory(nc, features)
            G.xTh, G.xTl = M.sb("xTh", [P, NC, T], F32R), M.sb("xTl", [P, NC, T], F32R)
            with ExitStack() as keys:
                MK = Memory(nc, keys)
                G.X = MK.sb("X", [P, NT, D])
                G.kvw = {n: (MK.sb(f"kv_w{n}h", [P, cols], F32R), MK.sb(f"kv_w{n}l", [P, cols], F32R))
                         for n, cols in (("g", NC * EXPERTS), ("k", NC * D), ("v", NC * D))}
                weights = SplitWeights(G, MK, "kv_", [
                    (G.kvw[n][0], G.kvw[n][1], I[src].rearrange("(c p) n -> p c n", p=P))
                    for n, src in (("g", "wgT"), ("k", "kT"), ("v", "vT"))])
                stage_normalize(nc, G, "a_", I["x"], None, None, weights=weights)
                stage_kv(nc, G, I, S)
            if STOP == "kv":
                return
            with ExitStack() as tokens:
                MX = Memory(nc, tokens)
                G.acch, G.accl = MX.sb("acch", [P, T], F32R), MX.sb("accl", [P, T], F32R)
                stage_experts(nc, G, I, S)
                if STOP == "ex":
                    return
                G.X = MX.sb("tokens", [P, NT, D])
                stage_attend0(nc, G, I)
                if STOP == "at":
                    return
                stage_output0(nc, G, I)
                if STOP == "o0":
                    return
                G.give_back_semaphores()
                stage_normalize(nc, G, "b_", None, S.xn, S.r, I["w_router"], S.score)
            stage_qkv(nc, G, I, S)
            if STOP == "qkv":
                return
        G.give_back_semaphores()
        with ExitStack() as routed:
            G.WA = Memory(nc, routed).sb("WA", [P, NC * (NHQ + 2 * NHK) * HDF])
            G.wqkv_in = G.sem("wqkv_in")
            stage_attend1(nc, G, I, S)
            if STOP == "l1":
                return
            stage_routed(nc, G, I, S)
            if STOP == "ro":
                return
        stage_output1(nc, G, I, S, out)


def halves(g):
    return np.stack([g, np.roll(g, g.shape[0] // 2)])


def rotary(width):
    inv = np.float32(1.0) / np.float32(10000.0) ** (np.arange(0, width, 2, dtype=np.float32) / np.float32(width))
    ang = np.arange(T, dtype=np.float32)[:, None] * inv[None, :].astype(np.float32)
    return np.concatenate([np.cos(ang), np.cos(ang)], 1), np.concatenate([-np.sin(ang), np.sin(ang)], 1)


def constants():
    c32, s32 = rotary(HD)
    c128, s128 = rotary(HDF)
    return {"cos32": c32, "sin32": s32, "cos128": c128, "sin128": s128}


LAYOUT = {
    "x": lambda a: a["L0_attn_hidden_states"][0],
    "qT": lambda a: a["L0_attn_q_w"].T,
    "kT": lambda a: a["L0_attn_k_w"].T,
    "vT": lambda a: a["L0_attn_v_w"].T,
    "oT": lambda a: a["L0_attn_o_w"].T,
    "q_b": lambda a: a["L0_attn_q_b"].reshape(NC, P).T,
    "k_b": lambda a: a["L0_attn_k_b"],
    "v_b": lambda a: a["L0_attn_v_b"],
    "o_b": lambda a: a["L0_attn_o_b"],
    "wgT": lambda a: a["L0_ffn_Wg"].T,
    "biases": lambda a: a["L0_ffn_biases"],
    "wdT": lambda a: a["L0_ffn_Wdown"].T,
    "wupT": lambda a: a["L0_ffn_Wup"].T,
    "sw1T": lambda a: a["L0_ffn_sw1"].T,
    "swgT": lambda a: a["L0_ffn_swg"].T,
    "sw2T": lambda a: a["L0_ffn_sw2"].T,
    "w_qkv": lambda a: a["L1_attn_w_qkv"],
    "w_out": lambda a: a["L1_attn_w_out"],
    "q_gamma": lambda a: halves(a["L1_attn_q_gamma"]),
    "k_gamma": lambda a: halves(a["L1_attn_k_gamma"]),
    "w_router": lambda a: a["L1_ffn_w_router"].reshape(NC, P).T,
    "ln1_w": lambda a: a["L1_ffn_ln1_w"].reshape(NC, P).T,
    "ln2_w": lambda a: a["L1_ffn_ln2_w"].reshape(NC, P).T,
    **{n: (lambda a, n=n: a["L1_ffn_" + n])
       for n in ("wq", "bq", "wk", "bk", "wv", "bv", "wo", "w_gate", "w_up", "w_down")},
    "ew": lambda a: np.concatenate([a["L0_ffn_rw1"].transpose(0, 2, 1), a["L0_ffn_rwg"].transpose(0, 2, 1),
                                    a["L0_ffn_rw2"].transpose(0, 2, 1)[:, :P], a["L0_ffn_rw2"].transpose(0, 2, 1)[:, P:]],
                                   axis=2),
}


def kernel(**inputs):
    import concourse.bacc as bacc
    from concourse.bass_utils import run_bass_kernel_spmd

    arrays = {name: np.ascontiguousarray(view(inputs)) for name, view in LAYOUT.items()}
    arrays.update(constants())
    nc = bacc.Bacc("TRN2", target_bir_lowering=False, num_devices=1)
    dram = {name: nc.dram_tensor(name + "_in", a.shape, mybir.dt.from_np(a.dtype), kind="ExternalInput").ap()
            for name, a in arrays.items()}
    out = nc.dram_tensor("out", [T, D], F32, kind="ExternalOutput").ap()
    program(nc, dram, out)
    nc.finalize()
    res = run_bass_kernel_spmd(nc, [{name + "_in": a for name, a in arrays.items()}], core_ids=[0])
    return res.results[0]["out"].reshape(1, T, D)
```

```python
from contextlib import ExitStack

import numpy as np

import concourse.bass as bass
from concourse import mybir

P = 128
F32 = mybir.dt.float32
F32R = mybir.dt.float32r
BF16 = mybir.dt.bfloat16
U32 = mybir.dt.uint32
I32 = mybir.dt.int32
ALU = mybir.AluOpType
ACT = mybir.ActivationFunctionType
AX = mybir.AxisListType.X

T = 2048
D = 512
NT = T // P
NC = D // P
TB = 512
NB = T // TB
BT = TB // P
BANK = 512
LN_EPS = 1e-5
RMS_EPS = 1e-6
NEG = -1e30

H0, HD = 16, 32
EXPERTS, TOPK, LAT, HID = 16, 8, 128, 256
ROUTE_SCALE = 2.5
WINDOW = 1024

SEL = T // 8
NS = SEL // P
NHQ, NHK, HDF = 16, 8, 128
INTER = 2048


def raw(ap):
    return ap.bitcast(F32)


class Chain:

    def __init__(self, eng, sem):
        self.eng, self.sem, self.n = eng, sem, 0

    def done(self, ins):
        self.n += 1
        ins.then_inc(self.sem, 1)
        self.eng.wait_ge(self.sem, self.n)


def mm3(pe, out, parts, start=True, stop=True, **kw):
    last = None
    for n, ((ah, al), (bh, bl)) in enumerate(parts):
        end = n == len(parts) - 1
        pe.matmul(out, ah, bh, start=start and n == 0, stop=False, **kw)
        pe.matmul(out, ah, bl, start=False, stop=False, **kw)
        last = pe.matmul(out, al, bh, start=False, stop=stop and end, **kw)
    return last


def mm32(pe, out, parts, start=True, stop=True, **kw):
    last = None
    for n, (a, b) in enumerate(parts):
        last = pe.matmul(out, a, b, start=start and n == 0, stop=stop and n == len(parts) - 1, **kw)
    return last


class Memory:

    def __init__(self, nc, stack, tag=""):
        self.nc, self.stack, self.tag = nc, stack, tag

    def sb(self, name, shape, dt=F32):
        return self.stack.enter_context(self.nc.sbuf_tensor(self.tag + name, shape, dt))


class Shared:
    pass


def stage_constants(nc, G):
    zeroed, made, blocks = G.sem("const_zeroed"), G.sem("const_made"), G.sem("const_blocks")
    with nc.sbuf_tensor("headsel32", [P, NC, P], F32) as headsel, nc.Block() as block:

        @block.gpsimd
        def _(pool):
            pool.memset(G.ident[:, :], 0.0)
            pool.memset(headsel[:, :, :], 0.0)
            pool.memset(G.upper[:, :], 0.0)
            pool.memset(G.strict[:, :], 1.0)
            pool.memset(G.lower[:, :], 0.0).then_inc(zeroed, 1)
            pool.wait_ge(zeroed, 1)
            pool.affine_select(out=G.ident[:, :], in_=G.ident[:, :], compare_op=ALU.not_equal, fill=1.0,
                               base=0, pattern=[[-1, P]], channel_multiplier=1).then_inc(made, 1)
            pool.affine_select(out=G.upper[:, :], in_=G.upper[:, :], compare_op=ALU.is_ge, fill=NEG,
                               base=0, pattern=[[1, P]], channel_multiplier=-1).then_inc(made, 1)
            pool.affine_select(out=G.lower[:, :], in_=G.lower[:, :], compare_op=ALU.is_ge, fill=NEG,
                               base=0, pattern=[[-1, P]], channel_multiplier=1).then_inc(made, 1)
            hs = headsel[:, :, :].rearrange("p g (j d) -> p g j d", d=HD)
            pool.affine_select(out=hs, in_=hs, compare_op=ALU.not_equal, fill=1.0, base=0,
                               pattern=[[P // HD, NC], [1, P // HD], [0, HD]], channel_multiplier=-1).then_inc(made, 1)
            pool.affine_select(out=G.strict[:, :], in_=G.strict[:, :], compare_op=ALU.is_gt, fill=0.0,
                               base=0, pattern=[[1, P]], channel_multiplier=-1).then_inc(made, 1)

        @block.vector
        def _(dve):
            dve.memset(G.headmask[:, :], 0.0).then_inc(blocks, 1)
            dve.memset(G.ones[:, :], 1.0)
            dve.memset(G.ksb[:, :, :], 0.0)
            dve.wait_ge(blocks, 1)
            for j in range(P // HD):
                dve.memset(G.headmask[j * HD:(j + 1) * HD, j * HD:(j + 1) * HD], 1.0)
            dve.wait_ge(made, 5)
            dve.tensor_copy(G.headsel[:, :, :], headsel[:, :, :])
            dve.tensor_copy(G.identb[:, :], G.ident[:, :])
            dve.tensor_copy(G.identr[:, :], G.ident[:, :]).then_inc(blocks, 1)
            dve.wait_ge(blocks, 2)


def stage_normalize(nc, G, x_dram, weights):
    x_in = [G.sem(f"a_x_in{g}") for g in range(NB)]
    var_ready, sd_ready, rstd_ready, xn_ready, xt_ready, hi_ready, lo_ready, link = (
        G.sem("a_" + n) for n in ("var", "sd", "rstd", "xn", "xt", "hi", "lo", "link"))
    RING = 4
    PIECES = [(0, 0), (0, 1), (1, 3), (3, None)]
    X, xTh, xTl = G.X, G.xTh, G.xTl
    with ExitStack() as stack:
        M = Memory(nc, stack, "a_")
        stats, mv = M.sb("stats", [P, NT, 6]), M.sb("mv", [P, NT, 2])
        ve, sd, rstd, shift = (M.sb(n, [P, NT]) for n in ("ve", "sd", "rstd", "shift"))
        xn = M.sb("xn", [P, RING, D])
        block = stack.enter_context(nc.Block())

        @block.sync
        def _(sp):
            for g in range(NB):
                sp.dma_start(X[:, g * BT:(g + 1) * BT, :],
                             x_dram.rearrange("(t p) d -> p t d", p=P)[:, g * BT:(g + 1) * BT, :]).then_inc(x_in[g], 16)
            weights.load(sp)

        @block.vector
        def _(dve):
            chain = Chain(dve, link)

            def statistics(g):
                cols = slice(g * BT, (g + 1) * BT)
                dve.wait_ge(x_in[g], 16)
                for t in range(g * BT, (g + 1) * BT):
                    last = dve.bn_stats(stats[:, t, :], X[:, t, :])
                chain.done(last)
                for t in range(g * BT, (g + 1) * BT):
                    last = dve.bn_aggr(mv[:, t, :], stats[:, t, :])
                chain.done(last)
                dve.tensor_scalar_add(ve[:, cols], mv[:, cols, 1], LN_EPS).then_inc(var_ready, 1)

            def scales(g):
                cols = slice(g * BT, (g + 1) * BT)
                dve.wait_ge(sd_ready, g + 1)
                chain.done(dve.reciprocal(rstd[:, cols], sd[:, cols]))
                dve.scalar_tensor_tensor(shift[:, cols], mv[:, cols, 0], -1.0, rstd[:, cols], ALU.mult, ALU.mult
                                         ).then_inc(rstd_ready, 1)

            def low(t):
                dve.wait_ge(hi_ready, t + 1)
                cols = slice(t * P, (t + 1) * P)
                dve.tensor_tensor(xTl[:, :, cols], G.ps[t % RING][:, :].rearrange("p (c n) -> p c n", c=NC),
                                  raw(xTh[:, :, cols]), ALU.subtract).then_inc(lo_ready, 1)

            statistics(0)
            scales(0)
            for g in range(NB):
                if g + 1 < NB:
                    statistics(g + 1)
                for t in range(g * BT, (g + 1) * BT):
                    if t % BT == BT - 1 and g + 1 < NB:
                        scales(g + 1)
                    low(t)
                weights.low(dve, *PIECES[g])

        @block.tensor
        def _(pe):
            for t in range(NT):
                pe.wait_ge(xn_ready, t + 1)
                if t >= RING:
                    pe.wait_ge(lo_ready, t - RING + 1)
                for c in range(NC):
                    last = pe.transpose(G.ps[t % RING][:, c * P:(c + 1) * P],
                                        xn[:, t % RING, c * P:(c + 1) * P], G.ident[:, :])
                last.then_inc(xt_ready, 1)

        @block.scalar
        def _(act):
            def root(g):
                act.wait_ge(var_ready, g + 1)
                act.activation(sd[:, g * BT:(g + 1) * BT], ve[:, g * BT:(g + 1) * BT], ACT.Sqrt).then_inc(sd_ready, 1)

            def normal(t):
                if t % BT == 0:
                    act.wait_ge(rstd_ready, t // BT + 1)
                if t >= RING:
                    act.wait_ge(xt_ready, t - RING + 1)
                act.activation(xn[:, t % RING, :], X[:, t, :], ACT.Identity, bias=shift[:, t:t + 1],
                               scale=rstd[:, t:t + 1]).then_inc(xn_ready, 1)

            def high(t):
                act.wait_ge(xt_ready, t + 1)
                act.activation(xTh[:, :, t * P:(t + 1) * P], G.ps[t % RING][:, :].rearrange("p (c n) -> p c n", c=NC),
                               ACT.Copy).then_inc(hi_ready, 1)

            root(0)
            for t in range(NT):
                normal(t)
                if t % BT == BT - 1 and t + 1 < NT:
                    root(t // BT + 1)
                if t >= 1:
                    high(t - 1)
                if t % BT == BT - 1 and t + 1 < NT:
                    weights.high(act, *PIECES[t // BT])
            high(NT - 1)
            weights.high(act, *PIECES[NB - 1])


class SplitWeights:

    def __init__(self, G, M, tag, jobs, cols=1024):
        self.w_in = [G.sem(f"{tag}w_in{n}") for n in range(2)]
        self.w_hi, self.w_lo = G.sem(tag + "w_hi"), G.sem(tag + "w_lo")
        self.pieces, self.upto = [], []
        for hi, lo, src in jobs:
            chunks, n = src.shape[1], src.shape[2]
            step = max(1, min(chunks, cols // n))
            for c in range(0, chunks, step):
                part = slice(c * n, (c + step) * n)
                self.pieces.append((hi[:, part], lo[:, part], src[:, c:c + step, :]))
            self.upto.append(len(self.pieces))
        self.stage = M.sb(tag + "stage", [P, 2, max(p[0].shape[1] for p in self.pieces)])

    def at(self, n):
        return self.stage[:, n % 2, 0:self.pieces[n][0].shape[1]]

    def load(self, queue):
        for n, (hi, lo, src) in enumerate(self.pieces):
            if n >= 2:
                queue.wait_ge(self.w_lo, n - 1)
            queue.dma_start(self.at(n).rearrange("p (c n) -> p c n", c=src.shape[1]), src
                            ).then_inc(self.w_in[n % 2], 16)

    def high(self, act, first=0, end=None):
        for n in range(first, len(self.pieces) if end is None else end):
            hi = self.pieces[n][0]
            act.wait_ge(self.w_in[n % 2], 16 * (n // 2 + 1))
            act.activation(hi, self.at(n), ACT.Copy).then_inc(self.w_hi, 1)

    def low(self, dve, first=0, end=None):
        for n in range(first, len(self.pieces) if end is None else end):
            hi, lo = self.pieces[n][:2]
            dve.wait_ge(self.w_hi, n + 1)
            dve.tensor_tensor(lo, self.at(n), raw(hi), ALU.subtract).then_inc(self.w_lo, 1)

    def ready(self, pe, job):
        pe.wait_ge(self.w_lo, self.upto[job])


def stage_kv(nc, G, I, S):
    logit_ready, p1 = G.sem("kv_logit"), G.sem("kv_exp")
    k_mm, v_mm, kx_ready, e_ready, r_ready = (G.sem("kv_" + n) for n in ("k_mm", "v_mm", "kx", "e", "r"))
    kp_ready, v_ready, kv_done, link = (G.sem("kv_" + n) for n in ("kp", "v", "done", "link"))
    bias_in, gate_done, wt_mm, wt_sb, wt_out, sums = (G.sem("kv_" + n) for n in
                                                   ("bias", "gate", "wtmm", "wtsb", "wtout", "sums"))
    n_ready, ez_mm = G.sem("kv_n"), G.sem("kv_ez")
    GATES = 7
    pss, xTh, xTl = G.ps, G.xTh, G.xTl
    with ExitStack() as stack:
        M = Memory(nc, stack, "kv_")
        kbb, vbb, gb = M.sb("kbb", [P, D]), M.sb("vbb", [P, D]), M.sb("gb", [P, EXPERTS])
        kx, ke, kr = M.sb("kx", [P, 2, D]), M.sb("ke", [P, 2, D]), M.sb("kr", [P, 2, D])
        kp, vv = M.sb("kp", [P, 2, D]), M.sb("vv", [P, 2, D])
        gz, gp = M.sb("gz", [P, NT, EXPERTS]), M.sb("gp", [P, NT, EXPERTS])
        gbias, grep = M.sb("gbias", [P, NT, EXPERTS]), M.sb("grep", [P, NT, EXPERTS])
        top = M.sb("top", [P, NT, 8])
        gw, gsum, ginv = M.sb("gw", [P, NT, EXPERTS]), M.sb("gsum", [P, NT]), M.sb("ginv", [P, NT])
        eT, wT = M.sb("eT", [EXPERTS, T]), M.sb("wT", [EXPERTS, T])
        def w(n, c):
            h, l = G.kvw[n]
            k = h.shape[1] // NC
            return h[:, c * k:(c + 1) * k], l[:, c * k:(c + 1) * k]

        def x(t, c):
            cols = slice(t * P, (t + 1) * P)
            return xTh[:, c, cols], xTl[:, c, cols]

        block = stack.enter_context(nc.Block())

        @block.sync
        def _(sp):
            sp.dma_start(kbb[:, :], I["k_b"].partition_broadcast(P)).then_inc(bias_in, 16)
            sp.dma_start(vbb[:, :], I["v_b"].partition_broadcast(P)).then_inc(bias_in, 16)
            sp.dma_start(gb[:, :], I["biases"].partition_broadcast(P)).then_inc(bias_in, 16)
            sp.wait_ge(wt_sb, 4)
            sp.dma_start(S.wscr, wT[:, :]).then_inc(wt_out, 16)
            sp.wait_ge(wt_out, 16)

        @block.tensor
        def _(pe):
            for b in range(NB):
                cols = slice(b * TB, (b + 1) * TB)
                mm3(pe, pss[b][0:EXPERTS, :], [(w("g", c), (xTh[:, c, cols], xTl[:, c, cols])) for c in range(NC)]
                    ).then_inc(logit_ready, 1)

            def sums_of(t):
                pe.wait_ge(kp_ready, t + 1)
                pe.wait_ge(v_ready, t + 1)
                for g in range(NC):
                    first = t == 0 and g == 0
                    pe.matmul(pss[4][:, g * P:(g + 1) * P], kp[:, t % 2, g * P:(g + 1) * P],
                              vv[:, t % 2, g * P:(g + 1) * P], start=first, stop=t == NT - 1,
                              skip_group_check=True)
                    last = pe.matmul(pss[5][:, 2 * g:2 * g + 2], kp[:, t % 2, g * P:(g + 1) * P],
                                     G.ones[:, 0:2], start=first, stop=t == NT - 1, skip_group_check=True)
                last.then_inc(kv_done, 1)

            for t in range(NT):
                if t < 2:
                    pe.wait_ge(p1, NB)
                else:
                    pe.wait_ge(kx_ready, t - 1)
                mm3(pe, pss[t % 2][:, :], [(x(t, c), w("k", c)) for c in range(NC)]).then_inc(k_mm, 1)
                if t >= 2:
                    pe.wait_ge(v_ready, t - 1)
                mm3(pe, pss[2 + t % 2][:, :], [(x(t, c), w("v", c)) for c in range(NC)]).then_inc(v_mm, 1)
                if t == 0:
                    for n in range(NT):
                        last = pe.transpose(pss[6][:, n * EXPERTS:(n + 1) * EXPERTS], eT[:, n * P:(n + 1) * P],
                                            G.ident[0:EXPERTS, 0:EXPERTS])
                    last.then_inc(ez_mm, 1)
                if t >= 1:
                    sums_of(t - 1)
                if GATES <= t < GATES + NB:
                    b = t - GATES
                    pe.wait_ge(gate_done, 1)
                    wait(pe, wt_sb, b)
                    for k in range(BT):
                        last = pe.transpose(pss[7][0:EXPERTS, k * P:(k + 1) * P], gw[:, b * BT + k, :], G.ident[:, :])
                    last.then_inc(wt_mm, 1)
            sums_of(NT - 1)

        @block.scalar
        def _(act):
            for b in range(NB):
                act.wait_ge(logit_ready, b + 1)
                act.activation(eT[:, b * TB:(b + 1) * TB], pss[b][0:EXPERTS, :], ACT.Exp, scale=-1.0).then_inc(p1, 1)
            for t in range(NT):
                act.wait_ge(kx_ready, t + 1)
                if t >= 2:
                    act.wait_ge(kp_ready, t - 1)
                act.activation(ke[:, t % 2, :], kx[:, t % 2, :], ACT.Relu, scale=-1.0).then_inc(n_ready, 1)
                act.wait_ge(n_ready, t + 1)
                act.activation(ke[:, t % 2, :], ke[:, t % 2, :], ACT.Exp, scale=-1.0).then_inc(e_ready, 1)
                act.activation(kr[:, t % 2, :], kx[:, t % 2, :], ACT.Relu).then_inc(r_ready, 1)
                if GATES < t <= GATES + NB:
                    g = t - GATES - 1
                    act.wait_ge(wt_mm, g + 1)
                    act.activation(wT[:, g * TB:(g + 1) * TB], pss[7][0:EXPERTS, :], ACT.Copy).then_inc(wt_sb, 1)

        @block.vector
        def _(dve):
            chain = Chain(dve, link)
            dve.wait_ge(bias_in, 48)

            def gates():
                dve.wait_ge(ez_mm, 1)
                chain.done(dve.tensor_scalar_add(gz[:, :, :], pss[6][:, 0:NT * EXPERTS].rearrange(
                    "p (t e) -> p t e", t=NT), 1.0))
                chain.done(dve.reciprocal(gp[:, :, :], gz[:, :, :]))
                chain.done(dve.tensor_tensor(gbias[:, :, :], gp[:, :, :],
                                             gb[:, :].unsqueeze(1).to_broadcast([P, NT, EXPERTS]), ALU.add))
                for t in range(NT):
                    last = dve.max(top[:, t, :], gbias[:, t, :])
                chain.done(last)
                for t in range(NT):
                    last = dve.match_replace(grep[:, t, :], top[:, t, :], gbias[:, t, :], NEG)
                chain.done(last)
                chain.done(dve.tensor_tensor(grep[:, :, :], grep[:, :, :], gbias[:, :, :], ALU.not_equal))
                chain.done(dve.tensor_tensor(gw[:, :, :], gp[:, :, :], grep[:, :, :], ALU.mult))
                chain.done(dve.reduce_sum(gsum[:, :], gw[:, :, :], axis=AX))
                chain.done(dve.reciprocal(ginv[:, :], gsum[:, :]))
                chain.done(dve.tensor_scalar(ginv[:, :], ginv[:, :], ROUTE_SCALE, None, ALU.mult))
                dve.tensor_tensor(gw[:, :, :], gw[:, :, :], ginv[:, :].unsqueeze(2).to_broadcast([P, NT, EXPERTS]),
                                  ALU.mult).then_inc(gate_done, 1)

            for t in range(NT):
                dve.wait_ge(k_mm, t + 1)
                if t >= 2:
                    dve.wait_ge(r_ready, t - 1)
                dve.tensor_tensor(kx[:, t % 2, :], pss[t % 2][:, :], kbb[:, :], ALU.add).then_inc(kx_ready, 1)
                dve.wait_ge(v_mm, t + 1)
                if t >= 2:
                    dve.wait_ge(kv_done, t - 1)
                dve.tensor_tensor(vv[:, t % 2, :], pss[2 + t % 2][:, :], vbb[:, :], ALU.add).then_inc(v_ready, 1)
                dve.wait_ge(e_ready, t + 1)
                dve.wait_ge(r_ready, t + 1)
                dve.tensor_tensor(kp[:, t % 2, :], ke[:, t % 2, :], kr[:, t % 2, :], ALU.add).then_inc(kp_ready, 1)
                if t == 2:
                    gates()
            dve.wait_ge(kv_done, NT)
            for g in range(NC):
                dve.tensor_tensor(G.kvb[:, g, :], pss[4][:, g * P:(g + 1) * P], G.headmask[:, :], ALU.mult)
            for g in range(NC):
                for j in range(P // HD):
                    rows = slice(j * HD, (j + 1) * HD)
                    h = g * (P // HD) + j
                    last = dve.tensor_copy(G.ksb[rows, g, h:h + 1], pss[5][rows, 2 * g:2 * g + 1])
            last.then_inc(sums, 1)
            dve.wait_ge(sums, 1)


def wait(eng, sem, value):
    if not isinstance(value, int) or value > 0:
        eng.wait_ge(sem, value)


def looped(eng, iterations, body):
    body(0, True, False)
    with eng.Fori(1, iterations - 1) as i:
        body(i, False, False)
    body(iterations - 1, False, True)


def stage_experts(nc, G, I, S):
    xl_mm, xl_hi, xl_lo = (G.sem("ex_" + n) for n in ("xl_mm", "xl_hi", "xl_lo"))
    w_in, wb_in = ([G.sem(f"ex_{n}{k}") for k in range(2)] for n in ("w_in", "wb_in"))
    w_hi, w_lo, g_mm, u_mm, r_done, rw_done = (G.sem("ex_" + n) for n in
                                              ("w_hi", "w_lo", "g_mm", "u_mm", "relu", "rw"))
    t_done, h_done, hh_done, hl_done, down_done = (G.sem("ex_" + n) for n in ("t", "h", "hh", "hl", "down"))
    acc_hi, acc_lo = G.sem("ex_acc_hi"), G.sem("ex_acc_lo")
    U = 2 * NB
    W = 2 * HID + 2 * LAT
    RING = 4
    LATE = 3
    with ExitStack() as stack:
        M = Memory(nc, stack, "ex_")
        xlh, xll = M.sb("xlh", [P, T], F32R), M.sb("xll", [P, T], F32R)
        wdh, wdl = M.sb("wdh", [P, NC * LAT], F32R), M.sb("wdl", [P, NC * LAT], F32R)
        weights = SplitWeights(G, M, "exw_", [(wdh[:, :], wdl[:, :], I["wdT"].rearrange("(c p) n -> p c n", p=P))])
        queries = SplitWeights(G, M, "atw_", [(G.wqh[:, :], G.wql[:, :], I["qT"].rearrange("(c p) n -> p c n", p=P))],
                               cols=D)
        ws = M.sb("ws", [P, 2, W])
        wh, wl = M.sb("wh", [P, 2, W], F32R), M.sb("wl", [P, 2, W], F32R)
        wb = M.sb("wb", [P, 2, T])
        r, rw, tt, h = (M.sb(n, [P, 2, TB]) for n in ("r", "rw", "t", "h"))
        hh, hl = M.sb("hh", [P, RING, TB], F32R), M.sb("hl", [P, RING, TB], F32R)
        block = stack.enter_context(nc.Block())
        acc = [G.ps[b] for b in range(NB)]
        gate = [G.ps[NB + k] for k in range(2)]
        up = [G.ps[NB + 2 + k] for k in range(2)]

        def where(k):
            return k // U, (k % U) // 2, k % 2

        @block.sync
        def _(sp):
            weights.load(sp)
            def load(e, par, early):
                if not early:
                    sp.wait_ge(w_lo, e - 1)
                sp.dma_start(ws[:, par, :], I["ew"][bass.ds(e, 1), :, :].rearrange("a p n -> (a p) n")
                             ).then_inc(w_in[par], 16)
                if not early:
                    sp.wait_ge(rw_done, (e - 1) * U)
                sp.dma_start(wb[:, par, :], S.wscr[bass.ds(e, 1), :].rearrange("a n -> (a n)").partition_broadcast(P)
                             ).then_inc(wb_in[par], 16)

            load(0, 0, True)
            load(1, 1, True)
            with sp.Fori(1, EXPERTS // 2) as i:
                for par in range(2):
                    load(i * 2 + par, par, False)
            queries.load(sp)

        @block.tensor
        def _(pe):
            weights.ready(pe, 0)
            for b in range(NB):
                cols = slice(b * TB, (b + 1) * TB)
                mm3(pe, acc[b][:, :], [((wdh[:, c * LAT:(c + 1) * LAT], wdl[:, c * LAT:(c + 1) * LAT]),
                                        (G.xTh[:, c, cols], G.xTl[:, c, cols])) for c in range(NC)]
                    ).then_inc(xl_mm, 1)
            pe.wait_ge(xl_lo, NB)

            def w(par, col):
                return wh[:, par, col:col + P], wl[:, par, col:col + P]

            def xl(b):
                return xlh[:, b * TB:(b + 1) * TB], xll[:, b * TB:(b + 1) * TB]

            def gates(i, k):
                n = i * 2 * U + k
                par, b, half = where(k % (2 * U))
                if k % U == 0:
                    wait(pe, w_lo, i * 2 + k // U + 1)
                wait(pe, r_done, n - 1)
                mm3(pe, gate[k % 2][:, :], [(w(par, HID + half * P), xl(b))]).then_inc(g_mm, 1)

            def ups(i, k):
                n = i * 2 * U + k
                par, b, half = where(k)
                wait(pe, h_done, n - 1)
                mm3(pe, up[k % 2][:, :], [(w(par, half * P), xl(b))]).then_inc(u_mm, 1)

            def downs(i, k, first, last):
                n = i * 2 * U + k
                par, b, half = where(k % (2 * U))
                wait(pe, hl_done, n + 1)
                s = k % RING
                mm3(pe, acc[b][:, :], [(w(par, 2 * HID + half * P), (hh[:, s, :], hl[:, s, :]))],
                    start=first and 0 <= k < U and half == 0, stop=last and k >= U and half == 1,
                    skip_group_check=True).then_inc(down_done, 1)

            gates(0, 0)
            gates(0, 1)

            def body(i, first, last):
                for k in range(2 * U):
                    if not (last and k >= 2 * U - 2):
                        gates(i, k + 2)
                    ups(i, k)
                    if not (first and k < LATE):
                        downs(i, k - LATE, first, last)

            looped(pe, EXPERTS // 2, body)
            for k in range(2 * U - LATE, 2 * U):
                downs(EXPERTS // 2 - 1, k, False, True)

        @block.scalar
        def _(act):
            weights.high(act)
            for b in range(NB):
                act.wait_ge(xl_mm, b + 1)
                act.activation(xlh[:, b * TB:(b + 1) * TB], acc[b][:, :], ACT.Copy).then_inc(xl_hi, 1)

            def split(i, e):
                n = i * 2 + e
                act.wait_ge(w_in[e % 2], i * 16 + 16 * (e // 2) + 16)
                wait(act, down_done, (n - 1) * U)
                act.activation(wh[:, e % 2, :], ws[:, e % 2, :], ACT.Copy).then_inc(w_hi, 1)

            def relu(i, k):
                n = i * 2 * U + k
                act.wait_ge(g_mm, n + 1)
                wait(act, t_done, n - 1)
                act.activation(r[:, k % 2, :], gate[k % 2][:, :], ACT.Relu).then_inc(r_done, 1)

            def high(i, k):
                n = i * 2 * U + k
                act.wait_ge(h_done, n + 1)
                wait(act, down_done, n - RING + 1)
                act.activation(hh[:, k % RING, :], h[:, k % 2, :], ACT.Copy).then_inc(hh_done, 1)

            split(0, 0)
            relu(0, 0)
            relu(0, 1)

            def body(i, first, last):
                for k in range(2 * U):
                    if not (last and k >= 2 * U - 2):
                        relu(i, k + 2)
                    high(i, k)
                    if k % U == 3 and not (last and k > U):
                        split(i, k // U + 1)
                    if last and k < len(queries.pieces):
                        queries.high(act, k, k + 1)

            looped(act, EXPERTS // 2, body)
            for b in range(NB):
                act.wait_ge(down_done, EXPERTS * U)
                act.activation(G.acch[:, b * TB:(b + 1) * TB], acc[b][:, :], ACT.Copy).then_inc(acc_hi, 1)

        @block.gpsimd
        def _(pool):
            def split(i, e):
                n = i * 2 + e
                pool.wait_ge(w_hi, n + 1)
                pool.tensor_tensor(wl[:, e % 2, :], ws[:, e % 2, :], raw(wh[:, e % 2, :]), ALU.subtract).then_inc(w_lo, 1)

            def weigh(i, k):
                n = i * 2 * U + k
                par, b, half = where(k)
                if k % U == 0:
                    pool.wait_ge(wb_in[par], i * 16 + 16)
                pool.wait_ge(r_done, n + 1)
                wait(pool, t_done, n - 1)
                pool.tensor_tensor(rw[:, k % 2, :], r[:, k % 2, :], wb[:, par, b * TB:(b + 1) * TB],
                                   ALU.mult).then_inc(rw_done, 1)

            split(0, 0)

            def body(i, first, last):
                for k in range(2 * U):
                    weigh(i, k)
                    if k % U == 4 and not (last and k > U):
                        split(i, k // U + 1)

            looped(pool, EXPERTS // 2, body)

        @block.vector
        def _(dve):
            weights.low(dve)
            for b in range(NB):
                cols = slice(b * TB, (b + 1) * TB)
                dve.wait_ge(xl_hi, b + 1)
                dve.tensor_tensor(xll[:, cols], acc[b][:, :], raw(xlh[:, cols]), ALU.subtract).then_inc(xl_lo, 1)

            def square(i, k):
                n = i * 2 * U + k
                dve.wait_ge(rw_done, n + 1)
                wait(dve, h_done, n - 1)
                dve.tensor_tensor(tt[:, k % 2, :], r[:, k % 2, :], rw[:, k % 2, :], ALU.mult).then_inc(t_done, 1)

            def hidden(i, k):
                n = i * 2 * U + k
                dve.wait_ge(u_mm, n + 1)
                dve.wait_ge(t_done, n + 1)
                wait(dve, hl_done, n - 1)
                dve.tensor_tensor(h[:, k % 2, :], up[k % 2][:, :], tt[:, k % 2, :], ALU.mult).then_inc(h_done, 1)

            def low(i, k):
                n = i * 2 * U + k
                dve.wait_ge(hh_done, n + 1)
                wait(dve, down_done, n - RING + 1)
                dve.tensor_tensor(hl[:, k % RING, :], h[:, k % 2, :], raw(hh[:, k % RING, :]), ALU.subtract
                                  ).then_inc(hl_done, 1)

            square(0, 0)

            def body(i, first, last):
                for k in range(2 * U):
                    hidden(i, k)
                    if not (last and k == 2 * U - 1):
                        square(i, k + 1)
                    low(i, k)
                    if last and k < len(queries.pieces):
                        queries.low(dve, k, k + 1)

            looped(dve, EXPERTS // 2, body)
            for b in range(NB):
                cols = slice(b * TB, (b + 1) * TB)
                dve.wait_ge(acc_hi, b + 1)
                dve.tensor_tensor(G.accl[:, cols], acc[b][:, :], raw(G.acch[:, cols]), ALU.subtract).then_inc(acc_lo, 1)


def stage_attend0(nc, G, I):
    q_mm, e_done, r_done, qp_done, z_mm, zi_done, zs_mm, zs_sb, a_mm, at_done, link, b_in = (
        G.sem("at_" + n) for n in ("q_mm", "e", "r", "qp", "z_mm", "zi", "zs_mm", "zs_sb", "a_mm", "at", "link", "b_in"))
    n_done, nqb_done = G.sem("at_n"), G.sem("at_nqb")
    with ExitStack() as stack:
        M = Memory(nc, stack, "at_")
        qh, ql = G.wqh, G.wql
        weights = SplitWeights(G, M, "o0s_", [
            (h[:, :], l[:, :], I[n + "T"].rearrange("(c p) n -> p c n", p=P))
            for n, (h, l) in (("sw1", G.sw["sw1"]), ("swg", G.sw["swg"]), ("o", (qh, ql)))], cols=D)
        shared = weights.upto[1]
        each = -(-shared // (NB - 1))
        cuts = [min(b * each, shared) for b in range(NB)] + [len(weights.pieces)]
        qb, nqb = M.sb("qb", [P, NC]), M.sb("nqb", [P, NC])
        e, r, qp = M.sb("e", [P, 2, TB]), M.sb("r", [P, 2, TB]), M.sb("qp", [P, 2 * NC, TB])
        zi, zs = M.sb("zi", [H0, TB]), M.sb("zs", [P, 2, TB])
        zh, zl = M.sb("zh", [P, 2, TB], F32R), M.sb("zl", [P, 2, TB], F32R)
        zz = M.sb("zz", [P, TB])
        block = stack.enter_context(nc.Block())
        UN = NB * NC

        @block.sync
        def _(sp):
            sp.dma_start(qb[:, :], I["q_b"]).then_inc(b_in, 16)
            weights.load(sp)

        @block.tensor
        def _(pe):
            def queries(b, groups):
                cols = slice(b * TB, (b + 1) * TB)
                for g in groups:
                    n = b * NC + g
                    wait(pe, e_done, n - 1)
                    wait(pe, r_done, n - 1)
                    mm3(pe, G.ps[n % 2][:, :], [((qh[:, c * D + g * P:c * D + (g + 1) * P], ql[:, c * D + g * P:c * D + (g + 1) * P]),
                                                 (G.xTh[:, c, cols], G.xTl[:, c, cols])) for c in range(NC)]).then_inc(q_mm, 1)

            def sums(b):
                wait(pe, zi_done, b - 1)
                for g in range(NC):
                    n = b * NC + g
                    pe.wait_ge(qp_done, n + 1)
                    last = pe.matmul(G.ps[6 + b % 2][0:H0, :], G.ksb[:, g, :], qp[:, n % (2 * NC), :],
                                     start=g == 0, stop=g == NC - 1)
                last.then_inc(z_mm, 1)

            def attend(b):
                for g in range(NC):
                    n = b * NC + g
                    wait(pe, at_done, n - 1)
                    pe.matmul(G.ps[2 + n % 2][:, :], G.kvb[:, g, :], qp[:, n % (2 * NC), :],
                              start=True, stop=True).then_inc(a_mm, 1)
                    if g == 0:
                        pe.wait_ge(zi_done, b + 1)
                    wait(pe, zs_sb, n - 1)
                    for m, z in enumerate((zh, zl)):
                        last = pe.matmul(G.ps[4 + n % 2][:, :], G.headsel[:, g, :], z[:, b % 2, :],
                                         start=m == 0, stop=m == 1)
                    last.then_inc(zs_mm, 1)

            queries(0, range(NC))
            for b in range(NB):
                if b + 1 < NB:
                    queries(b + 1, range(2))
                sums(b)
                if b + 1 < NB:
                    queries(b + 1, range(2, NC))
                attend(b)

        @block.scalar
        def _(act):
            act.wait_ge(b_in, 16)
            act.mul(nqb[:, :], qb[:, :], -1.0).then_inc(nqb_done, 1)
            act.wait_ge(nqb_done, 1)
            def features(b):
                for g in range(NC):
                    n = b * NC + g
                    act.wait_ge(q_mm, n + 1)
                    wait(act, qp_done, n - 1)
                    act.activation(e[:, n % 2, :], G.ps[n % 2][:, :], ACT.Relu, bias=nqb[:, g:g + 1],
                                   scale=-1.0).then_inc(n_done, 1)
                    act.wait_ge(n_done, n + 1)
                    act.activation(e[:, n % 2, :], e[:, n % 2, :], ACT.Exp, scale=-1.0).then_inc(e_done, 1)
                    act.activation(r[:, n % 2, :], G.ps[n % 2][:, :], ACT.Relu, bias=qb[:, g:g + 1]).then_inc(r_done, 1)

            features(0)
            for b in range(NB):
                if b + 1 < NB:
                    features(b + 1)
                if b == NB - 1:
                    act.wait_ge(q_mm, NB * NC)
                    weights.high(act, cuts[b], cuts[b + 1])
                for g in range(NC):
                    n = b * NC + g
                    act.wait_ge(zs_mm, n + 1)
                    wait(act, at_done, n - 1)
                    act.activation(zs[:, n % 2, :], G.ps[4 + n % 2][:, :], ACT.Copy).then_inc(zs_sb, 1)
                if b < NB - 1:
                    weights.high(act, cuts[b], cuts[b + 1])

        @block.vector
        def _(dve):
            chain = Chain(dve, link)
            chain.done(dve.memset(zz[:, :], 0.0))
            for s in range(2):
                dve.tensor_copy(zh[:, s, :], zz[:, :])
                last = dve.tensor_copy(zl[:, s, :], zz[:, :])
            chain.done(last)
            def features(b, groups):
                for g in groups:
                    n = b * NC + g
                    dve.wait_ge(e_done, n + 1)
                    dve.wait_ge(r_done, n + 1)
                    wait(dve, a_mm, n - 2 * NC + 1)
                    dve.tensor_tensor(qp[:, n % (2 * NC), :], e[:, n % 2, :], r[:, n % 2, :], ALU.add).then_inc(qp_done, 1)

            features(0, range(NC))
            for b in range(NB):
                if b + 1 < NB:
                    features(b + 1, range(2))
                dve.wait_ge(z_mm, b + 1)
                wait(dve, zs_mm, (b - 1) * NC)
                chain.done(dve.tensor_scalar_add(zi[:, :], G.ps[6 + b % 2][0:H0, :], RMS_EPS))
                chain.done(dve.reciprocal(zi[:, :], zi[:, :]))
                chain.done(dve.tensor_copy(zh[0:H0, b % 2, :], zi[:, :]))
                dve.tensor_tensor(zl[0:H0, b % 2, :], zi[:, :], raw(zh[0:H0, b % 2, :]),
                                  ALU.subtract).then_inc(zi_done, 1)
                if b + 1 < NB:
                    features(b + 1, range(2, NC))
                else:
                    weights.low(dve, cuts[b], cuts[b + 1])
                for g in range(NC):
                    n = b * NC + g
                    dve.wait_ge(a_mm, n + 1)
                    dve.wait_ge(zs_sb, n + 1)
                    dve.tensor_tensor(G.X[:, n, :], G.ps[2 + n % 2][:, :], zs[:, n % 2, :], ALU.mult).then_inc(at_done, 1)
                if b < NB - 1:
                    weights.low(dve, cuts[b], cuts[b + 1])


def stage_output0(nc, G, I, S):
    names = ("u_mm", "r", "t", "h", "hh", "hl", "ath", "atl", "o_mm", "x1")
    u_mm, r_done, t_done, h_done, hh_done, hl_done, ath_done, atl_done, o_mm, x1_done = (G.sem("o0_" + n) for n in names)
    x_in = [G.sem(f"o0_x_in{n}") for n in range(2)]
    xb_done, b_in = G.sem("o0_xb"), G.sem("o0_b_in")
    var_ready, sd_ready, rstd_ready, xn_ready, xt_ready, hi_ready, lo_ready, res_ready, link = (
        G.sem("b_" + n) for n in ("var", "sd", "rstd", "xn", "xt", "hi", "lo", "res", "link"))
    wr_in, wrh_done, wr_done, sc_mm, row_sb, pair_mm, pair_sb, r_stored = (G.sem("b_" + n) for n in (
        "wr_in", "wrh", "wr", "sc_mm", "row_sb", "pair_mm", "pair_sb", "r_stored"))
    RING = 3
    xn_stored = [G.sem(f"b_xn_stored{n}") for n in range(RING)]
    row_stored = [G.sem(f"b_row_stored{n}") for n in range(2)]
    with ExitStack() as stack:
        M = Memory(nc, stack, "o0_")
        w = dict(G.sw, o=(G.wqh, G.wql))
        jobs = []
        for name, src, cols in (("sw2", "sw2T", 2 * D), ("up", "wupT", D)):
            w[name] = (M.sb(name + "h", [P, cols], F32R), M.sb(name + "l", [P, cols], F32R))
            jobs.append((w[name][0][:, :], w[name][1][:, :], I[src].rearrange("(c p) n -> p c n", p=P)))
        weights = SplitWeights(G, M, "o0w_", jobs, cols=D)
        ob = M.sb("ob", [P, D])
        ath, atl = M.sb("ath", [P, NC, TB], F32R), M.sb("atl", [P, NC, TB], F32R)
        hsh, hsl = M.sb("hsh", [P, 2, TB], F32R), M.sb("hsl", [P, 2, TB], F32R)
        r = G.kvb[:, :, :].rearrange("p g n -> p (g n)")
        xr = M.sb("xr", [P, 2, D])
        stats, mv = M.sb("stats", [P, BT, 6]), M.sb("mv", [P, BT, 2])
        ve, sd, rstd, shift = (M.sb(n, [P, BT]) for n in ("ve", "sd", "rstd", "shift"))
        xn, row = M.sb("xn", [P, RING, D]), M.sb("row", [2, 2, TB])
        wr, wrh, wrl = M.sb("wr", [P, NC]), M.sb("wrh", [P, NC, 2], F32R), M.sb("wrl", [P, NC, 2], F32R)
        block = stack.enter_context(nc.Block())

        def cut(name, width, c, col, n):
            a = c * width + col
            return w[name][0][:, a:a + n], w[name][1][:, a:a + n]

        def in_turn(b, tile, norm):
            for k in range(BT):
                if b < NB:
                    tile(b * BT + k)
                if b >= 1:
                    norm((b - 1) * BT + k)

        @block.sync
        def _(sp):
            weights.load(sp)
            sp.dma_start(ob[:, :], I["o_b"].partition_broadcast(P)).then_inc(b_in, 16)
            sp.dma_start(wr[:, :], I["w_router"]).then_inc(wr_in, 16)

            def load_x(t):
                wait(sp, x1_done, t - 1)
                sp.dma_start(xr[:, t % 2, :], I["x"][t * P:(t + 1) * P, :]).then_inc(x_in[t % 2], 16)

            def store(t):
                sp.wait_ge(xn_ready, t + 1)
                sp.dma_start(S.xn[t * P:(t + 1) * P, :], xn[:, t % RING, :]).then_inc(xn_stored[t % RING], 16)
                sp.wait_ge(res_ready, t + 1)
                sp.dma_start(S.r[t * P:(t + 1) * P, :], G.X[:, t, :]).then_inc(r_stored, 16)

            def store_scores(b):
                sp.wait_ge(row_sb, b + 1)
                sp.dma_start(S.score[b * TB:(b + 1) * TB].unsqueeze(0), row[0:1, b % 2, :]).then_inc(row_stored[b % 2], 16)

            for b in range(NB + 1):
                in_turn(b, load_x, store)
                if b >= 2:
                    store_scores(b - 2)
            store_scores(NB - 1)
            sp.wait_ge(r_stored, NT * 16)
            for n in range(RING):
                sp.wait_ge(xn_stored[n], 16 * len(range(n, NT, RING)))
            for n in range(2):
                sp.wait_ge(row_stored[n], 16 * NB // 2)

        @block.gpsimd
        def _(pool):
            pool.wait_ge(b_in, 16)

            def biased(t):
                pool.wait_ge(x_in[t % 2], 16 * (t // 2 + 1))
                pool.tensor_tensor(xr[:, t % 2, :], xr[:, t % 2, :], ob[:, :], ALU.add).then_inc(xb_done, 1)

            def residual(t):
                pool.wait_ge(xn_ready, t + 1)
                pool.tensor_tensor(G.X[:, t, :], G.X[:, t, :], xn[:, t % RING, :], ALU.add).then_inc(res_ready, 1)

            for b in range(NB + 1):
                in_turn(b, biased, residual)

        @block.tensor
        def _(pe):
            def shared(b):
                cols = slice(b * TB, (b + 1) * TB)
                for half in range(2):
                    n = 2 * b + half
                    wait(pe, h_done, n - 1)
                    for k, name in enumerate(("swg", "sw1")):
                        mm3(pe, G.ps[2 * (n % 2) + k][:, :], [(cut(name, HID, c, half * P, P), (G.xTh[:, c, cols], G.xTl[:, c, cols]))
                                                              for c in range(NC)]).then_inc(u_mm, 1)

            def output(t):
                b, k = t // BT, t % BT
                if k == 0:
                    pe.wait_ge(atl_done, (b + 1) * NC)
                    pe.wait_ge(hl_done, 2 * (b + 1))
                wait(pe, x1_done, t - 1)
                rows = slice(k * P, (k + 1) * P)
                parts = [((ath[:, g, rows], atl[:, g, rows]), cut("o", D, g, 0, D)) for g in range(NC)]
                parts += [((hsh[:, c, rows], hsl[:, c, rows]), cut("sw2", D, c, 0, D)) for c in range(2)]
                parts += [((G.acch[:, t * P:(t + 1) * P], G.accl[:, t * P:(t + 1) * P]), cut("up", D, 0, 0, D))]
                mm3(pe, G.ps[4 + t % 2][:, :], parts).then_inc(o_mm, 1)

            def transposes(t):
                pe.wait_ge(xn_ready, t + 1)
                wait(pe, lo_ready, t - 1)
                if t % BT < 2:
                    wait(pe, row_sb, t // BT)
                    wait(pe, pair_sb, t // BT)
                for c in range(NC):
                    last = pe.transpose(G.ps[6 + t % 2][:, c * P:(c + 1) * P], xn[:, t % RING, c * P:(c + 1) * P],
                                        G.ident[:, :])
                last.then_inc(xt_ready, 1)

            def scores(b):
                if b == 0:
                    pe.wait_ge(wr_done, 1)
                pe.wait_ge(lo_ready, (b + 1) * BT)
                cols = slice(b * TB, (b + 1) * TB)
                mm3(pe, G.ps[6][0:2, :], [((wrh[:, c, :], wrl[:, c, :]), (G.xTh[:, c, cols], G.xTl[:, c, cols]))
                                          for c in range(NC)]).then_inc(sc_mm, 1)
                pe.wait_ge(row_sb, b + 1)
                for k in range(BT):
                    last = pe.transpose(G.ps[7][:, 2 * k:2 * k + 2], row[:, b % 2, k * P:(k + 1) * P], G.ident[0:2, 0:2])
                last.then_inc(pair_mm, 1)

            shared(0)
            for b in range(NB + 1):
                if b + 1 < NB:
                    shared(b + 1)
                if b == 0:
                    weights.ready(pe, 1)
                in_turn(b, output, transposes)
                if b >= 1:
                    scores(b - 1)

        @block.scalar
        def _(act):
            weights.high(act)

            def normal(t):
                wait(act, xt_ready, t - RING + 1)
                wait(act, res_ready, t - RING + 1)
                if t >= RING:
                    act.wait_ge(xn_stored[t % RING], 16 * (t // RING))
                k = t % BT
                act.activation(xn[:, t % RING, :], G.X[:, t, :], ACT.Identity, bias=shift[:, k:k + 1],
                               scale=rstd[:, k:k + 1]).then_inc(xn_ready, 1)

            def high(t):
                act.wait_ge(xt_ready, t + 1)
                act.activation(G.xTh[:, :, t * P:(t + 1) * P], G.ps[6 + t % 2].rearrange("p (c n) -> p c n", c=NC),
                               ACT.Copy).then_inc(hi_ready, 1)

            for b in range(NB + 1):
                if b < NB:
                    for half in range(2):
                        n = 2 * b + half
                        act.wait_ge(u_mm, 2 * n + 1)
                        wait(act, hl_done, n)
                        act.activation(r, G.ps[2 * (n % 2)][:, :], ACT.Relu).then_inc(r_done, 1)
                        wait(act, o_mm, b * BT)
                        for g in (2 * half, 2 * half + 1):
                            act.activation(ath[:, g, :], G.X[:, b * NC + g, :], ACT.Copy).then_inc(ath_done, 1)
                        act.wait_ge(h_done, n + 1)
                        act.activation(hsh[:, half, :], r, ACT.Copy).then_inc(hh_done, 1)
                if b >= 1:
                    act.wait_ge(rstd_ready, b)
                    act.wait_ge(u_mm, 4 * b)
                    for t in range((b - 1) * BT, b * BT):
                        normal(t)
                        if t % BT:
                            high(t - 1)
                    high(b * BT - 1)
                if b < NB:
                    act.wait_ge(var_ready, b + 1)
                    act.activation(sd[:, :], ve[:, :], ACT.Sqrt).then_inc(sd_ready, 1)
                if b >= 1:
                    act.wait_ge(sc_mm, b)
                    if b >= 3:
                        act.wait_ge(row_stored[(b - 1) % 2], 16 * ((b - 1) // 2))
                    act.activation(row[:, (b - 1) % 2, :], G.ps[6][0:2, :], ACT.Copy).then_inc(row_sb, 1)

        @block.vector
        def _(dve):
            weights.low(dve)
            chain = Chain(dve, link)
            dve.wait_ge(wr_in, 16)
            for n in range(2):
                last = dve.tensor_copy(wrh[:, :, n:n + 1], wr[:, :].unsqueeze(2))
            last.then_inc(wrh_done, 1)
            dve.wait_ge(wrh_done, 1)
            for n in range(2):
                last = dve.tensor_tensor(wrl[:, :, n:n + 1], wr[:, :].unsqueeze(2), raw(wrh[:, :, n:n + 1]), ALU.subtract)
            last.then_inc(wr_done, 1)

            def total(t):
                dve.wait_ge(o_mm, t + 1)
                dve.wait_ge(xb_done, t + 1)
                dve.tensor_tensor(G.X[:, t, :], G.ps[4 + t % 2][:, :], xr[:, t % 2, :], ALU.add).then_inc(x1_done, 1)

            def low(t):
                dve.wait_ge(hi_ready, t + 1)
                cols = slice(t * P, (t + 1) * P)
                dve.tensor_tensor(G.xTl[:, :, cols], G.ps[6 + t % 2].rearrange("p (c n) -> p c n", c=NC),
                                  raw(G.xTh[:, :, cols]), ALU.subtract).then_inc(lo_ready, 1)

            def score_columns(b):
                dve.wait_ge(pair_mm, b + 1)
                dve.tensor_copy(G.score[:, b * BT:(b + 1) * BT], G.ps[7][:, 0:2 * BT].rearrange(
                    "p (t n) -> p t n", n=2)[:, :, 0]).then_inc(pair_sb, 1)

            for b in range(NB + 1):
                if b < NB:
                    for half in range(2):
                        n = 2 * b + half
                        dve.wait_ge(r_done, n + 1)
                        dve.tensor_tensor(r, r, r, ALU.mult).then_inc(t_done, 1)
                        dve.wait_ge(t_done, n + 1)
                        dve.wait_ge(u_mm, 2 * n + 2)
                        dve.tensor_tensor(r, G.ps[2 * (n % 2) + 1][:, :], r, ALU.mult).then_inc(h_done, 1)
                        wait(dve, o_mm, b * BT)
                        for g in (2 * half, 2 * half + 1):
                            dve.wait_ge(ath_done, b * NC + g + 1)
                            dve.tensor_tensor(atl[:, g, :], G.X[:, b * NC + g, :], raw(ath[:, g, :]), ALU.subtract).then_inc(atl_done, 1)
                        dve.wait_ge(hh_done, n + 1)
                        dve.tensor_tensor(hsl[:, half, :], r, raw(hsh[:, half, :]), ALU.subtract).then_inc(hl_done, 1)
                    dve.wait_ge(atl_done, (b + 1) * NC)
                if b >= 2:
                    score_columns(b - 2)
                in_turn(b, total, low)
                if b < NB:
                    dve.wait_ge(x1_done, (b + 1) * BT)
                    for k in range(BT):
                        last = dve.bn_stats(stats[:, k, :], G.X[:, b * BT + k, :])
                    chain.done(last)
                    for k in range(BT):
                        last = dve.bn_aggr(mv[:, k, :], stats[:, k, :])
                    chain.done(last)
                    dve.tensor_scalar_add(ve[:, :], mv[:, :, 1], LN_EPS).then_inc(var_ready, 1)
                    wait(dve, xn_ready, b * BT)
                    dve.wait_ge(sd_ready, b + 1)
                    chain.done(dve.reciprocal(rstd[:, :], sd[:, :]))
                    dve.scalar_tensor_tensor(shift[:, :], mv[:, :, 0], -1.0, rstd[:, :], ALU.mult, ALU.mult
                                             ).then_inc(rstd_ready, 1)
            score_columns(NB - 1)
            dve.wait_ge(pair_sb, NB)


def stage_qkv(nc, G, I, S):
    names = ("qk_mm", "v_mm", "sq", "ms", "sd", "qn", "t1", "t2", "y", "yt_mm", "hh", "hl", "v_sb", "link", "tables", "ones")
    qk_mm, v_mm, sq_done, ms_done, sd_done, qn_done, t1_done, t2_done, y_done, yt_mm, hh_done, hl_done, v_sb, link, tables, ones_done = (
        G.sem("qkv_" + n) for n in names)
    tab_in = G.sem("qkv_tab_in")
    qk_out, v_out = ([G.sem(f"qkv_{n}{k}") for k in range(2)] for n in ("qk_out", "v_out"))
    with ExitStack() as stack:
        M = Memory(nc, stack, "qkv_")
        w = {n: (M.sb(n + "h", [P, NC * D], F32R), M.sb(n + "l", [P, NC * D], F32R)) for n in "qkv"}
        weights = SplitWeights(G, M, "qkvw_", [
            (w[n][0][:, :], w[n][1][:, :], I["w_qkv"][:, k * D:(k + 1) * D].rearrange("(c p) n -> p c n", p=P))
            for k, n in enumerate("qkv")])
        cs = [M.sb("cos", [P, NT, HD]), M.sb("sin", [P, NT, HD])]
        gam = M.sb("gam", [P, 2, 2, HD])
        tab = M.sb("tab", [P, 2, 2, NT, HD])
        sq = M.sb("sq", [P, 2, D])
        ms, sd, rs = (M.sb(n, [P, 2, H0]) for n in ("ms", "sd", "rs"))
        qn, t1, t2 = (M.sb(n, [P, 2, D]) for n in ("qn", "t1", "t2"))
        yh, yl = M.sb("yh", [P, 2, 2, NC, P], F32R), M.sb("yl", [P, 2, 2, NC, P], F32R)
        vs = M.sb("vs", [P, 2, H0, 2 * HD])
        block = stack.enter_context(nc.Block())

        @block.sync
        def _(sp):
            weights.load(sp)
            for k, n in enumerate(("cos32", "sin32")):
                sp.dma_start(cs[k][:, :, :], I[n].rearrange("(t p) d -> p t d", p=P)).then_inc(tab_in, 16)
            for k, n in enumerate(("q_gamma", "k_gamma")):
                for m in range(2):
                    sp.dma_start(gam[:, k, m, :], I[n][m, :].partition_broadcast(P)).then_inc(tab_in, 16)
            for t in range(NT):
                rows = slice(t * P, (t + 1) * P)
                sp.wait_ge(v_sb, t + 1)
                sp.dma_start(S.v[:, :, t, :].rearrange("r p n -> p r n"),
                             vs[:, t % 2, :, :].rearrange("p (r h) n -> p r (h n)", h=2)).then_inc(v_out[t % 2], 16)
                sp.wait_ge(hl_done, 2 * (t + 1))
                for k in range(2):
                    for part, y in enumerate((yh, yl)):
                        sp.dma_start(S.qk[k, part, :, rows].rearrange("(g p) t -> p g t", p=P),
                                     raw(y[:, t % 2, k, :, :])).then_inc(qk_out[t % 2], 16)
            for k in range(2):
                sp.wait_ge(v_out[k], 16 * NT // 2)
                sp.wait_ge(qk_out[k], 64 * NT // 2)

        @block.tensor
        def _(pe):
            def x(t, c):
                cols = slice(t * P, (t + 1) * P)
                return G.xTh[:, c, cols], G.xTl[:, c, cols]

            def product(t, n, bank):
                return mm3(pe, G.ps[bank], [(x(t, c), (w[n][0][:, c * D:(c + 1) * D], w[n][1][:, c * D:(c + 1) * D]))
                                            for c in range(NC)])

            def transposes(t):
                for k in range(2):
                    pe.wait_ge(y_done, 2 * t + k + 1)
                    wait(pe, hl_done, 2 * (t - 1) + k + 1)
                    for g in range(NC):
                        last = pe.transpose(G.ps[6 + k][:, g * P:(g + 1) * P], t2[:, k, g * P:(g + 1) * P], G.ident[:, :])
                    last.then_inc(yt_mm, 1)

            for t in range(NT):
                for k in range(2):
                    if t == 0:
                        weights.ready(pe, k)
                    wait(pe, qn_done, 2 * (t - 2) + k + 1)
                    product(t, "qk"[k], 2 * (t % 2) + k).then_inc(qk_mm, 1)
                if t >= 1:
                    transposes(t - 1)
                if t == 0:
                    weights.ready(pe, 2)
                wait(pe, v_sb, t - 1)
                product(t, "v", 4 + t % 2).then_inc(v_mm, 1)
            transposes(NT - 1)

        @block.scalar
        def _(act):
            weights.high(act)
            def high(t):
                for k in range(2):
                    act.wait_ge(yt_mm, 2 * t + k + 1)
                    if t >= 2:
                        act.wait_ge(qk_out[t % 2], 64 * (t // 2))
                    act.activation(yh[:, t % 2, k, :, :], G.ps[6 + k].rearrange("p (g n) -> p g n", g=NC),
                                   ACT.Copy).then_inc(hh_done, 1)

            act.wait_ge(ones_done, 1)
            for t in range(NT):
                for k in range(2):
                    act.wait_ge(qk_mm, 2 * t + k + 1)
                    wait(act, ms_done, t)
                    act.activation(sq[:, k, :], G.ps[2 * (t % 2) + k], ACT.Square).then_inc(sq_done, 1)
                act.wait_ge(ms_done, t + 1)
                act.activation(sd[:, :, :], ms[:, :, :], ACT.Sqrt).then_inc(sd_done, 1)
                if t >= 1:
                    high(t - 1)
                act.wait_ge(v_mm, t + 1)
                if t >= 2:
                    act.wait_ge(v_out[t % 2], 16 * (t // 2))
                act.activation(vs[:, t % 2, :, 0:HD], G.ps[4 + t % 2].rearrange("p (h d) -> p h d", h=H0),
                               ACT.Copy).then_inc(v_sb, 1)
            high(NT - 1)

        @block.gpsimd
        def _(pool):
            pool.memset(vs[:, :, :, HD:2 * HD], 1.0).then_inc(ones_done, 1)
            pool.wait_ge(tables, 1)
            for t in range(NT):
                for k in range(2):
                    pool.wait_ge(qn_done, 2 * t + k + 1)
                    wait(pool, y_done, 2 * (t - 1) + k + 1)
                    pool.tensor_tensor(t1[:, k, :].rearrange("p (h d) -> p h d", h=H0),
                                       qn[:, k, :].rearrange("p (h d) -> p h d", h=H0),
                                       tab[:, k, 0, t, :].unsqueeze(1).to_broadcast([P, H0, HD]), ALU.mult).then_inc(t1_done, 1)

        @block.vector
        def _(dve):
            weights.low(dve)
            chain = Chain(dve, link)
            dve.wait_ge(tab_in, 96)
            for k in range(2):
                for m in range(2):
                    last = dve.tensor_tensor(tab[:, k, m, :, :], cs[m][:, :, :],
                                             gam[:, k, m, :].unsqueeze(1).to_broadcast([P, NT, HD]), ALU.mult)
            last.then_inc(tables, 1)
            dve.wait_ge(tables, 1)

            def low(t):
                for k in range(2):
                    dve.wait_ge(hh_done, 2 * t + k + 1)
                    dve.tensor_tensor(yl[:, t % 2, k, :, :], G.ps[6 + k].rearrange("p (g n) -> p g n", g=NC),
                                      raw(yh[:, t % 2, k, :, :]), ALU.subtract).then_inc(hl_done, 1)

            for t in range(NT):
                dve.wait_ge(sq_done, 2 * (t + 1))
                chain.done(dve.reduce_sum(ms[:, :, :], sq[:, :, :].rearrange("p k (h d) -> p k h d", h=H0), axis=AX))
                wait(dve, sd_done, t)
                dve.tensor_scalar(ms[:, :, :], ms[:, :, :], 1.0 / HD, RMS_EPS, ALU.mult, ALU.add).then_inc(ms_done, 1)
                if t >= 1:
                    low(t - 1)
                dve.wait_ge(sd_done, t + 1)
                chain.done(dve.reciprocal(rs[:, :, :], sd[:, :, :]))
                for k in range(2):
                    dve.tensor_tensor(qn[:, k, :].rearrange("p (h d) -> p h d", h=H0),
                                      G.ps[2 * (t % 2) + k].rearrange("p (h d) -> p h d", h=H0),
                                      rs[:, k, :].unsqueeze(2).to_broadcast([P, H0, HD]), ALU.mult).then_inc(qn_done, 1)
                for k in range(2):
                    dve.wait_ge(qn_done, 2 * t + k + 1)
                    wait(dve, yt_mm, 2 * (t - 1) + k + 1)
                    q4 = qn[:, k, :].rearrange("p (h d) -> p h d", h=H0)
                    r4 = t2[:, k, :].rearrange("p (h d) -> p h d", h=H0)
                    half = HD // 2
                    for m in range(2):
                        sin = tab[:, k, 1, t, m * half:(m + 1) * half].unsqueeze(1).to_broadcast([P, H0, half])
                        last = dve.tensor_tensor(r4[:, :, m * half:(m + 1) * half],
                                                 q4[:, :, (1 - m) * half:(2 - m) * half], sin, ALU.mult)
                    last.then_inc(t2_done, 1)
                for k in range(2):
                    dve.wait_ge(t2_done, 2 * t + k + 1)
                    dve.wait_ge(t1_done, 2 * t + k + 1)
                    dve.tensor_tensor(t2[:, k, :], t2[:, k, :], t1[:, k, :], ALU.add).then_inc(y_done, 1)
            low(NT - 1)


class Plan:

    def __init__(self, b):
        back = WINDOW // P
        q0, q1 = b * BT, (b + 1) * BT
        keys = [(kt, max(q0, kt), min(q1 - 1, kt + back)) for kt in range(max(0, q0 - back), q1)]
        self.keys = sorted(keys, key=lambda k: -(k[2] - k[1]))
        self.maxima = []
        for qt in range(q0, q1):
            first = max(0, qt - back)
            count = qt - first + 1
            pieces = -(-count // BT)
            cuts = [first + count * k // pieces for k in range(pieces + 1)]
            self.maxima.append((qt, list(zip(cuts, cuts[1:]))))
        self.chunks = 2 * sum(len(c) for _, c in self.maxima)
        self.back = back


def sums_of(dram, b0, b1):
    n = (b1 - b0) * H0 * TB // P
    return dram[b0:b1].rearrange("b h t -> (b h t)").rearrange("(p n) -> p n", n=n)


def stage_attend1(nc, G, I, S):
    K3 = 3 * HD
    KM = K3 + 2
    plans = [Plan(b) for b in range(NB)]
    PAIRS = H0 // 2
    keys_before = [sum(len(p.keys) for p in plans[:b]) for b in range(NB)]
    KEYS = sum(len(p.keys) for p in plans)
    chunks_before = [sum(p.chunks for p in plans[:b]) for b in range(NB)]
    CHUNKS = sum(p.chunks for p in plans)
    scale = 1.0 / float(np.sqrt(HD))
    s_mm, p_done, av_mm, a_mm, a_red, m_done, mr_mm, mr_sb, o_sb, kones, link = (G.sem("l1_" + n) for n in (
        "s_mm", "p", "av_mm", "a_mm", "a_red", "m", "mr_mm", "mr_sb", "o_sb", "kones", "link"))
    q_in, k_in, v_in = ([G.sem(f"l1_{n}{k}") for k in range(2)] for n in ("q_in", "k_in", "v_in"))
    o_out = [G.sem(f"l1_o_out{k}") for k in range(2)]
    den_in, rden, rden_out = (G.sem("l1_" + n) for n in ("den_in", "rden", "rden_out"))
    first_in = [G.sem(f"l1_first_in{b}") for b in range(NB)]
    nm_done, mh_done = G.sem("l1_nm"), G.sem("l1_mh")
    sr_in, iota_done, se_link, sel_done, pos_mm, oh_done, pick_mm = (G.sem("se_" + n) for n in (
        "sr_in", "iota", "link", "sel", "pos_mm", "oh", "pick_mm"))
    PR = 2
    LEAD = 36
    PLACES, PICKS = 2, 6
    with ExitStack() as stack:
        M = Memory(nc, stack, "l1_")
        q, k = M.sb("q", [P, 2, 2, T], F32R), M.sb("k", [P, 2, 2, T], F32R)
        v = M.sb("v", [P, 2, NT, 2, 2 * HD])
        pt = M.sb("pt", [P, PR, 2, TB])
        mx, nm = M.sb("mx", [P, 2, BT, 3]), M.sb("nm", [P, 2, BT])
        mrow = M.sb("mrow", [P, 2, BT, KM], F32R)
        ob = M.sb("ob", [P, 2, TB])
        zero, dn = M.sb("zero", [P, KM]), M.sb("dn", [P, (NB - 1) * H0 * TB // P])
        sr, junk, same = M.sb("sr", [P, T]), M.sb("junk", [P, 2, T], BF16), M.sb("same", [P, 2, P])
        count, rank, sel = M.sb("count", [P, NT, 3]), M.sb("rank", [P, NT]), M.sb("sel", [P, NT], BF16)
        place, numi, ordi = M.sb("place", [P, NT]), M.sb("numi", [P, NT], I32), M.sb("ordi", [P, SEL], I32)
        order, before = M.sb("order", [P, SEL]), M.sb("before", [P, P])
        onehot, number = M.sb("onehot", [P, NT, SEL], BF16), M.sb("number", [P, NT, 2], BF16)
        onesb, parti = M.sb("onesb", [P, P], BF16), M.sb("parti", [P, NT], I32)
        picked = M.sb("picked", [P, NS, 2])
        block = stack.enter_context(nc.Block())

        def unit(i, u):
            par, b = (u // NB) % 2, u % NB
            pair = i * 2 + u // NB
            return par, b, pair * KEYS + keys_before[b], pair * CHUNKS + chunks_before[b], pair * NB + b

        @block.sync
        def _(sp):
            def load(pair, par, early):
                if not early:
                    sp.wait_ge(av_mm, (pair - 1) * KEYS)
                rows = bass.ds(pair * 2 * HD, 2 * HD)
                for dst, which, sem in ((q, 0, q_in[par]), (k, 1, k_in[par])):
                    for n, part in enumerate((0, which, 1 - which)):
                        sp.dma_start(raw(dst[n * HD:(n + 1) * HD, par, :, :]),
                                     S.qk[which, part, rows, :].rearrange("(h d) t -> d h t", h=2)).then_inc(sem, 16)
                load_values(pair, par)

            def load_values(pair, par):
                sp.dma_start(v[:, par, :, :, :].rearrange("p t h n -> p (t h n)"),
                             S.v[bass.ds(pair, 1), :, :, :].rearrange("a p t n -> (a p) (t n)")).then_inc(v_in[par], 16)

            def store(unit_no, pair, b):
                sp.wait_ge(o_sb, unit_no + 1)
                for h in range(2):
                    rows = slice(h * 2 * HD, h * 2 * HD + HD)
                    sp.dma_start(S.o[bass.ds(pair * 2 * HD + h * HD, HD), b * TB:(b + 1) * TB], ob[rows, b % 2, :]
                                 ).then_inc(o_out[b % 2], 16)
                    one = slice(h * 2 * HD + HD, h * 2 * HD + HD + 1)
                    sp.dma_start(S.den[b, bass.ds(pair * 2 + h, 1), :], ob[one, b % 2, :]
                                 ).then_inc(o_out[b % 2], 16)

            for b in range(NB):
                cols = slice(b * TB, (b + 1) * TB)
                for dst, which in ((q, 0), (k, 1)):
                    for n, part in enumerate((0, which, 1 - which)):
                        sp.dma_start(raw(dst[n * HD:(n + 1) * HD, 0, :, cols]),
                                     S.qk[which, part, 0:2 * HD, cols].rearrange("(h d) t -> d h t", h=2)
                                     ).then_inc(first_in[b], 16)
                if b == 0:
                    load_values(0, 0)
            load(1, 1, True)
            sp.dma_start(sr[:, :], S.score.partition_broadcast(P)).then_inc(sr_in, 16)
            load_routed_qkv(sp, G, I)

            def body(i, first, last):
                for u in range(2 * NB):
                    par, b, _, _, no = unit(i, u)
                    if last and u == 2 * NB - 1:
                        sp.wait_ge(o_out[0], 64 * PAIRS * NB // 2)
                        sp.wait_ge(o_out[1], 64 * (PAIRS * NB // 2 - 1))
                        sp.dma_start(dn[:, :], sums_of(S.den, 0, NB - 1)).then_inc(den_in, 16)
                        sp.wait_ge(rden, 1)
                        sp.dma_start(sums_of(S.rden, 0, NB - 1), dn[:, :]).then_inc(rden_out, 16)
                    store(no, i * 2 + par, b)
                    if b == NB - 1 and not last:
                        load(i * 2 + 2 + par, par, False)

            looped(sp, PAIRS // 2, body)
            for n in range(2):
                sp.wait_ge(o_out[n], 64 * PAIRS * NB // 2)
            sp.wait_ge(rden_out, 16)

        assert KEYS % 2 == 0

        def position(u, j):
            return (u // NB) * KEYS + keys_before[u % NB] + j

        def step_slot(b, j):
            return (keys_before[b] + j) % 2

        sequence, late = [], []
        for u in range(2 * NB):
            chunks = [(u, "chunk", h, m, c, k0, k1) for h in range(2)
                      for m, (qt, cuts) in enumerate(plans[u % NB].maxima) for c, (k0, k1) in enumerate(cuts)]
            sequence += chunks[:3] + late + chunks[3:]
            late = [(u, "rows", 0), (u, "rows", 1)]
        sequence += late
        SEQ = len(sequence)
        assert SEQ % 2 == 0
        chunks_upto = [sum(e[1] == "chunk" for e in sequence[:n + 1]) for n in range(SEQ)]
        rows_upto = [n + 1 - c for n, c in enumerate(chunks_upto)]

        def released(i, n):
            if n < 2:
                if isinstance(i, int) and i == 0:
                    return None
                i, n = i - 1, n + SEQ
            if sequence[n - 2][1] == "chunk":
                return a_red, i * 2 * CHUNKS + chunks_upto[n - 2]
            return mr_sb, i * 4 * NB + rows_upto[n - 2]

        def due(i, pos, last):
            def upto(p):
                even = LEAD + SEQ * (p + 1) // (2 * KEYS)
                return min(even, 14 + 8 * (p + 1)) if isinstance(i, int) and i == 0 else even
            for n in range(0 if pos < 0 else upto(pos - 1), upto(pos)):
                if n < SEQ:
                    yield i, n
                elif not last:
                    yield i + 1, n - SEQ

        @block.tensor
        def _(pe):
            def maximum(i, n):
                u, kind, h = sequence[n][:3]
                par, b, _, _, no = unit(i, u)
                bank = G.ps[6 + n % 2]
                before = released(i, n)
                if before:
                    wait(pe, *before)
                if kind == "chunk":
                    _, _, _, m, c, k0, k1 = sequence[n]
                    if h == 0 and m == 0 and c == 0:
                        if par == 0 and isinstance(i, int) and i == 0:
                            pe.wait_ge(first_in[b], 96)
                        elif b == 0:
                            pe.wait_ge(q_in[par], (i + par) * 48)
                            pe.wait_ge(k_in[par], (i + par) * 48)
                    qt = b * BT + m
                    out = bank[:, 0:(k1 - k0) * P]
                    diag, edge = k1 == qt + 1, qt >= plans[b].back and k0 == qt - plans[b].back
                    last = pe.matmul(out, q[0:K3, par, h, qt * P:(qt + 1) * P], k[0:K3, par, h, k0 * P:k1 * P],
                                     start=True, stop=not (diag or edge))
                    if diag:
                        last = pe.matmul(bank[:, (k1 - 1 - k0) * P:(k1 - k0) * P], G.identb[:, :], G.lower[:, :],
                                         start=False, stop=not edge)
                    if edge:
                        last = pe.matmul(bank[:, 0:P], G.identb[:, :], G.upper[:, :], start=False, stop=True)
                    last.then_inc(a_mm, 1)
                else:
                    pe.wait_ge(m_done, no + 1)
                    for m in range(BT):
                        last = pe.matmul(bank[0:KM, m * P:(m + 1) * P], mrow[:, h, m, :], G.identr[:, :],
                                         start=True, stop=True)
                    last.then_inc(mr_mm, 1)

            def scores(i, u, j):
                par, b, keys, _, no = unit(i, u)
                kt, qa, qz = plans[b].keys[j]
                n = keys + j
                wait(pe, p_done, n - 1)
                if j == 0:
                    pe.wait_ge(mr_sb, 2 * no + 2)
                width = (qz - qa + 1) * P
                slot = step_slot(b, j)
                diag, edge = kt == qa, kt + plans[b].back == qz
                for h in range(2):
                    bank = G.ps[2 * slot + h]
                    last = pe.matmul(bank[:, 0:width], k[0:KM, par, h, kt * P:(kt + 1) * P],
                                     q[0:KM, par, h, qa * P:(qz + 1) * P], start=True, stop=not (diag or edge))
                    if diag:
                        last = pe.matmul(bank[:, 0:P], G.identb[:, :], G.upper[:, :], start=False, stop=not edge)
                    if edge:
                        last = pe.matmul(bank[:, width - P:width], G.identb[:, :], G.lower[:, :], start=False, stop=True)
                last.then_inc(s_mm, 1)

            def places():
                pe.wait_ge(sel_done, 1)
                pe.wait_ge(a_red, PAIRS * CHUNKS)
                pe.wait_ge(mr_sb, PAIRS * NB * 2)
                pe.matmul(G.ps[6][:, 0:NT], G.strict[:, :], sel[:, :], start=True, stop=False, skip_group_check=True)
                for t in range(NT - 1):
                    last = pe.matmul(G.ps[6][:, t + 1:NT], onesb[:, :], sel[:, t:t + 1].to_broadcast([P, NT - 1 - t]),
                                     start=False, stop=t == NT - 2, skip_group_check=True)
                last.then_inc(pos_mm, 1)

            def picks():
                for m in range(NS):
                    for t in range(NT):
                        pe.wait_ge(oh_done, t + 1)
                        last = pe.matmul(G.ps[7][:, 2 * m:2 * m + 2], onehot[:, t, m * P:(m + 1) * P], number[:, t, :],
                                         start=t == 0, stop=t == NT - 1)
                last.then_inc(pick_mm, 1)

            def values(i, u, j):
                par, b, keys, _, no = unit(i, u)
                kt, qa, qz = plans[b].keys[j]
                n = keys + j
                pe.wait_ge(p_done, n + 1)
                if j == 0:
                    wait(pe, o_sb, no - 1)
                    if b == 0:
                        pe.wait_ge(v_in[par], (i + 1) * 16)
                bank = G.ps[4 + b % 2]
                for h in range(2):
                    last = pe.matmul(bank[h * 2 * HD:(h + 1) * 2 * HD, (qa - b * BT) * P:(qz + 1 - b * BT) * P],
                                     v[:, par, kt, h, :], pt[:, step_slot(b, j), h, 0:(qz - qa + 1) * P],
                                     start=j == 0, stop=j == len(plans[b].keys) - 1)
                last.then_inc(av_mm, 1)

            for at in due(0, -1, False):
                maximum(*at)
            scores(0, 0, 0)

            def body(i, first, last):
                for u in range(2 * NB):
                    b = u % NB
                    end = last and u == 2 * NB - 1
                    steps = len(plans[b].keys)
                    for j in range(steps):
                        for at in due(i, position(u, j), last):
                            maximum(*at)
                        if end and j == PLACES:
                            places()
                        if end and j == PICKS:
                            picks()
                        if j + 1 < steps:
                            scores(i, u, j + 1)
                        elif not end:
                            scores(i, u + 1, 0)
                        values(i, u, j)

            looped(pe, PAIRS // 2, body)

        @block.gpsimd
        def _(pool):
            pool.memset(before[:, :], 1.0).then_inc(iota_done, 1)
            pool.iota(numi[:, :], [[1, NT]], base=0, channel_multiplier=0).then_inc(iota_done, 1)
            pool.iota(parti[:, :], [[0, NT]], base=0, channel_multiplier=1).then_inc(iota_done, 1)
            pool.iota(ordi[:, :], [[1, SEL]], base=1, channel_multiplier=0).then_inc(iota_done, 1)
            pool.wait_ge(iota_done, 4)
            pool.affine_select(out=before[:, :], in_=before[:, :], compare_op=ALU.is_gt, fill=0.0, base=0,
                               pattern=[[-1, P]], channel_multiplier=1).then_inc(iota_done, 1)

        @block.scalar
        def _(act):
            act.wait_ge(kones, 1)

            def exponentials(i, u, j):
                par, b, keys, _, no = unit(i, u)
                kt, qa, qz = plans[b].keys[j]
                n = keys + j
                width = (qz - qa + 1) * P
                slot = step_slot(b, j)
                act.wait_ge(s_mm, n + 1)
                wait(act, av_mm, n - 1)
                act.activation(pt[:, step_slot(b, j), :, 0:width],
                               G.banks[:, 2 * slot:2 * slot + 2, 0:width], ACT.Exp, scale=scale).then_inc(p_done, 1)

            def rows(i, n):
                u, kind, h = sequence[n][:3]
                if kind == "rows":
                    par, b, _, _, no = unit(i, u)
                    act.wait_ge(mr_mm, 2 * no + h + 1)
                    act.activation(q[K3:KM, par, h, b * TB:(b + 1) * TB], G.ps[6 + n % 2][K3:KM, :], ACT.Copy
                                   ).then_inc(mr_sb, 1)

            for at in due(0, -1, False):
                rows(*at)

            def body(i, first, last):
                for u in range(2 * NB):
                    for j in range(len(plans[u % NB].keys)):
                        exponentials(i, u, j)
                        for at in due(i, position(u, j), last):
                            rows(*at)

            looped(act, PAIRS // 2, body)

        @block.vector
        def _(dve):
            chain = Chain(dve, link)
            chain.done(dve.memset(zero[:, :], 0.0))
            for h in range(2):
                for m in range(BT):
                    dve.tensor_copy(mrow[:, h, m, :], zero[:, :])
            for par in range(2):
                for h in range(2):
                    last = dve.tensor_copy(k[K3:KM, par, h, :].rearrange("p (a n) -> p a n", n=P),
                                           G.ones[K3:KM, :].unsqueeze(1).to_broadcast([2, NT, P]))
            chain.done(last)
            dve.memset(mx[:, :, :, :], NEG).then_inc(kones, 1)
            dve.wait_ge(kones, 1)

            def reduce(i, n):
                if sequence[n][1] == "rows":
                    return
                u, _, h, m, c, k0, k1 = sequence[n]
                dve.wait_ge(a_mm, i * 2 * CHUNKS + chunks_upto[n])
                dve.reduce_max(mx[:, h, m, c:c + 1], G.ps[6 + n % 2][:, 0:(k1 - k0) * P], axis=AX).then_inc(a_red, 1)
                if chunks_upto[n] == (u // NB) * CHUNKS + chunks_before[u % NB] + plans[u % NB].chunks:
                    negate(i, u)

            def negate(i, u):
                par, b, _, chunks, no = unit(i, u)
                pieces = max(len(c) for _, c in plans[b].maxima)
                dve.wait_ge(a_red, chunks + plans[b].chunks)
                dve.tensor_reduce(nm[:, :, :], mx[:, :, :, 0:pieces], AX, ALU.max, negate=True).then_inc(nm_done, 1)
                dve.wait_ge(nm_done, no + 1)
                wait(dve, mr_mm, 2 * no)
                dve.tensor_copy(mrow[:, :, :, K3:K3 + 1], nm[:, :, :].unsqueeze(3)).then_inc(mh_done, 1)
                dve.wait_ge(mh_done, no + 1)
                dve.tensor_tensor(mrow[:, :, :, K3 + 1:KM], nm[:, :, :].unsqueeze(3), raw(mrow[:, :, :, K3:K3 + 1]),
                                  ALU.subtract).then_inc(m_done, 1)

            def output(i, u):
                par, b, keys, _, no = unit(i, u)
                dve.wait_ge(av_mm, keys + len(plans[b].keys))
                if i_at_least(i, u, 2):
                    dve.wait_ge(o_out[b % 2], (i * 4 + (u // 2)) * 64)
                dve.tensor_copy(ob[:, b % 2, :], G.ps[4 + b % 2]).then_inc(o_sb, 1)

            def i_at_least(i, u, n):
                return not isinstance(i, int) or i * 2 * NB + u >= n

            tokens = Chain(dve, se_link)

            def ranks(t):
                own = G.score[:, t:t + 1]
                if t == 0:
                    dve.memset(count[:, :, :], 0.0)
                    dve.wait_ge(iota_done, 5)
                    dve.tensor_copy(number[:, :, 0], numi[:, :])
                    dve.tensor_copy(number[:, :, 1], parti[:, :])
                    dve.tensor_copy(onesb[:, :], G.ones[:, :])
                    tokens.done(dve.tensor_copy(order[:, :], ordi[:, :]))
                    dve.wait_ge(sr_in, 16)
                else:
                    dve.tensor_scalar(junk[:, t % 2, 0:t * P], sr[:, 0:t * P], own, 0.0, ALU.is_ge, ALU.add,
                                      accum_out=count[:, t, 0:1])
                dve.tensor_scalar(junk[:, t % 2, t * P:T], sr[:, t * P:T], own, 0.0, ALU.is_gt, ALU.add,
                                  accum_out=count[:, t, 1:2])
                tokens.done(dve.scalar_tensor_tensor(same[:, t % 2, :], sr[:, t * P:(t + 1) * P], own, before[:, :],
                                                     ALU.is_equal, ALU.mult, accum_out=count[:, t, 2:3]))
                if t == NT - 1:
                    tokens.done(dve.reduce_sum(rank[:, :], count[:, :, :], axis=AX))
                    dve.tensor_scalar(sel[:, :], rank[:, :], float(SEL), None, ALU.is_lt).then_inc(sel_done, 1)
                    dve.wait_ge(sel_done, 1)

            def onehots():
                dve.wait_ge(pos_mm, 1)
                tokens.done(dve.scalar_tensor_tensor(place[:, :], G.ps[6][:, 0:NT], 1.0, sel[:, :], ALU.add, ALU.mult))
                for t in range(NT):
                    dve.tensor_scalar(onehot[:, t, :], order[:, :], place[:, t:t + 1], None, ALU.is_equal
                                      ).then_inc(oh_done, 1)

            def chosen():
                dve.wait_ge(pick_mm, 1)
                tokens.done(dve.tensor_copy(picked[:, :, :], G.ps[7][:, 0:2 * NS].rearrange("p (m n) -> p m n", n=2)))
                tokens.done(dve.scalar_tensor_tensor(G.idx[:, :], picked[:, :, 0], float(P), picked[:, :, 1],
                                                     ALU.mult, ALU.add))

            for at in due(0, -1, False):
                reduce(*at)

            def body(i, first, last):
                for u in range(2 * NB):
                    for j in range(len(plans[u % NB].keys)):
                        for at in due(i, position(u, j), last):
                            reduce(*at)
                        if first and position(u, j) % 4 == 3 and position(u, j) // 4 < NT:
                            ranks(position(u, j) // 4)
                    if last and u == 2 * NB - 1:
                        onehots()
                        chosen()
                        dve.wait_ge(den_in, 16)
                        dve.reciprocal(dn[:, :], dn[:, :]).then_inc(rden, 1)
                    output(i, u)

            looped(dve, PAIRS // 2, body)


class Routed:

    def __init__(self, G, M):
        self.xs, self.sc = M.sb("xs", [P, NS, D]), M.sb("sc", [P, NS])
        self.cs = [M.sb("routed_cos", [P, NS, HDF]), M.sb("routed_sin", [P, NS, HDF])]
        self.hn, self.hT = M.sb("hn", [P, NS, D]), M.sb("hT", [P, NC, SEL])
        self.ln = M.sb("ln", [P, 2, NC])
        self.rows = M.sb("rows", [P, 2, D])
        self.ms, self.sd, self.rs = (M.sb(n, [P, NS]) for n in ("ms", "sd", "rs"))
        self.bias = M.sb("bias", [P, (NHQ + 2 * NHK) * HDF])
        self.sq_done, self.ms_done, self.sd_done, self.hn_done, self.hT_mm, self.hT_done, self.ln_in = (
            G.sem("ro_" + n) for n in ("sq", "ms", "sd", "hn", "hT_mm", "hT", "ln_in"))
        self.b_in = [G.sem(f"ro_b_in{k}") for k in range(3)]

    def load_bias(self, queue, I, k):
        FQ, FK = NHQ * HDF, NHK * HDF
        a, name, n = ((FQ, "bk", FK), (0, "bq", FQ), (FQ + FK, "bv", FK))[k]
        queue.dma_start(self.bias[:, a:a + n], I[name].partition_broadcast(P)).then_inc(self.b_in[k], 16)

    def normalise(self, dve, chain, x, k):
        dve.tensor_tensor(self.hn[:, :, :], x, x, ALU.mult).then_inc(self.sq_done, 1)
        dve.wait_ge(self.sq_done, k + 1)
        chain.done(dve.reduce_sum(self.ms[:, :], self.hn[:, :, :], axis=AX))
        dve.tensor_scalar(self.ms[:, :], self.ms[:, :], 1.0 / D, RMS_EPS, ALU.mult, ALU.add).then_inc(self.ms_done, 1)
        dve.wait_ge(self.sd_done, k + 1)
        chain.done(dve.reciprocal(self.rs[:, :], self.sd[:, :]))
        for m in range(NS):
            dve.tensor_scalar(self.hn[:, m, :], x[:, m, :], self.rs[:, m:m + 1], None, ALU.mult).then_inc(self.hn_done, 1)

    def root(self, act, k):
        act.wait_ge(self.ms_done, k + 1)
        act.activation(self.sd[:, :], self.ms[:, :], ACT.Sqrt).then_inc(self.sd_done, 1)

    def transposed(self, pe, G, k):
        for m in range(NS):
            pe.wait_ge(self.hn_done, k * NS + m + 1)
            for c in range(NC):
                last = pe.transpose(G.ps[6 + m][:, c * P:(c + 1) * P], self.hn[:, m, c * P:(c + 1) * P], G.ident[:, :])
            last.then_inc(self.hT_mm, 1)

    def weigh(self, dve, G, k):
        dve.wait_ge(self.ln_in, 32)
        for m in range(NS):
            dve.wait_ge(self.hT_mm, k * NS + m + 1)
            dve.tensor_tensor(self.hT[:, :, m * P:(m + 1) * P], G.ps[6 + m].rearrange("p (c n) -> p c n", c=NC),
                              self.ln[:, k, :].unsqueeze(2).to_broadcast([P, NC, P]), ALU.mult).then_inc(self.hT_done, 1)


def stage_output1(nc, G, I, S, R, out):
    ohi, olo, on, o_mm, res, zs_mm, link = (G.sem("o1_" + n) for n in ("hi", "lo", "on", "mm", "res", "zs_mm", "link"))
    den_in, rden, rden_out, z_done, gath = (G.sem("o1_" + n) for n in ("den_in", "rden", "rden_out", "z", "gath"))
    o_in, z_in, r_in, stored = ([G.sem(f"o1_{n}{k}") for k in range(2)] for n in ("o_in", "z_in", "r_in", "stored"))
    R.out_stored = stored
    with ExitStack() as stack:
        M = Memory(nc, stack, "o1_")
        wh, wl = M.sb("wh", [P, NC * D], F32R), M.sb("wl", [P, NC * D], F32R)
        weights = SplitWeights(G, M, "o1w_", [(wh[:, :], wl[:, :], I["w_out"].rearrange("(c p) n -> p c n", p=P))])
        dn = M.sb("dn", [P, H0 * TB // P])
        o = M.sb("o", [P, 2, NC, TB])
        z, zero = M.sb("z", [H0, 2, TB]), M.sb("zero", [P, TB])
        zh, zl = M.sb("zh", [P, 2, TB], F32R), M.sb("zl", [P, 2, TB], F32R)
        oh, ol = M.sb("oh", [P, 2, NC, TB], F32R), M.sb("ol", [P, 2, NC, TB], F32R)
        r = R.rows
        block = stack.enter_context(nc.Block())

        @block.sync
        def _(sp):
            sp.dma_start(dn[:, :], sums_of(S.den, NB - 1, NB)).then_inc(den_in, 16)
            for b in range(NB):
                cols = slice(b * TB, (b + 1) * TB)
                if b == NB - 1:
                    sp.wait_ge(rden, 1)
                    sp.dma_start(sums_of(S.rden, NB - 1, NB), dn[:, :]).then_inc(rden_out, 16)
                    sp.wait_ge(rden_out, 16)
                if b >= 2:
                    sp.wait_ge(z_done, b - 1)
                sp.dma_start(z[:, b % 2, :], S.rden[b, :, :]).then_inc(z_in[b % 2], 16)
                wait(sp, olo, (b - 1) * NC)
                sp.dma_start(o[:, b % 2, :, :], S.o[:, cols].rearrange("(g p) t -> p g t", p=P)).then_inc(o_in[b % 2], 16)
                if b == 0:
                    weights.load(sp)
                    sp.dma_start(R.ln[:, 0, :], I["ln1_w"]).then_inc(R.ln_in, 16)
                    sp.dma_start(R.ln[:, 1, :], I["ln2_w"]).then_inc(R.ln_in, 16)
            R.load_bias(sp, I, 0)

        @block.gpsimd
        def _(pool):
            def residual(t):
                if t >= 2:
                    pool.wait_ge(stored[t % 2], 16 * (t // 2))
                pool.dma_start(r[:, t % 2, :], S.r[t * P:(t + 1) * P, :]).then_inc(r_in[t % 2], 16)

            residual(0)
            residual(1)
            for m in range(NS):
                where = bass.IndirectOffsetOnAxis(G.idx[:, m:m + 1], 0)
                pool.indirect_dma_start(R.xs[:, m, :], None, S.xn, where).then_inc(gath, 16)
                for n, name in enumerate(("cos128", "sin128")):
                    pool.indirect_dma_start(R.cs[n][:, m, :], None, I[name], where).then_inc(gath, 16)
                pool.indirect_dma_start(R.sc[:, m:m + 1], None, S.score.unsqueeze(1), where).then_inc(gath, 16)
            for t in range(2, NT):
                residual(t)
            pool.wait_ge(gath, 16 * 4 * NS)

        @block.scalar
        def _(act):
            weights.high(act)

            def highs(b):
                for g in range(NC):
                    act.wait_ge(on, b * NC + g + 1)
                    wait(act, o_mm, (b - 1) * BT)
                    act.activation(oh[:, b % 2, g, :], o[:, b % 2, g, :], ACT.Copy).then_inc(ohi, 1)

            highs(0)
            for b in range(NB):
                if b + 1 < NB:
                    highs(b + 1)
                for k in range(BT):
                    t = b * BT + k
                    act.wait_ge(res, t + 1)
                    act.dma_start(out[t * P:(t + 1) * P, :], r[:, t % 2, :]).then_inc(stored[t % 2], 16)
                if b == NB - 2:
                    R.root(act, 0)

        @block.vector
        def _(dve):
            chain = Chain(dve, link)
            chain.done(dve.memset(zero[:, :], 0.0))
            for s in range(2):
                dve.tensor_copy(zh[:, s, :], zero[:, :])
                last = dve.tensor_copy(zl[:, s, :], zero[:, :])
            chain.done(last)

            def inverses(b):
                dve.wait_ge(z_in[b % 2], 16 * (b // 2 + 1))
                wait(dve, zs_mm, (b - 1) * NC)
                chain.done(dve.tensor_copy(zh[0:H0, b % 2, :], z[:, b % 2, :]))
                dve.tensor_tensor(zl[0:H0, b % 2, :], z[:, b % 2, :], raw(zh[0:H0, b % 2, :]),
                                  ALU.subtract).then_inc(z_done, 1)

            def normalised(b):
                dve.wait_ge(o_in[b % 2], 16 * (b // 2 + 1))
                for g in range(NC):
                    dve.wait_ge(zs_mm, b * NC + g + 1)
                    dve.tensor_tensor(o[:, b % 2, g, :], G.ps[2 + g], o[:, b % 2, g, :], ALU.mult).then_inc(on, 1)

            def lows(b):
                for g in range(NC):
                    dve.wait_ge(ohi, b * NC + g + 1)
                    dve.tensor_tensor(ol[:, b % 2, g, :], o[:, b % 2, g, :], raw(oh[:, b % 2, g, :]), ALU.subtract).then_inc(olo, 1)

            inverses(0)
            inverses(1)
            weights.low(dve)
            dve.wait_ge(den_in, 16)
            dve.reciprocal(dn[:, :], dn[:, :]).then_inc(rden, 1)
            normalised(0)
            lows(0)
            for b in range(NB):
                if b + 1 < NB:
                    normalised(b + 1)
                    lows(b + 1)
                if b + 2 < NB:
                    inverses(b + 2)
                if b == NB - 1:
                    dve.wait_ge(gath, 16 * 4 * NS)
                    R.normalise(dve, chain, R.xs[:, :, :], 0)
                for k in range(BT):
                    t = b * BT + k
                    dve.wait_ge(o_mm, t + 1)
                    dve.wait_ge(r_in[t % 2], 16 * (t // 2 + 1))
                    dve.tensor_tensor(r[:, t % 2, :], G.ps[t % 2], r[:, t % 2, :], ALU.add).then_inc(res, 1)
            R.weigh(dve, G, 0)

        @block.tensor
        def _(pe):
            def spread(b):
                pe.wait_ge(z_done, b + 1)
                for g in range(NC):
                    wait(pe, on, (b - 1) * NC + g + 1)
                    for m, part in enumerate((zh, zl)):
                        last = pe.matmul(G.ps[2 + g], G.headsel[:, g, :], part[:, b % 2, :], start=m == 0, stop=m == 1)
                    last.then_inc(zs_mm, 1)

            spread(0)
            spread(1)
            weights.ready(pe, 0)
            for t in range(NT):
                b, k = t // BT, t % BT
                pe.wait_ge(olo, (b + 1) * NC)
                wait(pe, res, t - 1)
                rows = slice(k * P, (k + 1) * P)
                mm3(pe, G.ps[t % 2], [((oh[:, b % 2, g, rows], ol[:, b % 2, g, rows]),
                                       (wh[:, g * D:(g + 1) * D], wl[:, g * D:(g + 1) * D])) for g in range(NC)]
                    ).then_inc(o_mm, 1)
                if k == 1 and b + 2 < NB:
                    spread(b + 2)
            R.transposed(pe, G, 0)


def routed_qkv(G):
    cut = lambda a, n: G.WA[:, NC * a:NC * (a + n)].rearrange("p (c n) -> p c n", c=NC)
    FQ, FK = NHQ * HDF, NHK * HDF
    return cut(0, FQ), cut(FQ, FK), cut(FQ + FK, FK)


def load_routed_qkv(queue, G, I):
    wq, wk, wv = routed_qkv(G)
    for w, name in ((wk, "wk"), (wq, "wq"), (wv, "wv")):
        queue.dma_start(w, I[name].rearrange("(c p) n -> p c n", p=P)).then_inc(G.wqkv_in, 16)


def stage_routed(nc, G, I, R, out):
    names = ("qk_mm", "qb", "t1", "y", "yt_mm", "yt", "v_mm", "v", "link")
    qk_mm, qb_done, t1_done, y_done, yt_mm, yt_done, v_mm, v_done, link = (G.sem("ro_" + n) for n in names)
    b_in, hT_done = R.b_in, R.hT_done
    names = ("s_mm", "nm", "p", "pn", "pt_mm", "pt", "av_mm", "o", "wo_mm", "x1", "gu_mm", "sig", "m", "dn_mm", "delta", "gate")
    s_mm, nm_done, p_done, pn_done, pt_mm, pt_done, av_mm, o_done, wo_mm, x1_done, gu_mm, sig_done, m_done, dn_mm, delta_done, gate_done = (
        G.sem("ro_" + n) for n in names)
    wo_in, wgu_in, wd_in, added = (G.sem("ro_" + n) for n in ("wo_in", "wgu_in", "wd_in", "added"))
    FQ, FK = NHQ * HDF, NHK * HDF
    QU, KU = FQ // BANK, FK // BANK
    HB = BANK // HDF
    NF = INTER // P
    scale = 1.0 / float(np.sqrt(HDF))
    with ExitStack() as stack:
        M = Memory(nc, stack, "ro_")
        WA = G.WA
        WB = M.sb("WB", [P, NHQ * D])
        wq, wk, wv = routed_qkv(G)
        wg = WA[:, 0:NC * INTER].rearrange("p (c n) -> p c n", c=NC)
        wu = WA[:, NC * INTER:2 * NC * INTER].rearrange("p (c n) -> p c n", c=NC)
        wb = WB[:, :].rearrange("p (h n) -> p h n", n=D)
        bias = R.bias
        oT = bias[:, :].rearrange("p (h n) -> p h n", h=NHQ)
        qT = M.sb("qT", [P, NHQ, SEL])
        kT, v = M.sb("kT", [P, NHK, SEL]), M.sb("v", [P, NS, FK])
        xs, cs, sc, hn, hT = R.xs, R.cs, R.sc, R.hn, R.hT
        x1 = M.sb("x1", [P, NS, D])
        qb, t1, y = (M.sb(n, [P, 2, BANK]) for n in ("qb", "t1", "y"))
        nm, ssum, rsum = (M.sb(n, [P, 3, NS]) for n in ("nm", "ssum", "rsum"))
        SB = (0, 1, 6)
        pr, pt = M.sb("pr", [P, 3, 3 * P]), M.sb("pt", [P, 2, 3 * P])
        sig = M.sb("sig", [P, 2, SEL])
        gate = M.sb("gate", [P, NS])
        block = stack.enter_context(nc.Block())

        units = [(wq, 0, u, m, qT) for u in range(QU) for m in range(NS)]
        units = [(wk, FQ, u, m, kT) for u in range(KU) for m in range(NS)] + units
        vunits = [(u, m) for u in range(KU) for m in range(NS)]

        @block.sync
        def _(sp):
            view = lambda name: I[name].rearrange("(c p) n -> p c n", p=P)
            R.load_bias(sp, I, 1)
            R.load_bias(sp, I, 2)
            sp.dma_start(wb, I["wo"].rearrange("(h p) n -> p h n", p=P)).then_inc(wo_in, 16)
            sp.wait_ge(qk_mm, len(units))
            sp.wait_ge(v_mm, len(vunits))
            sp.dma_start(wg, view("w_gate")).then_inc(wgu_in, 16)
            sp.dma_start(wu, view("w_up")).then_inc(wgu_in, 16)
            sp.wait_ge(wo_mm, NS)
            sp.dma_start(wb, I["w_down"].rearrange("(h p) n -> p h n", p=P)).then_inc(wd_in, 16)

        @block.gpsimd
        def _(pool):
            for n, (w, off, u, m, dst) in enumerate(units):
                pool.wait_ge(qb_done, n + 1)
                wait(pool, y_done, n - 1)
                pool.tensor_tensor(t1[:, n % 2, :].rearrange("p (h d) -> p h d", d=HDF),
                                   qb[:, n % 2, :].rearrange("p (h d) -> p h d", d=HDF),
                                   cs[0][:, m, :].unsqueeze(1).to_broadcast([P, HB, HDF]), ALU.mult).then_inc(t1_done, 1)
            for k in range(2):
                pool.wait_ge(R.out_stored[k], 16 * NT // 2)
            for m in range(NS):
                pool.wait_ge(delta_done, m + 1)
                where = bass.IndirectOffsetOnAxis(G.idx[:, m:m + 1], 0)
                pool.indirect_dma_start(out, where, hn[:, m, :], None, compute_op=ALU.add).then_inc(added, 16)
                pool.wait_ge(added, 16 * (m + 1))

        @block.tensor
        def _(pe):
            pe.wait_ge(hT_done, NS)

            def transposes(n):
                pe.wait_ge(y_done, n + 1)
                wait(pe, yt_done, n - 1)
                for j in range(HB):
                    last = pe.transpose(G.ps[2 + n % 2][:, j * P:(j + 1) * P], y[:, n % 2, j * P:(j + 1) * P], G.ident[:, :])
                last.then_inc(yt_mm, 1)

            def values(n):
                u, m = vunits[n]
                wait(pe, v_done, n - 1)
                mm32(pe, G.ps[4 + n % 2], [(hT[:, c, m * P:(m + 1) * P], wv[:, c, u * BANK:(u + 1) * BANK])
                                           for c in range(NC)]).then_inc(v_mm, 1)

            for n, (w, off, u, m, dst) in enumerate(units):
                if n == 0:
                    pe.wait_ge(G.wqkv_in, 48)
                wait(pe, qb_done, n - 1)
                mm32(pe, G.ps[n % 2], [(hT[:, c, m * P:(m + 1) * P], w[:, c, u * BANK:(u + 1) * BANK])
                                       for c in range(NC)]).then_inc(qk_mm, 1)
                if n >= 1:
                    transposes(n - 1)
            for n in range(len(vunits)):
                values(n)
                if n == 0:
                    transposes(len(units) - 1)

            def scores(h):
                wait(pe, p_done, NS * (h - 2))
                bank = G.ps[SB[h % 3]]
                for m in range(NS):
                    out = bank[:, m * P:(2 * m + 1) * P]
                    pe.matmul(out, qT[:, h, m * P:(m + 1) * P], kT[:, h * NHK // NHQ, 0:(m + 1) * P],
                              start=m == 0, stop=False, skip_group_check=True)
                    last = pe.matmul(bank[:, 2 * m * P:(2 * m + 1) * P], G.identb[:, :], G.lower[:, :],
                                     start=False, stop=True, skip_group_check=True)
                last.then_inc(s_mm, 1)

            def spread(h):
                pe.wait_ge(pn_done, h + 1)
                wait(pe, pt_done, h - 1)
                for j in range(3):
                    last = pe.transpose(G.ps[2 + h % 2][:, j * P:(j + 1) * P], pr[:, h % 3, j * P:(j + 1) * P], G.ident[:, :])
                last.then_inc(pt_mm, 1)

            def attend(h):
                pe.wait_ge(pt_done, h + 1)
                wait(pe, o_done, h - 1)
                cols = slice((h * NHK // NHQ) * HDF, (h * NHK // NHQ + 1) * HDF)
                out = G.ps[4 + h % 2]
                pe.matmul(out[:, 0:2 * P], v[:, 0, cols], pt[:, h % 2, 0:2 * P], start=True, stop=False, skip_group_check=True)
                pe.matmul(out[:, P:2 * P], v[:, 1, cols], pt[:, h % 2, 2 * P:3 * P], start=False, stop=True,
                          skip_group_check=True).then_inc(av_mm, 1)

            pe.wait_ge(yt_done, len(units))
            pe.wait_ge(qb_done, len(units))
            pe.wait_ge(v_done, len(vunits))
            scores(0)
            scores(1)
            for h in range(NHQ):
                if h + 2 < NHQ:
                    scores(h + 2)
                spread(h)
                if h >= 1:
                    attend(h - 1)
            attend(NHQ - 1)
            pe.wait_ge(wo_in, 16)
            pe.wait_ge(o_done, NHQ)
            for m in range(NS):
                mm32(pe, G.ps[m], [(oT[:, h, m * P:(m + 1) * P], wb[:, h, :]) for h in range(NHQ)]).then_inc(wo_mm, 1)
            R.transposed(pe, G, 1)
            pe.wait_ge(hT_done, 2 * NS)
            pe.wait_ge(wgu_in, 32)
            for f in range(NF):
                wait(pe, m_done, f - 1)
                for n, w in enumerate((wg, wu)):
                    last = mm32(pe, G.ps[2 + f % 2][:, n * SEL:(n + 1) * SEL],
                                [(w[:, c, f * P:(f + 1) * P], hT[:, c, :]) for c in range(NC)])
                last.then_inc(gu_mm, 1)
            pe.wait_ge(wd_in, 16)
            for m in range(NS):
                for f in range(NF):
                    pe.wait_ge(m_done, f + 1)
                    last = pe.matmul(G.ps[4 + m], qT[:, f, m * P:(m + 1) * P], wb[:, f, :], start=f == 0, stop=f == NF - 1)
                last.then_inc(dn_mm, 1)

        @block.scalar
        def _(act):
            def rotated(n):
                w, off, u, m, dst = units[n]
                act.wait_ge(yt_mm, n + 1)
                act.activation(dst[:, u * HB:(u + 1) * HB, m * P:(m + 1) * P],
                               G.ps[2 + n % 2].rearrange("p (h n) -> p h n", h=HB), ACT.Copy).then_inc(yt_done, 1)

            for n in range(len(units)):
                rotated(n)

            def probabilities(h):
                for m in range(NS):
                    act.wait_ge(nm_done, NS * h + m + 1)
                    if m == 0:
                        wait(act, pt_mm, h - 2)
                    act.activation(pr[:, h % 3, m * P:(2 * m + 1) * P], G.ps[SB[h % 3]][:, m * P:(2 * m + 1) * P], ACT.Exp,
                                   bias=nm[:, h % 3, m:m + 1], scale=scale,
                                   accum_out=ssum[:, h % 3, m:m + 1]).then_inc(p_done, 1)

            def spread(h):
                act.wait_ge(pt_mm, h + 1)
                wait(act, av_mm, h - 1)
                act.activation(pt[:, h % 2, :], G.ps[2 + h % 2][:, 0:3 * P], ACT.Copy).then_inc(pt_done, 1)

            def output(h):
                act.wait_ge(av_mm, h + 1)
                act.activation(oT[:, h, :], G.ps[4 + h % 2][:, 0:SEL], ACT.Copy).then_inc(o_done, 1)

            probabilities(0)
            probabilities(1)
            for h in range(NHQ):
                spread(h)
                if h + 2 < NHQ:
                    probabilities(h + 2)
                if h >= 1:
                    output(h - 1)
            output(NHQ - 1)
            R.root(act, 1)
            act.activation(gate[:, :], sc[:, :], ACT.Sigmoid).then_inc(gate_done, 1)
            for f in range(NF):
                act.wait_ge(gu_mm, f + 1)
                wait(act, m_done, f - 1)
                act.activation(sig[:, f % 2, :], G.ps[2 + f % 2][:, 0:SEL], ACT.Sigmoid).then_inc(sig_done, 1)

        @block.vector
        def _(dve):
            chain = Chain(dve, link)

            dve.wait_ge(b_in[0], 16)
            for n, (w, off, u, m, dst) in enumerate(units):
                dve.wait_ge(qk_mm, n + 1)
                wait(dve, t1_done, n - 1)
                if w is wq and u == 0 and m == 0:
                    dve.wait_ge(b_in[1], 16)
                a = off + u * BANK
                dve.tensor_tensor(qb[:, n % 2, :], G.ps[n % 2], bias[:, a:a + BANK], ALU.add).then_inc(qb_done, 1)
                dve.wait_ge(qb_done, n + 1)
                wait(dve, yt_mm, n - 1)
                q4 = qb[:, n % 2, :].rearrange("p (h d) -> p h d", d=HDF)
                y4 = y[:, n % 2, :].rearrange("p (h d) -> p h d", d=HDF)
                half = HDF // 2
                for k in range(2):
                    last = dve.tensor_tensor(y4[:, :, k * half:(k + 1) * half], q4[:, :, (1 - k) * half:(2 - k) * half],
                                             cs[1][:, m, k * half:(k + 1) * half].unsqueeze(1).to_broadcast([P, HB, half]),
                                             ALU.mult)
                chain.done(last)
                dve.wait_ge(t1_done, n + 1)
                dve.tensor_tensor(y[:, n % 2, :], y[:, n % 2, :], t1[:, n % 2, :], ALU.add).then_inc(y_done, 1)
            dve.wait_ge(b_in[2], 16)
            for n, (u, m) in enumerate(vunits):
                dve.wait_ge(v_mm, n + 1)
                dve.tensor_tensor(v[:, m, u * BANK:(u + 1) * BANK], G.ps[4 + n % 2],
                                  bias[:, FQ + FK + u * BANK:FQ + FK + (u + 1) * BANK], ALU.add).then_inc(v_done, 1)

            def maxima(h):
                dve.wait_ge(s_mm, h + 1)
                wait(dve, p_done, NS * (h - 2))
                for m in range(NS):
                    dve.tensor_reduce(nm[:, h % 3, m:m + 1], G.ps[SB[h % 3]][:, m * P:(2 * m + 1) * P], AX, ALU.max, negate=True
                                      ).then_inc(link, 1)
                    chain.n += 1
                dve.wait_ge(link, chain.n)
                dve.tensor_scalar(nm[:, h % 3, :], nm[:, h % 3, :], scale, None, ALU.mult).then_inc(nm_done, NS)

            def normalised(h):
                dve.wait_ge(p_done, NS * (h + 1))
                chain.done(dve.reciprocal(rsum[:, h % 3, :], ssum[:, h % 3, :]))
                for m in range(NS):
                    cols = slice(m * P, (2 * m + 1) * P)
                    last = dve.tensor_scalar(pr[:, h % 3, cols], pr[:, h % 3, cols], rsum[:, h % 3, m:m + 1], None, ALU.mult)
                last.then_inc(pn_done, 1)

            maxima(0)
            maxima(1)
            for h in range(NHQ):
                normalised(h)
                if h + 2 < NHQ:
                    maxima(h + 2)
            for m in range(NS):
                dve.wait_ge(wo_mm, m + 1)
                dve.tensor_tensor(x1[:, m, :], G.ps[m], xs[:, m, :], ALU.add).then_inc(x1_done, 1)
            dve.wait_ge(x1_done, NS)
            R.normalise(dve, chain, x1[:, :, :], 1)
            R.weigh(dve, G, 1)
            for f in range(NF):
                dve.wait_ge(sig_done, f + 1)
                chain.done(dve.tensor_tensor(sig[:, f % 2, :], G.ps[2 + f % 2][:, 0:SEL], sig[:, f % 2, :], ALU.mult))
                dve.tensor_tensor(qT[:, f, :], G.ps[2 + f % 2][:, SEL:2 * SEL], sig[:, f % 2, :], ALU.mult).then_inc(m_done, 1)
            dve.wait_ge(gate_done, 1)
            dve.tensor_tensor(x1[:, :, :], x1[:, :, :], xs[:, :, :], ALU.subtract).then_inc(x1_done, 1)
            dve.wait_ge(x1_done, NS + 1)
            for m in range(NS):
                dve.wait_ge(dn_mm, m + 1)
                chain.done(dve.tensor_tensor(hn[:, m, :], G.ps[4 + m], x1[:, m, :], ALU.add))
                dve.tensor_scalar(hn[:, m, :], hn[:, m, :], gate[:, m:m + 1], None, ALU.mult).then_inc(delta_done, 1)


class Scratch:

    def __init__(self, nc):
        def dram(name, shape, dt=F32):
            return nc.dram_tensor(name, shape, dt, kind="Internal").ap()
        self.wscr = dram("gates_by_expert", [EXPERTS, T])
        self.xn = dram("layer1_xn", [T, D])
        self.r = dram("layer1_residual", [T, D])
        self.qk = dram("layer1_qk", [2, 2, D, T])
        self.v = dram("layer1_v", [H0 // 2, P, NT, 4 * HD])
        self.o = dram("layer1_o", [D, T])
        self.den = dram("layer1_sums", [NB, H0, TB])
        self.score = dram("layer1_scores", [T])
        self.rden = dram("layer1_inverse_sums", [NB, H0, TB])


class Globals:
    def __init__(self, nc, stack):
        self.nc, self.stack = nc, stack
        M = Memory(nc, stack)
        self.banks = stack.enter_context(nc.psum_tensor("banks", [P, 8, BANK], F32))
        self.ps = [self.banks[:, i, :] for i in range(8)]
        self.ident, self.identb = M.sb("ident", [P, P]), M.sb("identb", [P, P], BF16)
        self.identr = M.sb("identr", [P, P], F32R)
        self.upper, self.lower = M.sb("upper", [P, P], BF16), M.sb("lower", [P, P], BF16)
        self.strict, self.headmask = M.sb("strict", [P, P], BF16), M.sb("headmask", [P, P])
        self.ones = M.sb("ones", [P, P])
        self.kvb, self.ksb = M.sb("kvb", [P, NC, P]), M.sb("ksb", [P, NC, H0])
        self.score = M.sb("score", [P, NT])
        self.idx = M.sb("idx", [P, NS], U32)
        self.headsel = M.sb("headsel", [P, NC, P], F32R)

        self.sems = []

    def sem(self, name):
        self.sems.append(self.nc.alloc_semaphore(name=name))
        return self.sems[-1]

    def give_back_semaphores(self):
        self.nc.clear_and_free_semaphores(self.sems)
        self.nc.all_engine_barrier()
        self.sems = []


def program(nc, I, out):
    S = Scratch(nc)
    with ExitStack() as stack:
        G = Globals(nc, stack)
        stage_constants(nc, G)
        with ExitStack() as features:
            M = Memory(nc, features)
            G.xTh, G.xTl = M.sb("xTh", [P, NC, T], F32R), M.sb("xTl", [P, NC, T], F32R)
            with ExitStack() as keys:
                MK = Memory(nc, keys)
                G.X = MK.sb("X", [P, NT, D])
                G.kvw = {n: (MK.sb(f"kv_w{n}h", [P, cols], F32R), MK.sb(f"kv_w{n}l", [P, cols], F32R))
                         for n, cols in (("g", NC * EXPERTS), ("k", NC * D), ("v", NC * D))}
                weights = SplitWeights(G, MK, "kv_", [
                    (G.kvw[n][0], G.kvw[n][1], I[src].rearrange("(c p) n -> p c n", p=P))
                    for n, src in (("g", "wgT"), ("k", "kT"), ("v", "vT"))])
                stage_normalize(nc, G, I["x"], weights)
                stage_kv(nc, G, I, S)
            with ExitStack() as tokens:
                MX = Memory(nc, tokens)
                G.acch, G.accl = MX.sb("acch", [P, T], F32R), MX.sb("accl", [P, T], F32R)
                G.wqh, G.wql = MX.sb("wqh", [P, NC * D], F32R), MX.sb("wql", [P, NC * D], F32R)
                stage_experts(nc, G, I, S)
                G.X = MX.sb("tokens", [P, NT, D])
                G.sw = {n: (MX.sb(n + "h", [P, NC * HID], F32R), MX.sb(n + "l", [P, NC * HID], F32R))
                        for n in ("sw1", "swg")}
                stage_attend0(nc, G, I)
                stage_output0(nc, G, I, S)
                G.give_back_semaphores()
            stage_qkv(nc, G, I, S)
        G.give_back_semaphores()
        with ExitStack() as routed:
            G.WA = Memory(nc, routed).sb("WA", [P, NC * (NHQ + 2 * NHK) * HDF])
            G.wqkv_in = G.sem("wqkv_in")
            stage_attend1(nc, G, I, S)
            R = Routed(G, Memory(nc, routed))
            stage_output1(nc, G, I, S, R, out)
            stage_routed(nc, G, I, R, out)


def halves(g):
    return np.stack([g, np.roll(g, g.shape[0] // 2)])


def rotary(width):
    inv = np.float32(1.0) / np.float32(10000.0) ** (np.arange(0, width, 2, dtype=np.float32) / np.float32(width))
    ang = np.arange(T, dtype=np.float32)[:, None] * inv[None, :].astype(np.float32)
    return np.concatenate([np.cos(ang), np.cos(ang)], 1), np.concatenate([-np.sin(ang), np.sin(ang)], 1)


def constants():
    c32, s32 = rotary(HD)
    c128, s128 = rotary(HDF)
    return {"cos32": c32, "sin32": s32, "cos128": c128, "sin128": s128}


LAYOUT = {
    "x": lambda a: a["L0_attn_hidden_states"][0],
    "qT": lambda a: a["L0_attn_q_w"].T,
    "kT": lambda a: a["L0_attn_k_w"].T,
    "vT": lambda a: a["L0_attn_v_w"].T,
    "oT": lambda a: a["L0_attn_o_w"].T,
    "q_b": lambda a: a["L0_attn_q_b"].reshape(NC, P).T,
    "k_b": lambda a: a["L0_attn_k_b"],
    "v_b": lambda a: a["L0_attn_v_b"],
    "o_b": lambda a: a["L0_attn_o_b"],
    "wgT": lambda a: a["L0_ffn_Wg"].T,
    "biases": lambda a: a["L0_ffn_biases"],
    "wdT": lambda a: a["L0_ffn_Wdown"].T,
    "wupT": lambda a: a["L0_ffn_Wup"].T,
    "sw1T": lambda a: a["L0_ffn_sw1"].T,
    "swgT": lambda a: a["L0_ffn_swg"].T,
    "sw2T": lambda a: a["L0_ffn_sw2"].T,
    "w_qkv": lambda a: a["L1_attn_w_qkv"],
    "w_out": lambda a: a["L1_attn_w_out"],
    "q_gamma": lambda a: halves(a["L1_attn_q_gamma"]),
    "k_gamma": lambda a: halves(a["L1_attn_k_gamma"]),
    "w_router": lambda a: a["L1_ffn_w_router"].reshape(NC, P).T,
    "ln1_w": lambda a: a["L1_ffn_ln1_w"].reshape(NC, P).T,
    "ln2_w": lambda a: a["L1_ffn_ln2_w"].reshape(NC, P).T,
    **{n: (lambda a, n=n: a["L1_ffn_" + n])
       for n in ("wq", "bq", "wk", "bk", "wv", "bv", "wo", "w_gate", "w_up", "w_down")},
    "ew": lambda a: np.concatenate([a["L0_ffn_rw1"].transpose(0, 2, 1), a["L0_ffn_rwg"].transpose(0, 2, 1),
                                    a["L0_ffn_rw2"].transpose(0, 2, 1)[:, :P], a["L0_ffn_rw2"].transpose(0, 2, 1)[:, P:]],
                                   axis=2),
}


def kernel(**inputs):
    import concourse.bacc as bacc
    from concourse.bass_utils import run_bass_kernel_spmd

    arrays = {name: np.ascontiguousarray(view(inputs)) for name, view in LAYOUT.items()}
    arrays.update(constants())
    nc = bacc.Bacc("TRN2", target_bir_lowering=False, num_devices=1)
    dram = {name: nc.dram_tensor(name + "_in", a.shape, mybir.dt.from_np(a.dtype), kind="ExternalInput").ap()
            for name, a in arrays.items()}
    out = nc.dram_tensor("out", [T, D], F32, kind="ExternalOutput").ap()
    program(nc, dram, out)
    nc.finalize()
    res = run_bass_kernel_spmd(nc, [{name + "_in": a for name, a in arrays.items()}], core_ids=[0])
    return res.results[0]["out"].reshape(1, T, D)
```
